# Optimizing a Trainium2 kernel written in Bass

```python
import numpy as np
import jax
import jax.numpy as jnp

def _softmax(x, axis=-1):
    return jax.nn.softmax(x, axis=axis)

def _gelu(x):
    return jax.nn.gelu(x, approximate=True)

def _silu(x):
    return jax.nn.silu(x)

def _sigmoid(x):
    return jax.nn.sigmoid(x)

def _layernorm(x, axis=-1, eps=1e-05):
    m = jnp.mean(x, axis=axis, keepdims=True)
    v = jnp.var(x, axis=axis, keepdims=True)
    return (x - m) / jnp.sqrt(v + eps)

def _scatter_add(tgt, idx, src, axis=0):
    return tgt.at[idx].add(src)

def _segment_sum(src, seg, n):
    return jax.ops.segment_sum(src, seg, n)
kernel_name = 'mk_lm_tower_d4_tok_ids1024_r4_81b16a'

def setup_inputs(seed: int=0):
    np.random.seed(seed)
    _w = jnp.asarray

    def _rec_inputs():
        import jax
        import jax.numpy as jnp
        _rk = jax.random.key(seed)
        x = jax.random.randint(jax.random.fold_in(_rk, 1), (16, 128), 0, 12564, jnp.int32)
        return x
    x = _rec_inputs()

    def _L0_tok_setup():
        import jax, jax.numpy as jnp
        import numpy as np
        VOCAB = 50257
        DIM = 256
        PADDING_IDX = 0
        key = jax.random.key(seed)
        k_w, k_ids = jax.random.split(key)
        weight = jax.random.normal(k_w, (VOCAB, DIM), dtype=jnp.float32)
        weight = weight.at[PADDING_IDX].set(0.0)
        input_ids = jax.random.randint(k_ids, (16, 512), 0, VOCAB, dtype=jnp.int64)
        return {'weight': weight, 'input_ids': input_ids}
    _L0_tok_all = _L0_tok_setup()
    _L0_tok_in = {k: v for k, v in _L0_tok_all.items() if k in ('weight',)}
    del _L0_tok_all

    def _L0_attn_setup():
        import jax, jax.numpy as jnp
        import numpy as np
        import math
        HEADS = 16
        LN_EPS = 1e-05

        def _layernorm(x, w, b):
            mu = jnp.mean(x, axis=-1, keepdims=True)
            var = jnp.mean((x - mu) ** 2, axis=-1, keepdims=True)
            return (x - mu) * jax.lax.rsqrt(var + LN_EPS) * w + b
        key = jax.random.key(seed)
        ks = jax.random.split(key, 8)
        b, t, e = (2, 512, 256)
        s = e // HEADS
        sc = 1.0 / math.sqrt(e)
        inp = {'x': jax.random.normal(ks[0], (b, t, e), dtype=jnp.float32), 'Wk': jax.random.normal(ks[1], (e, e), dtype=jnp.float32) * sc, 'Wq': jax.random.normal(ks[2], (e, e), dtype=jnp.float32) * sc, 'Wv': jax.random.normal(ks[3], (e, e), dtype=jnp.float32) * sc, 'Wo': jax.random.normal(ks[4], (e, e), dtype=jnp.float32) * sc, 'bo': jnp.zeros((e,), dtype=jnp.float32), 'kln_w': jnp.ones((s,), dtype=jnp.float32), 'kln_b': jnp.zeros((s,), dtype=jnp.float32), 'qln_w': jnp.ones((s,), dtype=jnp.float32), 'qln_b': jnp.zeros((s,), dtype=jnp.float32)}
        return inp
    _L0_attn_all = _L0_attn_setup()
    _L0_attn_in = {k: v for k, v in _L0_attn_all.items() if k in ('Wk', 'Wq', 'Wv', 'Wo', 'bo', 'kln_w', 'kln_b', 'qln_w', 'qln_b')}
    del _L0_attn_all

    def _L0_ffn_setup():
        import jax, jax.numpy as jnp
        import numpy as np
        ALPHA = 1.702
        LIMIT = 7.0
        K = 2
        key = jax.random.key(seed)
        ks = jax.random.split(key, 4)
        B, S, H, E, I = (1, 256, 256, 8, 256)
        return {'hidden_states': jax.random.normal(ks[0], (B, S, H), jnp.float32), 'router_weight': jax.random.normal(ks[1], (E, H), jnp.float32), 'router_bias': jnp.zeros((E,), jnp.float32), 'gate_up_proj': jax.random.normal(ks[2], (E, H, 2 * I), jnp.float32) * 0.02, 'gate_up_bias': jnp.zeros((E, 2 * I), jnp.float32), 'down_proj': jax.random.normal(ks[3], (E, I, H), jnp.float32) * 0.02, 'down_bias': jnp.zeros((E, H), jnp.float32)}
    _L0_ffn_all = _L0_ffn_setup()
    _L0_ffn_in = {k: v for k, v in _L0_ffn_all.items() if k in ('router_weight', 'router_bias', 'gate_up_proj', 'gate_up_bias', 'down_proj', 'down_bias')}
    del _L0_ffn_all

    def _L1_attn_setup():
        import jax, jax.numpy as jnp
        import numpy as np
        import math
        B, T, E, H, DQ, NB, MAXLEN = (4, 256, 256, 16, 64, 10, 256)
        NEG = -1000000000.0

        def _attn_forward(X, Wq, bq, Wk, Wv, Wproj, bproj, Wr, br, b_nd):
            b, t, e = X.shape
            maxlen = b_nd.shape[1]
            nb = b_nd.shape[0]
            h = H
            dq = Wq.shape[1] // h
            Q = (X @ Wq + bq).reshape(b, t, h, dq).transpose(0, 2, 1, 3)
            K = (X @ Wk).reshape(b, t, h, dq).transpose(0, 2, 1, 3)
            V = (X @ Wv).reshape(b, t, h, dq).transpose(0, 2, 1, 3)
            R = (X @ Wr + br).reshape(b, t, h, nb).transpose(0, 2, 1, 3)
            d = jnp.arange(t)[:, None] - jnp.arange(t)[None, :]
            valid = (d >= 0) & (d < maxlen)
            bias = jnp.where(valid, 0.0, NEG).astype(jnp.float32)
            D_ntT = jnp.where(valid[None, :, :], b_nd[:, jnp.clip(d, 0, maxlen - 1)], 0.0)
            extra = jnp.einsum('bhtn,ntp->bhtp', R, D_ntT)
            logits = jnp.einsum('bhtd,bhpd->bhtp', Q, K) / math.sqrt(dq) + bias + extra
            W = jax.nn.softmax(logits, axis=-1)
            A = jnp.einsum('bhtp,bhpd->bhtd', W, V)
            A = A.transpose(0, 2, 1, 3).reshape(b, t, h * dq)
            return A @ Wproj + bproj
        key = jax.random.key(seed)
        k = jax.random.split(key, 10)
        X = jax.random.normal(k[0], (B, T, E), jnp.float32)
        Wq = jax.random.normal(k[1], (E, H * DQ), jnp.float32) * (0.1 / math.sqrt(E))
        bq = jnp.zeros((H * DQ,), jnp.float32)
        Wk = jax.random.normal(k[2], (E, H * DQ), jnp.float32) * (0.2 / math.sqrt(E))
        Wv = jax.random.normal(k[3], (E, H * DQ), jnp.float32) * (1.0 / math.sqrt(E))
        Wproj = jax.random.normal(k[4], (H * DQ, E), jnp.float32) * (1.0 / math.sqrt(H * DQ))
        bproj = jnp.zeros((E,), jnp.float32)
        Wr = jax.random.normal(k[5], (E, H * NB), jnp.float32) * (0.1 / math.sqrt(E))
        br = jnp.zeros((H * NB,), jnp.float32)
        b_nd = jax.random.normal(k[6], (NB, MAXLEN), jnp.float32) * 0.2
        return dict(X=X, Wq=Wq, bq=bq, Wk=Wk, Wv=Wv, Wproj=Wproj, bproj=bproj, Wr=Wr, br=br, b_nd=b_nd)
    _L1_attn_all = _L1_attn_setup()
    _L1_attn_in = {k: v for k, v in _L1_attn_all.items() if k in ('Wq', 'bq', 'Wk', 'Wv', 'Wproj', 'bproj', 'Wr', 'br', 'b_nd')}
    del _L1_attn_all

    def _L1_ffn_setup():
        import jax, jax.numpy as jnp
        import numpy as np
        B, S, D, F, E = (4, 512, 256, 1024, 8)
        key = jax.random.key(seed)
        ks = jax.random.split(key, 7)
        s1 = 1.0 / np.sqrt(D)
        s2 = 1.0 / np.sqrt(F)
        x = jax.random.normal(ks[0], (B, S, D), dtype=jnp.float32)
        W1 = jax.random.uniform(ks[1], (E, D, F), jnp.float32, -s1, s1)
        b1 = jax.random.uniform(ks[2], (E, F), jnp.float32, -s1, s1)
        W2 = jax.random.uniform(ks[3], (E, F, D), jnp.float32, -s2, s2)
        b2 = jax.random.uniform(ks[4], (E, D), jnp.float32, -s2, s2)
        Wr = jax.random.uniform(ks[5], (D, E), jnp.float32, -s1, s1)
        br = jax.random.uniform(ks[6], (E,), jnp.float32, -s1, s1)
        return {'x': x, 'W1': W1, 'b1': b1, 'W2': W2, 'b2': b2, 'Wr': Wr, 'br': br}
    _L1_ffn_all = _L1_ffn_setup()
    _L1_ffn_in = {k: v for k, v in _L1_ffn_all.items() if k in ('W1', 'b1', 'W2', 'b2', 'Wr', 'br')}
    del _L1_ffn_all

    def _L2_attn_setup():
        import jax, jax.numpy as jnp
        import numpy as np
        D_MODEL = 256
        N_HEADS = 16
        HEAD_DIM = D_MODEL // N_HEADS
        EPS = 1e-05

        def _layernorm(x, g, b):
            mu = jnp.mean(x, axis=-1, keepdims=True)
            var = jnp.mean(jnp.square(x - mu), axis=-1, keepdims=True)
            return (x - mu) * jax.lax.rsqrt(var + EPS) * g + b

        def _gdn(x, Wq, Wk, Wv, Wb, Wg, Wo, bo):
            B, S, D = x.shape
            H, Dh = (N_HEADS, HEAD_DIM)
            q = (x @ Wq).reshape(B, S, H, Dh) * Dh ** (-0.5)
            k = (x @ Wk).reshape(B, S, H, Dh)
            k = k / (jnp.linalg.norm(k, axis=-1, keepdims=True) + 1e-06)
            v = (x @ Wv).reshape(B, S, H, Dh)
            beta = jax.nn.sigmoid(x @ Wb)
            g = jax.nn.sigmoid(x @ Wg)
            qt = jnp.moveaxis(q, 1, 0)
            kt = jnp.moveaxis(k, 1, 0)
            vt = jnp.moveaxis(v, 1, 0)
            bt = jnp.moveaxis(beta, 1, 0)
            gt = jnp.moveaxis(g, 1, 0)
            S0 = jnp.zeros((B, H, Dh, Dh), x.dtype)

            def step(Sst, inp):
                q_t, k_t, v_t, b_t, g_t = inp
                Sst = Sst * g_t[..., None, None]
                kS = jnp.einsum('bhk,bhkv->bhv', k_t, Sst)
                Sst = Sst + b_t[..., None, None] * jnp.einsum('bhk,bhv->bhkv', k_t, v_t - kS)
                o_t = jnp.einsum('bhk,bhkv->bhv', q_t, Sst)
                return (Sst, o_t)
            _, out = jax.lax.scan(step, S0, (qt, kt, vt, bt, gt))
            out = jnp.moveaxis(out, 0, 1).reshape(B, S, D)
            return out @ Wo + bo
        key = jax.random.key(seed)
        ks = jax.random.split(key, 16)
        B, S, D = (4, 512, D_MODEL)
        s = 0.02
        inp = {'x': jax.random.normal(ks[0], (B, S, D), dtype=jnp.float32), 'Wq': jax.random.normal(ks[1], (D, D), jnp.float32) * s, 'Wk': jax.random.normal(ks[2], (D, D), jnp.float32) * s, 'Wv': jax.random.normal(ks[3], (D, D), jnp.float32) * s, 'Wb': jax.random.normal(ks[4], (D, N_HEADS), jnp.float32) * s, 'Wg': jax.random.normal(ks[5], (D, N_HEADS), jnp.float32) * s, 'Wo': jax.random.normal(ks[6], (D, D), jnp.float32) * s, 'bo': jnp.zeros((D,), jnp.float32), 'ln1_g': jnp.ones((D,), jnp.float32), 'ln1_b': jnp.zeros((D,), jnp.float32), 'ln2_g': jnp.ones((D,), jnp.float32), 'ln2_b': jnp.zeros((D,), jnp.float32), 'w1': jax.random.normal(ks[7], (D, 4 * D), jnp.float32) * s, 'b1': jnp.zeros((4 * D,), jnp.float32), 'w2': jax.random.normal(ks[8], (4 * D, D), jnp.float32) * s, 'b2': jnp.zeros((D,), jnp.float32)}
        return inp
    _L2_attn_all = _L2_attn_setup()
    _L2_attn_in = {k: v for k, v in _L2_attn_all.items() if k in ('Wq', 'Wk', 'Wv', 'Wb', 'Wg', 'Wo', 'bo', 'ln1_g', 'ln1_b', 'ln2_g', 'ln2_b', 'w1', 'b1', 'w2', 'b2')}
    del _L2_attn_all

    def _L2_ffn_setup():
        import jax, jax.numpy as jnp
        import numpy as np
        BLOCK = 16
        _GRID = jnp.array([0.0, 0.5, 1.0, 1.5, 2.0, 3.0, 4.0, 6.0], dtype=jnp.float32)
        _MID = jnp.array([0.25, 0.75, 1.25, 1.75, 2.5, 3.5, 5.0], dtype=jnp.float32)

        def fp4_quant_dequant(x):
            shape = x.shape
            xb = x.reshape(shape[:-1] + (shape[-1] // BLOCK, BLOCK))
            scale = jnp.max(jnp.abs(xb), axis=-1, keepdims=True) / 6.0
            scale = jnp.maximum(scale, jnp.float32(1e-12))
            xn = xb / scale
            idx = jnp.searchsorted(_MID, jnp.abs(xn))
            q = _GRID[idx] * jnp.sign(xn) * scale
            return q.reshape(shape)

        def fp4_linear(x, w):
            xq = fp4_quant_dequant(x)
            wq = fp4_quant_dequant(w)
            return jnp.einsum('bsk,nk->bsn', xq, wq)
        key = jax.random.key(seed)
        k1, k2, k3, k4 = jax.random.split(key, 4)
        H, I = (256, 704)
        x = jax.random.normal(k1, (4, 1024, H), dtype=jnp.float32)
        w_gate = jax.random.normal(k2, (I, H), dtype=jnp.float32) * 0.02
        w_up = jax.random.normal(k3, (I, H), dtype=jnp.float32) * 0.02
        w_down = jax.random.normal(k4, (H, I), dtype=jnp.float32) * 0.02
        return {'x': x, 'w_gate': w_gate, 'w_up': w_up, 'w_down': w_down}
    _L2_ffn_all = _L2_ffn_setup()
    _L2_ffn_in = {k: v for k, v in _L2_ffn_all.items() if k in ('w_gate', 'w_up', 'w_down')}
    del _L2_ffn_all

    def _L3_attn_setup():
        import jax, jax.numpy as jnp
        import numpy as np
        import math
        B, L, HID, H = (4, 256, 256, 16)
        DH = HID // H
        MAX_SEQ = 256
        key = jax.random.key(seed)
        ks = jax.random.split(key, 6)
        s = 0.02
        return {'x': jax.random.normal(ks[0], (B, L, HID), jnp.float32), 'Wq': jax.random.normal(ks[1], (HID, HID), jnp.float32) * s, 'bq': jnp.zeros((HID,), jnp.float32), 'Wk': jax.random.normal(ks[2], (HID, HID), jnp.float32) * s, 'bk': jnp.zeros((HID,), jnp.float32), 'Wv': jax.random.normal(ks[3], (HID, HID), jnp.float32) * s, 'bv': jnp.zeros((HID,), jnp.float32), 'Wo': jax.random.normal(ks[4], (HID, HID), jnp.float32) * s, 'bo': jnp.zeros((HID,), jnp.float32), 'rel_emb': jax.random.normal(ks[5], (2 * MAX_SEQ - 1, DH), jnp.float32) * s}
    _L3_attn_all = _L3_attn_setup()
    _L3_attn_in = {k: v for k, v in _L3_attn_all.items() if k in ('Wq', 'bq', 'Wk', 'bk', 'Wv', 'bv', 'Wo', 'bo', 'rel_emb')}
    del _L3_attn_all

    def _L3_ffn_setup():
        import jax, jax.numpy as jnp
        import numpy as np
        E = 16
        K = 4
        G = 4
        TG = 2
        NS = 2
        H = 256
        I = 352
        SCALE = 1.0

        def _gate(x2d, gate_w, gate_bias):
            T = x2d.shape[0]
            logits = x2d.astype(jnp.float32) @ gate_w.astype(jnp.float32).T
            scores = jax.nn.sigmoid(logits)
            sfc = scores + gate_bias[None, :]
            grp = sfc.reshape(T, G, E // G)
            top2, _ = jax.lax.top_k(grp, 2)
            group_scores = top2.sum(-1)
            _, gidx = jax.lax.top_k(group_scores, TG)
            gmask = jnp.zeros((T, G), sfc.dtype).at[jnp.arange(T)[:, None], gidx].set(1.0)
            smask = jnp.repeat(gmask, E // G, axis=1) > 0
            tmp = jnp.where(smask, sfc, 0.0)
            _, topk_idx = jax.lax.top_k(tmp, K)
            topk_w = jnp.take_along_axis(scores, topk_idx, axis=1)
            topk_w = topk_w / (topk_w.sum(-1, keepdims=True) + 1e-20)
            return (topk_idx, topk_w * SCALE)
        key = jax.random.key(seed)
        ks = jax.random.split(key, 8)
        bound = 1.0 / np.sqrt(H)
        return {'hidden_states': jax.random.normal(ks[0], (1, 256, H), jnp.float32), 'gate_w': jax.random.uniform(ks[1], (E, H), jnp.float32, -bound, bound), 'gate_bias': jnp.zeros((E,), jnp.float32), 'gate_proj': jax.random.normal(ks[2], (E, I, H), jnp.float32) * 0.02, 'up_proj': jax.random.normal(ks[3], (E, I, H), jnp.float32) * 0.02, 'down_proj': jax.random.normal(ks[4], (E, H, I), jnp.float32) * 0.02, 'shared_gate_w': jax.random.normal(ks[5], (I * NS, H), jnp.float32) * 0.02, 'shared_up_w': jax.random.normal(ks[6], (I * NS, H), jnp.float32) * 0.02, 'shared_down_w': jax.random.normal(ks[7], (H, I * NS), jnp.float32) * 0.02}
    _L3_ffn_all = _L3_ffn_setup()
    _L3_ffn_in = {k: v for k, v in _L3_ffn_all.items() if k in ('gate_w', 'gate_bias', 'gate_proj', 'up_proj', 'down_proj', 'shared_gate_w', 'shared_up_w', 'shared_down_w')}
    del _L3_ffn_all
    return {'x': x, 'L0_tok_weight': _L0_tok_in['weight'], 'L0_attn_Wk': _L0_attn_in['Wk'], 'L0_attn_Wq': _L0_attn_in['Wq'], 'L0_attn_Wv': _L0_attn_in['Wv'], 'L0_attn_Wo': _L0_attn_in['Wo'], 'L0_attn_bo': _L0_attn_in['bo'], 'L0_attn_kln_w': _L0_attn_in['kln_w'], 'L0_attn_kln_b': _L0_attn_in['kln_b'], 'L0_attn_qln_w': _L0_attn_in['qln_w'], 'L0_attn_qln_b': _L0_attn_in['qln_b'], 'L0_ffn_router_weight': _L0_ffn_in['router_weight'], 'L0_ffn_router_bias': _L0_ffn_in['router_bias'], 'L0_ffn_gate_up_proj': _L0_ffn_in['gate_up_proj'], 'L0_ffn_gate_up_bias': _L0_ffn_in['gate_up_bias'], 'L0_ffn_down_proj': _L0_ffn_in['down_proj'], 'L0_ffn_down_bias': _L0_ffn_in['down_bias'], 'L1_attn_Wq': _L1_attn_in['Wq'], 'L1_attn_bq': _L1_attn_in['bq'], 'L1_attn_Wk': _L1_attn_in['Wk'], 'L1_attn_Wv': _L1_attn_in['Wv'], 'L1_attn_Wproj': _L1_attn_in['Wproj'], 'L1_attn_bproj': _L1_attn_in['bproj'], 'L1_attn_Wr': _L1_attn_in['Wr'], 'L1_attn_br': _L1_attn_in['br'], 'L1_attn_b_nd': _L1_attn_in['b_nd'], 'L1_ffn_W1': _L1_ffn_in['W1'], 'L1_ffn_b1': _L1_ffn_in['b1'], 'L1_ffn_W2': _L1_ffn_in['W2'], 'L1_ffn_b2': _L1_ffn_in['b2'], 'L1_ffn_Wr': _L1_ffn_in['Wr'], 'L1_ffn_br': _L1_ffn_in['br'], 'L2_attn_Wq': _L2_attn_in['Wq'], 'L2_attn_Wk': _L2_attn_in['Wk'], 'L2_attn_Wv': _L2_attn_in['Wv'], 'L2_attn_Wb': _L2_attn_in['Wb'], 'L2_attn_Wg': _L2_attn_in['Wg'], 'L2_attn_Wo': _L2_attn_in['Wo'], 'L2_attn_bo': _L2_attn_in['bo'], 'L2_attn_ln1_g': _L2_attn_in['ln1_g'], 'L2_attn_ln1_b': _L2_attn_in['ln1_b'], 'L2_attn_ln2_g': _L2_attn_in['ln2_g'], 'L2_attn_ln2_b': _L2_attn_in['ln2_b'], 'L2_attn_w1': _L2_attn_in['w1'], 'L2_attn_b1': _L2_attn_in['b1'], 'L2_attn_w2': _L2_attn_in['w2'], 'L2_attn_b2': _L2_attn_in['b2'], 'L2_ffn_w_gate': _L2_ffn_in['w_gate'], 'L2_ffn_w_up': _L2_ffn_in['w_up'], 'L2_ffn_w_down': _L2_ffn_in['w_down'], 'L3_attn_Wq': _L3_attn_in['Wq'], 'L3_attn_bq': _L3_attn_in['bq'], 'L3_attn_Wk': _L3_attn_in['Wk'], 'L3_attn_bk': _L3_attn_in['bk'], 'L3_attn_Wv': _L3_attn_in['Wv'], 'L3_attn_bv': _L3_attn_in['bv'], 'L3_attn_Wo': _L3_attn_in['Wo'], 'L3_attn_bo': _L3_attn_in['bo'], 'L3_attn_rel_emb': _L3_attn_in['rel_emb'], 'L3_ffn_gate_w': _L3_ffn_in['gate_w'], 'L3_ffn_gate_bias': _L3_ffn_in['gate_bias'], 'L3_ffn_gate_proj': _L3_ffn_in['gate_proj'], 'L3_ffn_up_proj': _L3_ffn_in['up_proj'], 'L3_ffn_down_proj': _L3_ffn_in['down_proj'], 'L3_ffn_shared_gate_w': _L3_ffn_in['shared_gate_w'], 'L3_ffn_shared_up_w': _L3_ffn_in['shared_up_w'], 'L3_ffn_shared_down_w': _L3_ffn_in['shared_down_w']}

def reference(x, L0_tok_weight, L0_attn_Wk, L0_attn_Wq, L0_attn_Wv, L0_attn_Wo, L0_attn_bo, L0_attn_kln_w, L0_attn_kln_b, L0_attn_qln_w, L0_attn_qln_b, L0_ffn_router_weight, L0_ffn_router_bias, L0_ffn_gate_up_proj, L0_ffn_gate_up_bias, L0_ffn_down_proj, L0_ffn_down_bias, L1_attn_Wq, L1_attn_bq, L1_attn_Wk, L1_attn_Wv, L1_attn_Wproj, L1_attn_bproj, L1_attn_Wr, L1_attn_br, L1_attn_b_nd, L1_ffn_W1, L1_ffn_b1, L1_ffn_W2, L1_ffn_b2, L1_ffn_Wr, L1_ffn_br, L2_attn_Wq, L2_attn_Wk, L2_attn_Wv, L2_attn_Wb, L2_attn_Wg, L2_attn_Wo, L2_attn_bo, L2_attn_ln1_g, L2_attn_ln1_b, L2_attn_ln2_g, L2_attn_ln2_b, L2_attn_w1, L2_attn_b1, L2_attn_w2, L2_attn_b2, L2_ffn_w_gate, L2_ffn_w_up, L2_ffn_w_down, L3_attn_Wq, L3_attn_bq, L3_attn_Wk, L3_attn_bk, L3_attn_Wv, L3_attn_bv, L3_attn_Wo, L3_attn_bo, L3_attn_rel_emb, L3_ffn_gate_w, L3_ffn_gate_bias, L3_ffn_gate_proj, L3_ffn_up_proj, L3_ffn_down_proj, L3_ffn_shared_gate_w, L3_ffn_shared_up_w, L3_ffn_shared_down_w):
    import jax
    import jax.numpy as jnp

    def _L0_tok_ref(weight, input_ids):
        import jax, jax.numpy as jnp
        import numpy as np
        VOCAB = 50257
        DIM = 256
        PADDING_IDX = 0
        return jnp.take(weight, input_ids, axis=0)

    def _L0_attn_ref(x, Wk, Wq, Wv, Wo, bo, kln_w, kln_b, qln_w, qln_b):
        import jax, jax.numpy as jnp
        import numpy as np
        import math
        HEADS = 16
        LN_EPS = 1e-05

        def _layernorm(x, w, b):
            mu = jnp.mean(x, axis=-1, keepdims=True)
            var = jnp.mean((x - mu) ** 2, axis=-1, keepdims=True)
            return (x - mu) * jax.lax.rsqrt(var + LN_EPS) * w + b
        b, t, e = x.shape
        h = HEADS
        s = e // h
        scale = 1.0 / math.sqrt(s)
        k = (x @ Wk).reshape(b, t, h, s)
        q = (x @ Wq).reshape(b, t, h, s)
        v = (x @ Wv).reshape(b, t, h, s)
        k = _layernorm(k, kln_w, kln_b)
        q = _layernorm(q, qln_w, qln_b)
        dot = jnp.einsum('bqhs,bkhs->bhqk', q, k) * scale
        causal = jnp.tril(jnp.ones((t, t), dtype=bool))
        dot = jnp.where(causal, dot, -jnp.inf)
        attn = jax.nn.softmax(dot, axis=-1)
        out = jnp.einsum('bhqk,bkhs->bqhs', attn, v).reshape(b, t, e)
        return out @ Wo + bo

    def _L0_ffn_ref(hidden_states, router_weight, router_bias, gate_up_proj, gate_up_bias, down_proj, down_bias):
        import jax, jax.numpy as jnp
        import numpy as np
        ALPHA = 1.702
        LIMIT = 7.0
        K = 2
        B, S, H = hidden_states.shape
        E = router_weight.shape[0]
        I = down_proj.shape[1]
        T = B * S
        flat = hidden_states.reshape(T, H)
        logits = flat @ router_weight.T + router_bias
        scores = jax.nn.softmax(logits, axis=-1)
        topk_vals, topk_idx = jax.lax.top_k(scores, K)
        w = jnp.zeros((T, E), scores.dtype).at[jnp.arange(T)[:, None], topk_idx].set(topk_vals)
        gu = jnp.einsum('th,ehf->tef', flat, gate_up_proj) + gate_up_bias
        gate = jnp.minimum(gu[..., :I], LIMIT)
        up = jnp.clip(gu[..., I:], -LIMIT, LIMIT)
        glu = gate * jax.nn.sigmoid(gate * ALPHA)
        act = (up + 1.0) * glu
        down = jnp.einsum('tei,eih->teh', act, down_proj) + down_bias
        out = jnp.einsum('teh,te->th', down, w)
        return out.reshape(B, S, H)

    def _L1_attn_ref(X, Wq, bq, Wk, Wv, Wproj, bproj, Wr, br, b_nd):
        import jax, jax.numpy as jnp
        import numpy as np
        import math
        B, T, E, H, DQ, NB, MAXLEN = (4, 256, 256, 16, 64, 10, 256)
        NEG = -1000000000.0

        def _attn_forward(X, Wq, bq, Wk, Wv, Wproj, bproj, Wr, br, b_nd):
            b, t, e = X.shape
            maxlen = b_nd.shape[1]
            nb = b_nd.shape[0]
            h = H
            dq = Wq.shape[1] // h
            Q = (X @ Wq + bq).reshape(b, t, h, dq).transpose(0, 2, 1, 3)
            K = (X @ Wk).reshape(b, t, h, dq).transpose(0, 2, 1, 3)
            V = (X @ Wv).reshape(b, t, h, dq).transpose(0, 2, 1, 3)
            R = (X @ Wr + br).reshape(b, t, h, nb).transpose(0, 2, 1, 3)
            d = jnp.arange(t)[:, None] - jnp.arange(t)[None, :]
            valid = (d >= 0) & (d < maxlen)
            bias = jnp.where(valid, 0.0, NEG).astype(jnp.float32)
            D_ntT = jnp.where(valid[None, :, :], b_nd[:, jnp.clip(d, 0, maxlen - 1)], 0.0)
            extra = jnp.einsum('bhtn,ntp->bhtp', R, D_ntT)
            logits = jnp.einsum('bhtd,bhpd->bhtp', Q, K) / math.sqrt(dq) + bias + extra
            W = jax.nn.softmax(logits, axis=-1)
            A = jnp.einsum('bhtp,bhpd->bhtd', W, V)
            A = A.transpose(0, 2, 1, 3).reshape(b, t, h * dq)
            return A @ Wproj + bproj
        return _attn_forward(X, Wq, bq, Wk, Wv, Wproj, bproj, Wr, br, b_nd)

    def _L1_ffn_ref(x, W1, b1, W2, b2, Wr, br):
        import jax, jax.numpy as jnp
        import numpy as np
        B, S, D, F, E = (4, 512, 256, 1024, 8)
        b, s, d = x.shape
        e = Wr.shape[1]
        logits = x @ Wr + br
        idx = jnp.argmax(logits, axis=-1)
        probs = jax.nn.softmax(logits, axis=-1)
        gates = jnp.take_along_axis(probs, idx[..., None], axis=-1)[..., 0]
        xf = x.reshape(-1, d)
        idxf = idx.reshape(-1)
        gf = gates.reshape(-1)
        out = jnp.zeros_like(xf)
        for ei in range(e):
            h = jax.nn.gelu(xf @ W1[ei] + b1[ei], approximate=False)
            y = h @ W2[ei] + b2[ei]
            mask = (idxf == ei).astype(xf.dtype)
            out = out + y * (gf * mask)[:, None]
        return out.reshape(b, s, d)

    def _L2_attn_ref(x, Wq, Wk, Wv, Wb, Wg, Wo, bo, ln1_g, ln1_b, ln2_g, ln2_b, w1, b1, w2, b2):
        import jax, jax.numpy as jnp
        import numpy as np
        D_MODEL = 256
        N_HEADS = 16
        HEAD_DIM = D_MODEL // N_HEADS
        EPS = 1e-05

        def _layernorm(x, g, b):
            mu = jnp.mean(x, axis=-1, keepdims=True)
            var = jnp.mean(jnp.square(x - mu), axis=-1, keepdims=True)
            return (x - mu) * jax.lax.rsqrt(var + EPS) * g + b

        def _gdn(x, Wq, Wk, Wv, Wb, Wg, Wo, bo):
            B, S, D = x.shape
            H, Dh = (N_HEADS, HEAD_DIM)
            q = (x @ Wq).reshape(B, S, H, Dh) * Dh ** (-0.5)
            k = (x @ Wk).reshape(B, S, H, Dh)
            k = k / (jnp.linalg.norm(k, axis=-1, keepdims=True) + 1e-06)
            v = (x @ Wv).reshape(B, S, H, Dh)
            beta = jax.nn.sigmoid(x @ Wb)
            g = jax.nn.sigmoid(x @ Wg)
            qt = jnp.moveaxis(q, 1, 0)
            kt = jnp.moveaxis(k, 1, 0)
            vt = jnp.moveaxis(v, 1, 0)
            bt = jnp.moveaxis(beta, 1, 0)
            gt = jnp.moveaxis(g, 1, 0)
            S0 = jnp.zeros((B, H, Dh, Dh), x.dtype)

            def step(Sst, inp):
                q_t, k_t, v_t, b_t, g_t = inp
                Sst = Sst * g_t[..., None, None]
                kS = jnp.einsum('bhk,bhkv->bhv', k_t, Sst)
                Sst = Sst + b_t[..., None, None] * jnp.einsum('bhk,bhv->bhkv', k_t, v_t - kS)
                o_t = jnp.einsum('bhk,bhkv->bhv', q_t, Sst)
                return (Sst, o_t)
            _, out = jax.lax.scan(step, S0, (qt, kt, vt, bt, gt))
            out = jnp.moveaxis(out, 0, 1).reshape(B, S, D)
            return out @ Wo + bo
        x = x + _gdn(_layernorm(x, ln1_g, ln1_b), Wq, Wk, Wv, Wb, Wg, Wo, bo)
        h = _layernorm(x, ln2_g, ln2_b)
        h = jax.nn.gelu(h @ w1 + b1, approximate=False) @ w2 + b2
        return x + h

    def _L2_ffn_ref(x, w_gate, w_up, w_down):
        import jax, jax.numpy as jnp
        import numpy as np
        BLOCK = 16
        _GRID = jnp.array([0.0, 0.5, 1.0, 1.5, 2.0, 3.0, 4.0, 6.0], dtype=jnp.float32)
        _MID = jnp.array([0.25, 0.75, 1.25, 1.75, 2.5, 3.5, 5.0], dtype=jnp.float32)

        def fp4_quant_dequant(x):
            shape = x.shape
            xb = x.reshape(shape[:-1] + (shape[-1] // BLOCK, BLOCK))
            scale = jnp.max(jnp.abs(xb), axis=-1, keepdims=True) / 6.0
            scale = jnp.maximum(scale, jnp.float32(1e-12))
            xn = xb / scale
            idx = jnp.searchsorted(_MID, jnp.abs(xn))
            q = _GRID[idx] * jnp.sign(xn) * scale
            return q.reshape(shape)

        def fp4_linear(x, w):
            xq = fp4_quant_dequant(x)
            wq = fp4_quant_dequant(w)
            return jnp.einsum('bsk,nk->bsn', xq, wq)
        gate = fp4_linear(x, w_gate)
        y = fp4_linear(x, w_up)
        h = jax.nn.silu(gate) * y
        return fp4_linear(h, w_down)

    def _L3_attn_ref(x, Wq, bq, Wk, bk, Wv, bv, Wo, bo, rel_emb):
        import jax, jax.numpy as jnp
        import numpy as np
        import math
        B, L, HID, H = (4, 256, 256, 16)
        DH = HID // H
        MAX_SEQ = 256
        b, l, hid = x.shape
        dh = rel_emb.shape[1]
        h = hid // dh
        max_seq = (rel_emb.shape[0] + 1) // 2

        def heads(y):
            return y.reshape(b, l, h, dh).transpose(0, 2, 1, 3)
        q = heads(x @ Wq + bq)
        k = heads(x @ Wk + bk)
        v = heads(x @ Wv + bv)
        scores = jnp.einsum('bhid,bhjd->bhij', q, k) / math.sqrt(dh)
        scores = jnp.clip(scores, -100000.0, 100000.0)
        pos_idx = jnp.arange(l)[:, None] - jnp.arange(l)[None, :] + max_seq - 1
        rel_pos = rel_emb[pos_idx]
        scores = scores + jnp.einsum('bhid,ijd->bhij', q, rel_pos)
        attn = jax.nn.softmax(scores, axis=-1)
        attn = attn / (attn.sum(axis=-1, keepdims=True) + 1e-08)
        ctx = jnp.einsum('bhij,bhjd->bhid', attn, v)
        ctx = ctx.transpose(0, 2, 1, 3).reshape(b, l, hid)
        return ctx @ Wo + bo

    def _L3_ffn_ref(hidden_states, gate_w, gate_bias, gate_proj, up_proj, down_proj, shared_gate_w, shared_up_w, shared_down_w):
        import jax, jax.numpy as jnp
        import numpy as np
        E = 16
        K = 4
        G = 4
        TG = 2
        NS = 2
        H = 256
        I = 352
        SCALE = 1.0

        def _gate(x2d, gate_w, gate_bias):
            T = x2d.shape[0]
            logits = x2d.astype(jnp.float32) @ gate_w.astype(jnp.float32).T
            scores = jax.nn.sigmoid(logits)
            sfc = scores + gate_bias[None, :]
            grp = sfc.reshape(T, G, E // G)
            top2, _ = jax.lax.top_k(grp, 2)
            group_scores = top2.sum(-1)
            _, gidx = jax.lax.top_k(group_scores, TG)
            gmask = jnp.zeros((T, G), sfc.dtype).at[jnp.arange(T)[:, None], gidx].set(1.0)
            smask = jnp.repeat(gmask, E // G, axis=1) > 0
            tmp = jnp.where(smask, sfc, 0.0)
            _, topk_idx = jax.lax.top_k(tmp, K)
            topk_w = jnp.take_along_axis(scores, topk_idx, axis=1)
            topk_w = topk_w / (topk_w.sum(-1, keepdims=True) + 1e-20)
            return (topk_idx, topk_w * SCALE)
        orig_shape = hidden_states.shape
        x = hidden_states.reshape(-1, H)
        topk_idx, topk_w = _gate(x, gate_w, gate_bias)
        combine_w = (jax.nn.one_hot(topk_idx, E, dtype=x.dtype) * topk_w[..., None]).sum(1)
        g = jnp.einsum('th,eih->tei', x, gate_proj)
        u = jnp.einsum('th,eih->tei', x, up_proj)
        act = jax.nn.silu(g) * u
        y = jnp.einsum('tei,ehi,te->th', act, down_proj, combine_w)
        sg = x @ shared_gate_w.T
        su = x @ shared_up_w.T
        y = y + jax.nn.silu(sg) * su @ shared_down_w.T
        return y.reshape(orig_shape)
    h = _L0_tok_ref(L0_tok_weight, x)
    h = h + _L0_attn_ref(_layernorm(h, axis=-1), L0_attn_Wk, L0_attn_Wq, L0_attn_Wv, L0_attn_Wo, L0_attn_bo, L0_attn_kln_w, L0_attn_kln_b, L0_attn_qln_w, L0_attn_qln_b)
    h = h + _L0_ffn_ref(_layernorm(h, axis=-1), L0_ffn_router_weight, L0_ffn_router_bias, L0_ffn_gate_up_proj, L0_ffn_gate_up_bias, L0_ffn_down_proj, L0_ffn_down_bias)
    h = h + _L1_attn_ref(_layernorm(h, axis=-1), L1_attn_Wq, L1_attn_bq, L1_attn_Wk, L1_attn_Wv, L1_attn_Wproj, L1_attn_bproj, L1_attn_Wr, L1_attn_br, L1_attn_b_nd)
    h = h + _L1_ffn_ref(_layernorm(h, axis=-1), L1_ffn_W1, L1_ffn_b1, L1_ffn_W2, L1_ffn_b2, L1_ffn_Wr, L1_ffn_br)
    h = h + _L2_attn_ref(_layernorm(h, axis=-1), L2_attn_Wq, L2_attn_Wk, L2_attn_Wv, L2_attn_Wb, L2_attn_Wg, L2_attn_Wo, L2_attn_bo, L2_attn_ln1_g, L2_attn_ln1_b, L2_attn_ln2_g, L2_attn_ln2_b, L2_attn_w1, L2_attn_b1, L2_attn_w2, L2_attn_b2)
    h = h + _L2_ffn_ref(_layernorm(h, axis=-1), L2_ffn_w_gate, L2_ffn_w_up, L2_ffn_w_down)
    h = h + _L3_attn_ref(_layernorm(h, axis=-1), L3_attn_Wq, L3_attn_bq, L3_attn_Wk, L3_attn_bk, L3_attn_Wv, L3_attn_bv, L3_attn_Wo, L3_attn_bo, L3_attn_rel_emb)
    h = h + _L3_ffn_ref(_layernorm(h, axis=-1), L3_ffn_gate_w, L3_ffn_gate_bias, L3_ffn_gate_proj, L3_ffn_up_proj, L3_ffn_down_proj, L3_ffn_shared_gate_w, L3_ffn_shared_up_w, L3_ffn_shared_down_w)
    return h

_drawn_inputs = setup_inputs


def setup_inputs(seed=0):
    import zlib

    import numpy as np

    out = dict(_drawn_inputs(seed))
    spreads = {'L0_attn_bo': (0.0, 0.1),
     'L0_attn_kln_w': (1.0, 0.2),
     'L0_attn_kln_b': (0.0, 0.8),
     'L0_attn_qln_w': (1.0, 0.2),
     'L0_attn_qln_b': (0.0, 0.494),
     'L0_ffn_router_bias': (0.0, 0.8),
     'L0_ffn_gate_up_bias': (0.0, 0.428),
     'L0_ffn_down_bias': (0.0, 0.1),
     'L1_attn_bq': (0.0, 0.8),
     'L1_attn_bproj': (0.0, 0.1),
     'L1_attn_br': (0.0, 0.8),
     'L2_attn_bo': (0.0, 0.1),
     'L2_attn_ln1_g': (1.0, 0.6),
     'L2_attn_ln1_b': (0.0, 0.8),
     'L2_attn_ln2_g': (1.0, 0.6),
     'L2_attn_ln2_b': (0.0, 0.8),
     'L2_attn_b1': (0.0, 0.486),
     'L2_attn_b2': (0.0, 0.1),
     'L3_attn_bq': (0.0, 0.8),
     'L3_attn_bk': (0.0, 0.8),
     'L3_attn_bv': (0.0, 0.582),
     'L3_attn_bo': (0.0, 0.1),
     'L3_ffn_gate_bias': (0.0, 0.8)}
    factors = {'L1_attn_Wq': 8.0,
     'L1_attn_Wk': 8.0,
     'L1_attn_Wr': 5.773,
     'L1_attn_b_nd': 4.251,
     'L1_ffn_b1': 8.0,
     'L1_ffn_b2': 8.0,
     'L1_ffn_br': 4.611,
     'L2_attn_Wq': 8.0,
     'L2_attn_Wk': 8.0,
     'L2_attn_Wv': 8.0,
     'L2_attn_Wb': 8.0,
     'L2_attn_Wg': 8.0,
     'L2_attn_Wo': 8.0,
     'L2_ffn_w_gate': 4.291,
     'L2_ffn_w_up': 4.251,
     'L2_ffn_w_down': 4.225,
     'L3_attn_Wq': 8.0,
     'L3_attn_Wk': 8.0,
     'L3_attn_Wv': 3.994,
     'L3_attn_Wo': 2.697,
     'L3_attn_rel_emb': 8.0,
     'L3_ffn_gate_w': 8.0,
     'L3_ffn_gate_proj': 8.0,
     'L3_ffn_up_proj': 8.0,
     'L3_ffn_down_proj': 8.0,
     'L3_ffn_shared_gate_w': 4.295,
     'L3_ffn_shared_up_w': 4.238,
     'L3_ffn_shared_down_w': 4.251}
    for name, (base, spread) in spreads.items():
        noise = np.random.default_rng([zlib.crc32(name.encode()), seed]).standard_normal(out[name].shape)
        drawn = base * np.exp(spread * noise) if base else spread * noise
        out[name] = jnp.asarray(drawn.astype(out[name].dtype))
    for name, factor in factors.items():
        out[name] = (out[name] * factor).astype(out[name].dtype)
    return out
```

```python
from contextlib import ExitStack

import numpy as np

import concourse.bass as bass
import concourse.mybir as mybir

F32 = mybir.dt.float32
BF16 = mybir.dt.bfloat16
I32 = mybir.dt.int32
U32 = mybir.dt.uint32
ALU = mybir.AluOpType
ACT = mybir.ActivationFunctionType
AX = mybir.AxisListType

P = 128
B = 16
D = 256
DC = D // P
LN_EPS = 1e-5


class Core:

    def __init__(self, nc, ins, out):
        self.nc, self.ins, self.out = nc, ins, out


class Chain:

    def __init__(self, eng, sem):
        self.eng, self.sem, self.base, self.count = eng, sem, 0, 0

    def begin(self, base):
        self.base, self.count = base, 0

    def step(self, ins):
        ins.then_inc(self.sem, 1)
        self.count += 1
        self.eng.wait_ge(self.sem, self.base + self.count)


def stage(nc, name):
    ctx = ExitStack()
    sems = []

    def clear():
        if sems:
            nc.clear_and_free_semaphores(sems)
            nc.all_engine_barrier()

    ctx.callback(clear)

    def sb(label, shape, dt=F32):
        return ctx.enter_context(nc.sbuf_tensor(f"{name}_{label}", shape, dt))

    def ps(label, shape, dt=F32):
        return ctx.enter_context(nc.psum_tensor(f"{name}_{label}", shape, dt))

    def sem(label):
        sems.append(nc.alloc_semaphore(name=f"{name}_{label}"))
        return sems[-1]

    return ctx, sb, ps, sem


def embed(core):
    nc, ins = core.nc, core.ins
    ctx, sb, ps, sem = stage(nc, "embed")
    with ctx:
        ids = sb("ids", [P, B], I32)
        causal = sb("causal", [P, 4 * P])
        ids_in, rows_in, consts_in = sem("ids_in"), sem("rows_in"), sem("consts_in")
        block = ctx.enter_context(nc.Block())

        @block.sync
        def _(sp):
            sp.dma_start(ids[:, :], ins["token_ids"]).then_inc(ids_in, 16)
            sp.dma_start(core.ident[:, :], ins["ident"]).then_inc(consts_in, 16)
            sp.dma_start(causal[:, :], ins["causal"]).then_inc(consts_in, 16)
            sp.wait_ge(consts_in, 32)

        @block.gpsimd
        def _(pool):
            pool.memset(core.minus_half[:, :], -0.5)
            pool.memset(core.ones[:, :], 1.0)
            pool.wait_ge(ids_in, 16)
            for b in range(B):
                pool.indirect_dma_start(
                    out=core.h[:, b, :], out_offset=None, in_=ins["L0_tok_weight"],
                    in_offset=bass.IndirectOffsetOnAxis(ap=ids[:, b:b + 1].bitcast(U32), axis=0),
                ).then_inc(rows_in, 16)
            pool.wait_ge(rows_in, 16 * B)

        @block.vector
        def _(dve):
            dve.wait_ge(consts_in, 32)
            dve.tensor_copy(core.ident_bf[:, :], core.ident[:, :])
            dve.tensor_copy(core.causal[:, :], causal[:, :])


class TokenNorm:

    def __init__(self, core, sb, sem, src):
        self.core, self.src = core, src
        self.parts = sb("ln_parts", [P, B, 6])
        self.mv = sb("ln_mv", [P, B, 2])
        self.rstd = sb("ln_rstd", [P, B, 1])
        self.parts_done, self.var_done, self.rstd_done = sem("ln_parts"), sem("ln_var"), sem("ln_rstd")

    def stats(self, dve):
        for b in range(B):
            dve.bn_stats(self.parts[:, b, :], self.src[:, b, :]).then_inc(self.parts_done, 1)
        dve.wait_ge(self.parts_done, B)
        for b in range(B):
            dve.bn_aggr(self.mv[:, b, :], self.parts[:, b, :]).then_inc(self.var_done, 1)
        dve.wait_ge(self.var_done, B)
        dve.tensor_scalar(self.rstd[:, :, 0], self.mv[:, :, 1], LN_EPS, None, ALU.add).then_inc(self.var_done, 1)

    def rsqrt(self, pool):
        pool.wait_ge(self.var_done, B + 1)
        pool.tensor_tensor(self.rstd[:, :, 0], self.rstd[:, :, 0], self.core.minus_half[:, 0:B], ALU.pow).then_inc(self.rstd_done, 1)

    def normalise(self, dve, out, b):
        return dve.tensor_scalar(out, self.src[:, b, :], self.mv[:, b, 0:1], self.rstd[:, b, :], ALU.subtract, ALU.mult)


def bias_row(core, sb, name):
    return sb(name, [1, D])


def attention(core, kind, q_name=None):
    nc, ins, h = core.nc, core.ins, core.h
    H = 16
    dh = 64 if kind == "nd" else 16
    strip = 64 if kind == "nd" else 32
    per = P // strip
    QC = H // per
    F = H * dh
    FC = F // P
    pre = {"headnorm": "L0_attn_", "nd": "L1_attn_", "rel": "L3_attn_"}[kind]
    nm = {"headnorm": "a0", "nd": "a1", "rel": "a3"}[kind]
    skewed = kind != "headnorm"
    GW = {"headnorm": 0, "nd": P, "rel": 2 * P}[kind]
    PITCH = 2 * P

    def place(head):
        c, s = head // per, head % per
        if kind == "nd":
            return 2 * (c // 4) + s, c % 4, s * strip, c
        return s, c, s * strip, c

    heads_of = {}
    for head in range(H):
        beta, slot, _, _ = place(head)
        heads_of[beta, slot] = head

    if kind == "headnorm":
        jobs = [("x", "act"), ("qk", "dve"), ("q", "act"), ("k", "act"), ("v", "act")]
    elif kind == "nd":
        jobs = [("x", "act"), ("q0", "act"), ("q1", "act"), ("k0", "act"), ("k1", "act"), ("r", "act")]
        jobs += [(f"g{i}", "act") for i in range(H * GW // 512)]
        jobs += [("v0", "act"), ("v1", "act")]
    else:
        jobs = [("x", "act"), ("q", "act"), ("k", "act")] + [(f"g{i}", "act") for i in range(H * GW // 512)]
        jobs += [("v", "act")]
    NF = len(jobs)
    names = [j[0] for j in jobs]
    NA = sum(j[1] == "act" for j in jobs)

    bank_of = {name: j % 2 for j, name in enumerate(names)}

    per_o = 512 // (dh + 1)
    o_jobs = [list(range(a, min(a + per_o, H))) for a in range(0, H, per_o)]
    t_jobs = [list(range(a, min(a + 4, FC))) for a in range(0, FC, 4)]
    NBK = len(o_jobs) + len(t_jobs) + 1

    ctx, sb, ps, sem = stage(nc, nm)
    with ctx:
        norm = TokenNorm(core, sb, sem, h)
        xn = sb("xn", [P, D])
        xT = sb("xT", [P, DC, P])
        qT = sb("qT", [P, QC, P])
        kT = sb("kT", [P, QC, P])
        va = sb("va", [P, H, dh + 1])
        prob = sb("prob", [P, 4, 512])
        probT = sb("probT", [P, 4, 512])
        top = sb("top", [P, H])
        inv = sb("inv", [P, H])
        o = sb("o", [P, F])
        oT = sb("oT", [P, FC, P])
        wo = sb("wo", [P, FC, D])
        bo = sb("bo", [1, D])
        wv = sb("wv", [P, DC, F])
        psS = ps("scores", [P, 4, 512])
        psF = ps("front", [P, 2, 512])
        psB = ps("back", [P, 2, 512])
        weights_in = sem("weights_in")
        xn_ready = sem("xn_ready")
        front_full = sem("front_full")
        front_act = sem("front_act")
        back_full = sem("back_full")
        back_read = sem("back_read")
        scores_full = sem("scores_full")
        shifted = sem("shifted")
        expd = sem("expd")
        probT_full = sem("probT_full")
        probT_read = sem("probT_read")
        ones_set = sem("ones_set")
        dve_chain = sem("dve_chain")
        n_weights = 3
        if kind == "headnorm":
            wqk = sb("wqk", [P, DC, 2 * F])
            qk = sb("qk", [P, 2 * H, 2 * dh])
            hsum = sb("hsum", [P, 2 * H])
            hvar = sb("hvar", [P, 2 * H])
            cen = sb("cen", [P, 2 * H, dh])
            sq = sb("sq", [P, 2 * H, dh])
            hw = sb("hw", [P, 2, dh])
            hb = sb("hb", [P, 2, dh])
            hv_done, hr_done, qk_ready = sem("hv_done"), sem("hr_done"), sem("qk_ready")
            n_weights += 5
        else:
            wq = sb("wq", [P, DC, QC * P])
            wk = sb("wk", [P, DC, QC * P])
            bq = sb("bq", [P, QC])
            g_sb = sb("g", [P, H, GW])
            e_sb = sb("e", [P, 4, 4, P])
            skew = nc.dram_tensor(f"{nm}_skew", [P, H, PITCH], F32, kind="Internal").ap()
            skew_read = bass.AP(skew.tensor, P - 1, [[H * PITCH - 1, P], [PITCH, H], [1, P]])
            g_out, e_in, g_set = sem("g_out"), sem("e_in"), sem("g_set")
            g_ready = front_act
            n_weights += 3
            dist = sb("dist", [P, GW])
            n_weights += 1
            if kind == "nd":
                wr = sb("wr", [P, DC, 4 * P])
                br = sb("br", [P, 4])
                rT = sb("rT", [P, 4, P])
                n_weights += 3
            else:
                bk = sb("bk", [P, QC])
                bv = sb("bv", [1, F])
                n_weights += 2

        block = ctx.enter_context(nc.Block())

        @block.sync
        def _(sp):
            n = 0

            def load(dst, src):
                nonlocal n
                n += 1
                sp.dma_start(dst, src).then_inc(weights_in, 16)

            def chunks(src):
                return src.rearrange("(c p) n -> p c n", p=P)

            load(wv[:, :, :], chunks(ins[pre + "Wv"]))
            load(wo[:, :, :], chunks(ins[pre + ("Wproj" if kind == "nd" else "Wo")]))
            load(bo[:, :], ins[pre + ("bproj" if kind == "nd" else "bo")].unsqueeze(0))
            if kind == "headnorm":
                load(wqk[:, :, 0:F], chunks(ins[pre + "Wq"]))
                load(wqk[:, :, F:2 * F], chunks(ins[pre + "Wk"]))
                for i, side in enumerate("qk"):
                    load(hw[:, i, :], ins[f"{pre}{side}ln_w"].partition_broadcast(P))
                load(hb[:, 0, :], ins[f"{pre}qln_b"].partition_broadcast(P))
                load(hb[:, 1, :], ins[f"{pre}kln_b"].partition_broadcast(P))
                n_load = n
            else:
                load(wq[:, :, :], chunks(ins[pre + "Wq_strips"]))
                load(wk[:, :, :], chunks(ins[pre + "Wk_strips"]))
                load(bq[:, :], ins[pre + "bq_strips"])
                load(dist[:, :], ins[pre + "dist"])
                if kind == "nd":
                    load(wr[:, :, :], chunks(ins[pre + "Wr_strips"]))
                    load(br[:, :], ins[pre + "br_strips"])
                    load(skew[:, :, P:PITCH], ins["masked"].partition_broadcast(P))
                else:
                    load(bk[:, :], ins[pre + "bk_strips"])
                    load(bv[:, :], ins[pre + "bv"].unsqueeze(0))
            core.n_weights = n
            if skewed:
                last_g = names.index(f"g{H * GW // 512 - 1}")
                def skewing(t):
                    if isinstance(t, int):
                        tables, loads = t * NA + last_g + 1, 16 * t + 16
                    else:
                        tables, loads = sp.to_reg(t * NA + last_g + 1), sp.to_reg(16 * t + 16)
                        previous, read = sp.to_reg(4 * t), sp.to_reg(16 * t)
                        sp.wait_ge(e_in, read)
                        sp.wait_ge(shifted, previous)
                    sp.wait_ge(front_act, tables)
                    sp.dma_start(skew[:, :, 0:GW], g_sb[:, :, :]).then_inc(g_out, 16)
                    sp.wait_ge(g_out, loads)
                    if isinstance(t, int):
                        sp.wait_ge(weights_in, 16 * n)
                    sp.dma_start(e_sb[:, :, :, :].rearrange("p b a k -> p (b a) k"), skew_read).then_inc(e_in, 16)

                skewing(0)
                with sp.Fori(1, B) as t:
                    skewing(t)
                sp.wait_ge(e_in, 16 * B)

        n_weights = core.n_weights

        @block.gpsimd
        def _(pool):
            pool.memset(va[:, :, dh:dh + 1], 1.0).then_inc(ones_set, 1)
            if kind == "headnorm":
                pool.memset(qk[:, :, :], 0.0).then_inc(ones_set, 1)
            norm.rsqrt(pool)
            if kind == "headnorm":
                def head_rsqrt(t):
                    pool.wait_ge(hv_done, t + 1)
                    pool.tensor_tensor(hvar[:, :], hvar[:, :], core.minus_half[:, 0:2 * H], ALU.pow).then_inc(hr_done, 1)

                with pool.Fori(0, B) as t:
                    head_rsqrt(t)

        @block.scalar
        def _(act):
            na = 0

            def front_read(t, name, out, **kw):
                j = names.index(name)
                act.wait_ge(front_full, t * NF + j + 1)
                return psF[:, bank_of[name], :]

            def done(i):
                i.then_inc(front_act, 1)

            def copy_x(t):
                src = front_read(t, "x", None)
                done(act.copy(xT[:, :, :], src[:, 0:D].rearrange("p (c t) -> p c t", c=DC)))

            def copy_v(t):
                if kind == "nd":
                    for i in range(2):
                        src = front_read(t, f"v{i}", None)
                        done(act.copy(va[:, 8 * i:8 * i + 8, 0:dh], src.rearrange("p (a d) -> p a d", d=dh)))
                else:
                    src = front_read(t, "v", None)
                    done(act.copy(va[:, :, 0:dh], src[:, 0:F].rearrange("p (a d) -> p a d", d=dh)))

            def copy_qk(t):
                if kind == "headnorm":
                    for name, dst in (("q", qT), ("k", kT)):
                        src = front_read(t, name, None)
                        done(act.copy(dst[:, :, :], src.rearrange("p (c t) -> p c t", c=4)))
                    return
                for side, dst in (("q", qT), ("k", kT)):
                    n = QC // 4
                    for i in range(n):
                        src = front_read(t, side if n == 1 else f"{side}{i}", None)
                        for c in range(4):
                            b = bq if side == "q" else (bk if kind == "rel" else None)
                            if b is None:
                                if c == 0:
                                    done(act.copy(dst[:, 4 * i:4 * i + 4, :], src.rearrange("p (c t) -> p c t", c=4)))
                            else:
                                ins_ = act.activation(dst[:, 4 * i + c, :], src[:, c * P:(c + 1) * P], ACT.Identity,
                                                      bias=b[:, 4 * i + c:4 * i + c + 1])
                                if c == 3:
                                    done(ins_)
                if kind == "nd":
                    src = front_read(t, "r", None)
                    for c in range(4):
                        ins_ = act.activation(rT[:, c, :], src[:, c * P:(c + 1) * P], ACT.Identity, bias=br[:, c:c + 1])
                    done(ins_)

            def copy_g(t):
                hp = 512 // GW
                for i in range(H // hp):
                    if i == 0 and (not isinstance(t, int) or t > 0):
                        act.wait_ge(g_out, 16 * t)
                    src = front_read(t, f"g{i}", None)
                    done(act.copy(g_sb[:, hp * i:hp * i + hp, :], src.rearrange("p (a d) -> p a d", d=GW)))

            def exp(t):
                for beta in range(4):
                    act.wait_ge(shifted, 4 * t + beta + 1)
                    act.activation(prob[:, beta, :], prob[:, beta, :], ACT.Exp,
                                   scale=1.0 if skewed else float(dh) ** -0.5).then_inc(expd, 1)

            def copy_pT(t):
                for beta in range(4):
                    act.wait_ge(probT_full, 4 * t + beta + 1)
                    act.copy(probT[:, beta, :], psS[:, beta, :]).then_inc(probT_read, 1)

            def front(t):
                copy_x(t)
                if skewed:
                    copy_qk(t)
                    copy_g(t)

            act.wait_ge(weights_in, 16 * n_weights)
            act.wait_ge(ones_set, 1 + (kind == "headnorm"))
            front(0)
            if not skewed:
                copy_qk(0)
            copy_v(0)
            with act.Fori(0, B - 1) as t:
                front(t + 1)
                exp(t)
                copy_pT(t)
                if not skewed:
                    copy_qk(t + 1)
                copy_v(t + 1)
            exp(B - 1)
            copy_pT(B - 1)

        @block.tensor
        def _(pe):
            def front_bank(t, name):
                j = names.index(name)
                bank = bank_of[name]
                prior = [i for i in range(j) if bank_of[names[i]] == bank]
                tt = t
                if not prior:
                    if isinstance(t, int) and t == 0:
                        return psF[:, bank, :]
                    prior = [i for i in range(NF) if bank_of[names[i]] == bank]
                    tt = t - 1
                p = prior[-1]
                if jobs[p][1] == "act":
                    n = sum(jobs[i][1] == "act" for i in range(p + 1))
                    pe.wait_ge(front_act, tt * NA + n)
                else:
                    pe.wait_ge(qk_ready, tt + 1)
                return psF[:, bank, :]

            def evacuated(t, name):
                j = names.index(name)
                n = sum(jobs[i][1] == "act" for i in range(j + 1))
                pe.wait_ge(front_act, t * NA + n)

            def front_x(t):
                bank = front_bank(t, "x")
                pe.wait_ge(xn_ready, t + 1)
                for c in range(DC):
                    mm = pe.transpose(bank[:, c * P:(c + 1) * P], xn[:, c * P:(c + 1) * P], core.ident[:, :])
                mm.then_inc(front_full, 1)

            def front_qk(t):
                evacuated(t, "x")
                if kind == "headnorm":
                    bank = front_bank(t, "qk")
                    for c in range(DC):
                        mm = pe.matmul(bank, xT[:, c, :], wqk[:, c, :], start=c == 0, stop=c == DC - 1)
                    mm.then_inc(front_full, 1)
                    return
                todo = [("q", wq, QC // 4), ("k", wk, QC // 4)] + ([("r", wr, 1)] if kind == "nd" else [])
                for side, w, n in todo:
                    for i in range(n):
                        bank = front_bank(t, side if n == 1 else f"{side}{i}")
                        for m in range(4):
                            for c in range(DC):
                                mm = pe.matmul(bank[:, m * P:(m + 1) * P], w[:, c, (4 * i + m) * P:(4 * i + m + 1) * P],
                                               xT[:, c, :], start=c == 0, stop=c == DC - 1)
                        mm.then_inc(front_full, 1)

            def front_g(t):
                hp = 512 // GW
                evacuated(t, "r" if kind == "nd" else "q")
                for i in range(H // hp):
                    bank = front_bank(t, f"g{i}")
                    for a in range(hp):
                        s, c = (hp * i + a) // 4, (hp * i + a) % 4
                        lhs = (rT if kind == "nd" else qT)[32 * s:32 * s + 16, c, :]
                        mm = pe.matmul(bank[:, a * GW:(a + 1) * GW], lhs, dist[32 * s:32 * s + 16, :], start=True, stop=True)
                    mm.then_inc(front_full, 1)

            def front_qkT(t):
                pe.wait_ge(qk_ready, t + 1)
                for i, name in enumerate(("q", "k")):
                    bank = front_bank(t, name)
                    for c in range(4):
                        src = qk[:, i * H + 4 * c:i * H + 4 * c + 4, :].rearrange("p a d -> p (a d)")
                        mm = pe.transpose(bank[:, c * P:(c + 1) * P], src, core.ident[:, :])
                    mm.then_inc(front_full, 1)

            def front_v(t):
                n = 2 if kind == "nd" else 1
                w = F // n
                for i in range(n):
                    bank = front_bank(t, "v" if n == 1 else f"v{i}")
                    for c in range(DC):
                        mm = pe.matmul(bank[:, 0:w], xT[:, c, :], wv[:, c, i * w:(i + 1) * w], start=c == 0,
                                       stop=c == DC - 1 and kind != "rel")
                    if kind == "rel":
                        mm = pe.matmul(bank[:, 0:w], core.ones[0:1, :], bv[:, :], start=False, stop=True)
                    mm.then_inc(front_full, 1)

            def scores(t):
                evacuated(t, names[NF - 1])
                if not isinstance(t, int) or t > 0:
                    pe.wait_ge(probT_read, 4 * t)
                for beta in range(4):
                    if kind == "headnorm":
                        pe.matmul(psS[:, beta, :], core.ident_bf[:, :], core.causal[:, :], start=True, stop=False)
                    for slot in range(4):
                        head = heads_of[beta, slot]
                        _, _, s0, c = place(head)
                        mm = pe.matmul(psS[:, beta, slot * P:(slot + 1) * P], qT[s0:s0 + dh, c, :], kT[s0:s0 + dh, c, :],
                                       start=kind != "headnorm", stop=slot == 3 or kind != "headnorm")
                    mm.then_inc(scores_full, 1)

            def weightsT(t):
                for beta in range(4):
                    pe.wait_ge(expd, 4 * t + beta + 1)
                    for slot in range(4):
                        mm = pe.transpose(psS[:, beta, slot * P:(slot + 1) * P], prob[:, beta, slot * P:(slot + 1) * P],
                                          core.ident[:, :])
                    mm.then_inc(probT_full, 1)

            def back_bank(t, j):
                if j >= 2:
                    pe.wait_ge(back_read, t * NBK + j - 1)
                elif not isinstance(t, int) or t > 0:
                    pe.wait_ge(back_read, t * NBK)
                return psB[:, j % 2, :]

            def values(t):
                for n, hs in enumerate(o_jobs):
                    bank = back_bank(t, n)
                    for i, head in enumerate(hs):
                        beta, slot, _, _ = place(head)
                        if n == 0 and i == 0:
                            pe.wait_ge(probT_read, 4 * t + 4)
                        mm = pe.matmul(bank[:, i * (dh + 1):(i + 1) * (dh + 1)], probT[:, beta, slot * P:(slot + 1) * P],
                                       va[:, head, :], start=True, stop=True)
                    mm.then_inc(back_full, 1)

            def project(t):
                for n, cs in enumerate(t_jobs):
                    j = len(o_jobs) + n
                    bank = back_bank(t, j)
                    pe.wait_ge(back_read, t * NBK + len(o_jobs))
                    for i, c in enumerate(cs):
                        mm = pe.transpose(bank[:, i * P:(i + 1) * P], o[:, c * P:(c + 1) * P], core.ident[:, :])
                    mm.then_inc(back_full, 1)
                bank = back_bank(t, NBK - 1)
                pe.wait_ge(back_read, t * NBK + NBK - 1)
                pe.matmul(bank[:, 0:D], core.ones[0:1, :], bo[:, :], start=True, stop=False)
                for c in range(FC):
                    mm = pe.matmul(bank[:, 0:D], oT[:, c, :], wo[:, c, :], start=False, stop=c == FC - 1)
                mm.then_inc(back_full, 1)

            def front(t):
                front_x(t)
                front_qk(t)
                if skewed:
                    front_g(t)

            pe.wait_ge(weights_in, 16 * n_weights)
            front(0)
            if not skewed:
                front_qkT(0)
            front_v(0)
            with pe.Fori(0, B - 1) as t:
                scores(t)
                front(t + 1)
                weightsT(t)
                values(t)
                if not skewed:
                    front_qkT(t + 1)
                front_v(t + 1)
                project(t)
            scores(B - 1)
            weightsT(B - 1)
            values(B - 1)
            project(B - 1)

        @block.vector
        def _(dve):
            chain = Chain(dve, dve_chain)
            norm.stats(dve)
            if kind == "headnorm":
                dve.wait_ge(ones_set, 2)
                dve.wait_ge(weights_in, 16 * n_weights)

            def normal(t):
                norm.normalise(dve, xn[:, :], t).then_inc(xn_ready, 1)

            def head_norm(t):
                dve.wait_ge(front_full, t * NF + 2)
                src = psF[:, 1, :].rearrange("p (a d) -> p a d", d=dh)
                chain.step(dve.tensor_reduce(hsum[:, :], src, AX.X, ALU.add))
                chain.step(dve.tensor_scalar(hsum[:, :], hsum[:, :], 1.0 / dh, None, ALU.mult))
                chain.step(dve.tensor_tensor(cen[:, :, :], src, hsum[:, :].unsqueeze(2).to_broadcast([P, 2 * H, dh]), ALU.subtract))
                chain.step(dve.tensor_tensor(sq[:, :, :], cen[:, :, :], cen[:, :, :], ALU.mult))
                chain.step(dve.tensor_reduce(hvar[:, :], sq[:, :, :], AX.X, ALU.add))
                dve.tensor_scalar(hvar[:, :], hvar[:, :], 1.0 / dh, LN_EPS, ALU.mult, ALU.add).then_inc(hv_done, 1)
                dve.wait_ge(hr_done, t + 1)
                chain.step(dve.tensor_tensor(cen[:, :, :], cen[:, :, :], hvar[:, :].unsqueeze(2).to_broadcast([P, 2 * H, dh]), ALU.mult))
                for i in range(2):
                    c2 = cen[:, i * H:(i + 1) * H, :]
                    ins_ = dve.tensor_tensor(sq[:, i * H:(i + 1) * H, :], c2, hw[:, i:i + 1, :].to_broadcast([P, H, dh]), ALU.mult)
                chain.step(ins_)
                for i in range(2):
                    ins_ = dve.tensor_tensor(qk[:, i * H:(i + 1) * H, 0:dh], sq[:, i * H:(i + 1) * H, :],
                                             hb[:, i:i + 1, :].to_broadcast([P, H, dh]), ALU.add)
                ins_.then_inc(qk_ready, 1)

            def shift(t):
                for beta in range(4):
                    dve.wait_ge(scores_full, 4 * t + beta + 1)
                    if beta == 0 and skewed:
                        dve.wait_ge(e_in, 16 * (t + 1))
                    src = psS[:, beta, :].rearrange("p (a k) -> p a k", k=P)
                    dst = prob[:, beta, :].rearrange("p (a k) -> p a k", k=P)
                    tp = top[:, 4 * beta:4 * beta + 4]
                    if skewed:
                        scale = float(dh) ** -0.5
                        chain.step(dve.scalar_tensor_tensor(out=dst, in0=src, scalar=scale, in1=e_sb[:, beta, :, :],
                                                            op0=ALU.mult, op1=ALU.add))
                        src = dst
                    chain.step(dve.tensor_reduce(tp, src, AX.X, ALU.max))
                    dve.tensor_tensor(dst, src, tp.unsqueeze(2).to_broadcast([P, 4, P]), ALU.subtract).then_inc(shifted, 1)

            def back(t):
                for n, hs in enumerate(o_jobs):
                    dve.wait_ge(back_full, t * NBK + n + 1)
                    src = psB[:, n % 2, 0:len(hs) * (dh + 1)].rearrange("p (a d) -> p a d", d=dh + 1)
                    iv = inv[:, hs[0]:hs[-1] + 1]
                    chain.step(dve.reciprocal(iv, src[:, :, dh]))
                    dve.tensor_tensor(o[:, hs[0] * dh:(hs[-1] + 1) * dh].rearrange("p (a d) -> p a d", d=dh),
                                      src[:, :, 0:dh], iv.unsqueeze(2).to_broadcast([P, len(hs), dh]),
                                      ALU.mult).then_inc(back_read, 1)
                for n, cs in enumerate(t_jobs):
                    j = len(o_jobs) + n
                    dve.wait_ge(back_full, t * NBK + j + 1)
                    dve.tensor_copy(oT[:, cs[0]:cs[-1] + 1, :],
                                    psB[:, j % 2, 0:len(cs) * P].rearrange("p (a d) -> p a d", d=P)).then_inc(back_read, 1)
                dve.wait_ge(back_full, t * NBK + NBK)
                dve.tensor_tensor(h[:, t, :], h[:, t, :], psB[:, (NBK - 1) % 2, 0:D], ALU.add).then_inc(back_read, 1)

            dve.wait_ge(norm.rstd_done, 1)
            normal(0)
            if not skewed:
                head_norm(0)
            first = chain.count
            steps = {"headnorm": 4 + 7 + 1, "nd": 8 + 3, "rel": 8 + 1}[kind]
            with dve.Fori(0, B - 1) as t:
                chain.begin(t * steps + first)
                dve.wait_ge(scores_full, 4 * t + 1)
                normal(t + 1)
                shift(t)
                if not skewed:
                    head_norm(t + 1)
                back(t)
                assert chain.count == steps
            chain.begin(first + (B - 1) * steps)
            shift(B - 1)
            back(B - 1)


def pick_first(dve, chain, score, best, mask, tmp, rank, groups, n):
    wide = [P, groups, n]
    chain.step(dve.tensor_reduce(best, score, AX.X, ALU.max))
    chain.step(dve.tensor_tensor(tmp, score, best.unsqueeze(2).to_broadcast(wide), ALU.is_equal))
    chain.step(dve.tensor_tensor(tmp, tmp, rank, ALU.mult))
    chain.step(dve.tensor_reduce(best, tmp, AX.X, ALU.max))
    chain.step(dve.tensor_tensor(mask, tmp, best.unsqueeze(2).to_broadcast(wide), ALU.is_equal))


def route_top2(core, dve, act_exp, chain, logits, w, bufs, E):
    wide = [P, B, E]
    score, tmp, mask, best, rank, tot = bufs
    chain.step(dve.tensor_reduce(best, logits, AX.X, ALU.max))
    act_exp(dve.tensor_tensor(score, logits, best.unsqueeze(2).to_broadcast(wide), ALU.subtract))
    chain.step(dve.tensor_reduce(tot, score, AX.X, ALU.add))
    chain.step(dve.reciprocal(tot, tot))
    chain.step(dve.tensor_tensor(score, score, tot.unsqueeze(2).to_broadcast(wide), ALU.mult))
    pick_first(dve, chain, score, best, mask, tmp, rank, B, E)
    chain.step(dve.tensor_tensor(w, score, mask, ALU.mult))
    chain.step(dve.scalar_tensor_tensor(out=score, in0=mask, scalar=-4.0, in1=score, op0=ALU.mult, op1=ALU.add))
    pick_first(dve, chain, score, best, mask, tmp, rank, B, E)
    chain.step(dve.tensor_tensor(score, score, mask, ALU.mult))
    chain.step(dve.tensor_tensor(w, w, score, ALU.add))


def route_top1(core, dve, act_exp, chain, logits, w, bufs, E):
    wide = [P, B, E]
    score, tmp, mask, best, rank, tot = bufs
    pick_first(dve, chain, logits, best, mask, tmp, rank, B, E)
    chain.step(dve.tensor_reduce(best, logits, AX.X, ALU.max))
    act_exp(dve.tensor_tensor(score, logits, best.unsqueeze(2).to_broadcast(wide), ALU.subtract))
    chain.step(dve.tensor_reduce(tot, score, AX.X, ALU.add))
    chain.step(dve.reciprocal(tot, tot))
    chain.step(dve.tensor_tensor(w, mask, tot.unsqueeze(2).to_broadcast(wide), ALU.mult))


def route_grouped(core, dve, act_sigmoid, chain, logits, w, bufs, E, bias, small):
    G, K = 4, 4
    N = E // G
    wide, grouped = [P, B, E], [P, B * G, N]
    score, tmp, mask, best, rank, tot = bufs
    sfc, rank4, gbest, gsum, gmask, gtmp, gpick = small
    by_group = lambda a: a.rearrange("p b (g n) -> p (b g) n", n=N)
    act_sigmoid(dve.tensor_copy(score, logits))
    chain.step(dve.tensor_tensor(sfc, score, bias.unsqueeze(1).to_broadcast(wide), ALU.add))
    chain.step(dve.tensor_reduce(gsum, by_group(sfc), AX.X, ALU.max))
    pick_first(dve, chain, by_group(sfc), gbest, by_group(mask), by_group(tmp), rank4.to_broadcast(grouped), B * G, N)
    chain.step(dve.scalar_tensor_tensor(out=tmp, in0=mask, scalar=-1e30, in1=sfc, op0=ALU.mult, op1=ALU.add))
    chain.step(dve.tensor_reduce(gbest, by_group(tmp), AX.X, ALU.max))
    chain.step(dve.tensor_tensor(gsum, gsum, gbest, ALU.add))
    per_row = lambda a: a.rearrange("p (b g) -> p b g", g=G)
    gb = tot
    pick_first(dve, chain, per_row(gsum), gb, per_row(gmask), per_row(gtmp), rank4.to_broadcast([P, B, G]), B, G)
    chain.step(dve.scalar_tensor_tensor(out=gsum, in0=gmask, scalar=-1e30, in1=gsum, op0=ALU.mult, op1=ALU.add))
    pick_first(dve, chain, per_row(gsum), gb, per_row(gpick), per_row(gtmp), rank4.to_broadcast([P, B, G]), B, G)
    chain.step(dve.tensor_tensor(gmask, gmask, gpick, ALU.add))
    chain.step(dve.tensor_tensor(by_group(sfc), by_group(sfc), gmask.unsqueeze(2).to_broadcast(grouped), ALU.mult))
    for k in range(K):
        pick_first(dve, chain, sfc, best, mask, tmp, rank, B, E)
        if k == 0:
            chain.step(dve.tensor_copy(w[:, :, 0:E], mask))
        else:
            chain.step(dve.tensor_tensor(w[:, :, 0:E], w[:, :, 0:E], mask, ALU.add))
        if k < K - 1:
            chain.step(dve.scalar_tensor_tensor(out=sfc, in0=mask, scalar=-1e30, in1=sfc, op0=ALU.mult, op1=ALU.add))
    chain.step(dve.tensor_tensor(w[:, :, 0:E], w[:, :, 0:E], score, ALU.mult))
    chain.step(dve.tensor_reduce(tot, w[:, :, 0:E], AX.X, ALU.add))
    chain.step(dve.tensor_scalar(tot, tot, 1e-20, None, ALU.add))
    chain.step(dve.reciprocal(tot, tot))
    chain.step(dve.tensor_tensor(w[:, :, 0:E], w[:, :, 0:E], tot.unsqueeze(2).to_broadcast(wide), ALU.mult))


def ffn(core, kind, src=None):
    nc, ins, h = core.nc, core.ins, core.h
    src = h if src is None else src
    nm = {"swiglu": "f0", "gelu": "f1", "dense": "f2", "silu": "f3"}[kind]
    E = {"swiglu": 8, "gelu": 8, "dense": 2, "silu": 18}[kind]
    ER = {"swiglu": 8, "gelu": 8, "dense": 0, "silu": 16}[kind]
    I = {"swiglu": 256, "gelu": 1024, "dense": 512, "silu": 352}[kind]
    gated = kind in ("swiglu", "silu")
    w1, w2 = ins[nm + "_w1"], ins[nm + "_w2"]
    NI = -(-I // P)
    width = [min(P, I - j * P) for j in range(NI)]
    W1 = I * (2 if gated else 1)
    G = 4
    TG = B // G
    N = TG * P

    ctx, sb, ps, sem = stage(nc, nm)
    with ctx:
        norm = TokenNorm(core, sb, sem, src)
        xn = sb("xn", [P, D])
        xTs = sb("xTs", [P, DC, P])
        xT = sb("xT", [P, DC, B * P])
        hid = sb("hid", [P, 2, NI, N])
        up_w = sb("up_w", [P, 2, DC, W1])
        down_w = sb("down_w", [P, 2, NI, D])
        nb = {"swiglu": 4, "gelu": NI, "dense": NI, "silu": 0}[kind]
        up_b = sb("up_b", [P, 2, max(nb, 1)])
        gate_t = sb("gate_t", [P, 2, N]) if gated else None
        sig_t = sb("sig_t", [P, 2, N]) if gated else None
        up_t = sb("up_t", [P, 2, N]) if kind == "swiglu" else None
        wts = sb("wts", [P, B * E, 1])
        w3 = wts[:, :, 0].rearrange("p (b e) -> p b e", e=E)
        psU = ps("up", [P, 4, 512])
        psD = ps("down", [P, 4, 512])
        psX, psL, psW, psO = psD[:, 0, 0:D], psD[:, 1, :], psD[:, 2, :], psD[:, 3, :]
        consts_in, xn_ready, x_full, x_read = sem("consts_in"), sem("xn_ready"), sem("x_full"), sem("x_read")
        logits_full, xTs_ready = sem("logits_full"), sem("xTs_ready")
        w_in = [sem("w_in0"), sem("w_in1")]
        up_full, hid_ready, lifted = sem("up_full"), sem("hid_ready"), sem("lifted")
        gate_read, sig_ready = sem("gate_read"), sem("sig_ready")
        down_full, h_added = sem("down_full"), sem("h_added")
        routed, act_done, dve_chain = sem("routed"), sem("act_done"), sem("dve_chain")
        wT_full, wT_ready, b_full, b_added = sem("wT_full"), sem("wT_ready"), sem("b_full"), sem("b_added")
        ew_chain = sem("ew_chain")
        consts = []
        if kind == "dense":
            gam, bet = sb("gam", [P, DC]), sb("bet", [P, DC])
            consts += [(gam[:, :], ins[nm + "_g"]), (bet[:, :], ins[nm + "_b"])]
        if ER:
            wr = sb("wr", [P, DC, ER])
            consts.append((wr[:, :, :], ins[nm + "_wr"].rearrange("(c p) n -> p c n", p=P)))
            rank = sb("rank", [P, B, ER])
            consts.append((rank[:, :, :].rearrange("p b e -> p (b e)"), ins[f"rank{ER}"].partition_broadcast(P)))
            r_b = sb("r_b", [P, ER])
            consts.append((r_b[:, :], ins[nm + "_rb"].partition_broadcast(P)))
            logits = sb("logits", [P, B, ER])
            bufs = [sb(n_, [P, B, ER])[:, :, :] for n_ in ("score", "tmp", "mask")]
            bufs += [sb("best", [P, B])[:, :], rank[:, :, :], sb("tot", [P, B])[:, :]]
            if kind == "silu":
                rank4 = sb("rank4", [P, 1, 4])
                consts.append((rank4[:, 0, :], ins["rank4"].partition_broadcast(P)))
                small = [sb("sfc", [P, B, ER])[:, :, :], rank4[:, :, :]] + [sb(n_, [P, B * 4])[:, :] for n_ in
                        ("gbest", "gsum", "gmask", "gtmp", "gpick")]
            else:
                b2 = sb("b2", [ER, D])
                consts.append((b2[:, :], ins[nm + "_b2"]))
                wT = sb("wT", [ER, P])
                w_s = sb("w_s", [P, ER])
        else:
            b2 = sb("b2", [1, D])
            consts.append((b2[:, :], ins[nm + "_b2"]))
        down_bias = kind != "silu"
        DMAS = 2 + (nb > 0)

        block = ctx.enter_context(nc.Block())

        def run_units(eng, first, second):
            def turn(i, u, last):
                for g in range(G):
                    if g < G - 1:
                        first(i, u, g + 1)
                    elif u == 0:
                        first(i, 1, 0)
                    elif not last:
                        first(i + 1, 0, 0)
                    if second is not None:
                        second(i, u, g)

            first(0, 0, 0)
            if E > 2:
                with eng.Fori(0, E // 2 - 1) as i:
                    turn(i, 0, False)
                    turn(i, 1, False)
            turn(E // 2 - 1, 0, False)
            turn(E // 2 - 1, 1, True)

        @block.sync
        def _(sp):
            for dst, s in consts:
                sp.dma_start(dst, s).then_inc(consts_in, 16)

            def load(e, u):
                sp.dma_start(up_w[:, u, :, :], w1[e].rearrange("(c p) n -> p c n", p=P)).then_inc(w_in[u], 16)
                sp.dma_start(down_w[:, u, :, :], w2[e].rearrange("(c p) n -> p c n", p=P)).then_inc(w_in[u], 16)
                if nb:
                    sp.dma_start(up_b[:, u, :], ins[nm + "_b1"][e]).then_inc(w_in[u], 16)

            load(0, 0)
            load(1, 1)
            if E > 2:
                with sp.Fori(1, E // 2) as i:
                    for u in range(2):
                        sp.wait_ge(down_full, TG * G * (2 * i + (u - 1)))
                        load(2 * i + u, u)

        @block.gpsimd
        def _(pool):
            if E > ER:
                pool.memset(w3[:, :, ER:E], 1.0).then_inc(routed, 1)
            norm.rsqrt(pool)

            def lift(n, j):
                pool.wait_ge(sig_ready, n * NI + j + 1)
                b = j % 2
                pool.tensor_tensor(sig_t[:, b, :], sig_t[:, b, :], gate_t[:, b, :], ALU.mult).then_inc(gate_read, 1)

            if kind == "swiglu":
                with pool.Fori(0, E * G) as n:
                    for j in range(NI):
                        lift(n, j)

        @block.scalar
        def _(act):
            act.wait_ge(consts_in, 16 * len(consts))
            if ER:
                act.wait_ge(routed, 1 + (E > ER))
                act.activation(bufs[0], bufs[0], ACT.Sigmoid if kind == "silu" else ACT.Exp).then_inc(act_done, 1)
                if down_bias:
                    with act.Fori(0, B) as t:
                        act.wait_ge(wT_full, t + 1)
                        act.copy(wT[:, :], psW[0:ER, 0:P]).then_inc(wT_ready, 1)

            def hidden(i, u, g):
                n = (2 * i + u) * G + g
                for j in range(NI):
                    m = width[j]
                    if kind in ("gelu", "dense"):
                        act.wait_ge(up_full, n * NI + j + 1)
                        act.activation(hid[0:m, g % 2, j, :], psU[0:m, (g * NI + j) % 4, :], ACT.Gelu,
                                       bias=up_b[:, u, j:j + 1]).then_inc(hid_ready, 1)
                    elif kind == "swiglu":
                        act.wait_ge(ew_chain, 2 * (n * NI + j) + 1)
                        act.activation(sig_t[:, j % 2, :], gate_t[:, j % 2, :], ACT.Sigmoid, scale=1.702).then_inc(sig_ready, 1)
                    else:
                        b = (g * NI + j) % 2
                        act.wait_ge(up_full, n * NI + j + 1)
                        act.activation(sig_t[0:m, b, :], psU[0:m, 2 * b, :], ACT.Silu).then_inc(sig_ready, 1)

            run_units(act, hidden, None)

        @block.tensor
        def _(pe):
            pe.wait_ge(consts_in, 16 * len(consts))
            with pe.Fori(0, B) as t:
                pe.wait_ge(xn_ready, t + 1)
                for c in range(DC):
                    mm = pe.transpose(psX[:, c * P:(c + 1) * P], xn[:, c * P:(c + 1) * P], core.ident[:, :])
                mm.then_inc(x_full, 1)
                pe.wait_ge(x_read, 2 * t + 2)
                if ER:
                    for c in range(DC):
                        mm = pe.matmul(psL[:, bass.ts(t, ER)], xTs[:, c, :], wr[:, c, :], start=c == 0, stop=c == DC - 1)
                    mm.then_inc(logits_full, 1)
            if down_bias:
                with pe.Fori(0, B) as t:
                    if ER:
                        pe.wait_ge(xTs_ready, t + 1)
                        pe.transpose(psW[0:ER, 0:P], w_s[:, :], core.ident[:, :]).then_inc(wT_full, 1)
                        pe.wait_ge(wT_ready, t + 1)
                        pe.matmul(psO[:, 0:D], wT[:, :], b2[:, :], start=True, stop=True).then_inc(b_full, 1)
                    else:
                        pe.matmul(psO[:, 0:D], core.ones[0:1, :], b2[:, :], start=True, stop=True).then_inc(b_full, 1)
                    pe.wait_ge(b_added, t + 1)

            def up(i, u, g):
                n = (2 * i + u) * G + g
                if g == 0:
                    pe.wait_ge(w_in[u], 16 * DMAS * (i + 1))
                for j in range(NI):
                    p = n * NI + j
                    m = width[j]
                    if gated:
                        b = (g * NI + j) % 2
                        if not (isinstance(n, int) and p < 2):
                            pe.wait_ge(hid_ready, p - 1)
                        banks = [(psU[0:m, 2 * b, :], j * P), (psU[0:m, 2 * b + 1, :], I + j * P)]
                    else:
                        b = (g * NI + j) % 4
                        if not (isinstance(n, int) and p < 4):
                            pe.wait_ge(hid_ready, p - 3)
                        banks = [(psU[0:m, b, :], j * P)]
                    for bank, col in banks:
                        for c in range(DC):
                            mm = pe.matmul(bank, up_w[:, u, c, col:col + m], xT[:, c, g * N:(g + 1) * N],
                                           start=c == 0, stop=c == DC - 1)
                    mm.then_inc(up_full, 1)

            def down(i, u, g):
                n = (2 * i + u) * G + g
                for k in range(TG):
                    pe.wait_ge(h_added, 4 * n + k + 1)
                    if k == 0:
                        pe.wait_ge(hid_ready, (n + 1) * NI)
                    for j in range(NI):
                        m = width[j]
                        mm = pe.matmul(psD[:, k, 0:D], hid[0:m, g % 2, j, k * P:(k + 1) * P], down_w[0:m, u, j, :],
                                       start=j == 0, stop=j == NI - 1)
                    mm.then_inc(down_full, 1)

            run_units(pe, up, down)

        @block.vector
        def _(dve):
            chain = Chain(dve, dve_chain)
            norm.stats(dve)
            dve.wait_ge(consts_in, 16 * len(consts))
            dve.wait_ge(norm.rstd_done, 1)
            with dve.Fori(0, B) as t:
                norm.normalise(dve, xn[:, :], t).then_inc(xn_ready, 1)
                dve.wait_ge(x_full, t + 1)
                for c in range(DC):
                    dst = xT[:, c, bass.ts(t, P)]
                    if kind == "dense":
                        i_ = dve.tensor_scalar(dst, psX[:, c * P:(c + 1) * P], gam[:, c:c + 1], bet[:, c:c + 1], ALU.mult, ALU.add)
                        if c == DC - 1:
                            i_.then_inc(x_read, 2)
                    else:
                        dve.tensor_scalar(dst, psX[:, c * P:(c + 1) * P], 1.0, None, ALU.mult)
                if ER:
                    dve.tensor_copy(xTs[:, :, :], psX.rearrange("p (c t) -> p c t", c=DC)).then_inc(x_read, 2)
            if ER:
                dve.wait_ge(logits_full, B)
                ps_l = psL[:, 0:B * ER].rearrange("p (b e) -> p b e", e=ER)
                r_bb = r_b[:, :].unsqueeze(1).to_broadcast([P, B, ER])

                def by_act(last):
                    last.then_inc(routed, 1)
                    dve.wait_ge(act_done, 1)

                if kind == "silu":
                    chain.step(dve.tensor_copy(logits[:, :, :], ps_l))
                    route_grouped(core, dve, by_act, chain, logits[:, :, :], w3, bufs, ER, r_b[:, :], small)
                else:
                    chain.step(dve.tensor_tensor(logits[:, :, :], ps_l, r_bb, ALU.add))
                    route = route_top2 if kind == "swiglu" else route_top1
                    route(core, dve, by_act, chain, logits[:, :, :], w3, bufs, ER)
            if down_bias:
                with dve.Fori(0, B) as t:
                    if ER:
                        dve.tensor_scalar(w_s[:, :], w3[:, t, :], 1.0, None, ALU.mult).then_inc(xTs_ready, 1)
                    dve.wait_ge(b_full, t + 1)
                    dve.tensor_tensor(h[:, t, :], h[:, t, :], psO[:, 0:D], ALU.add).then_inc(b_added, 1)
                dve.wait_ge(b_added, B)
            dve.sem_inc(h_added, 4)

            def hidden(i, u, g):
                n = (2 * i + u) * G + g
                if not gated:
                    return
                for j in range(NI):
                    m = width[j]
                    p = n * NI + j
                    if kind == "silu":
                        b = (g * NI + j) % 2
                        dve.wait_ge(sig_ready, p + 1)
                        dve.wait_ge(up_full, p + 1)
                        dve.tensor_tensor(hid[0:m, g % 2, j, :], sig_t[0:m, b, :], psU[0:m, 2 * b + 1, :], ALU.mult).then_inc(hid_ready, 1)
                    else:
                        b = j % 2
                        dve.wait_ge(up_full, p + 1)
                        dve.tensor_scalar(gate_t[:, b, :], psU[:, 2 * b, :], up_b[:, u, j:j + 1], 7.0, ALU.add, ALU.min).then_inc(ew_chain, 1)
                        dve.tensor_scalar(up_t[:, b, :], psU[:, 2 * b + 1, :], up_b[:, u, 2 + j:3 + j], 7.0, ALU.add, ALU.min).then_inc(ew_chain, 1)
                        dve.wait_ge(ew_chain, 2 * (p + 1))
                        dve.tensor_scalar(up_t[:, b, :], up_t[:, b, :], -7.0, 1.0, ALU.max, ALU.add).then_inc(lifted, 1)
                        dve.wait_ge(lifted, p + 1)
                        dve.wait_ge(gate_read, p + 1)
                        dve.tensor_tensor(hid[:, g % 2, j, :], sig_t[:, b, :], up_t[:, b, :], ALU.mult).then_inc(hid_ready, 1)

            def add(i, u, g):
                e = 2 * i + u
                n = e * G + g
                for k in range(TG):
                    dve.wait_ge(down_full, 4 * n + k + 1)
                    t = g * TG + k
                    dve.scalar_tensor_tensor(out=h[:, t, :], in0=psD[:, k, 0:D], scalar=wts[:, t * E + e, :], in1=h[:, t, :],
                                             op0=ALU.mult, op1=ALU.add).then_inc(h_added, 1)

            run_units(dve, hidden, add)


def delta_net(core, x0):
    nc, ins, h = core.nc, core.ins, core.h
    pre = "L2_attn_"
    H, dh, S2, BL = 16, 16, 2, B // 2
    W = 3 * D + 2 * H
    Q, K, V = range(3)
    ctx, sb, ps, sem = stage(nc, "dn")
    with ctx:
        pairs_kq = sb("kq", [P, S2, 2, dh, P])
        pairs_bv = sb("bv", [P, S2, dh, P])
        pairs_g = sb("gates", [P, S2, 2, P])
        tokens = sb("tokens", [P, 3, B, D])
        rates = sb("rates", [P, 2, B, H])
        proj_in = ExitStack()
        ctx1, sb1, ps1, sem1 = stage(nc, "dn1")
        with ctx1:
            outer = TokenNorm(core, sb1, sem1, h)
            ctx_i, sbi, _, semi = stage(nc, "dn1i")
            ctx1.enter_context(ctx_i)
            inner = TokenNorm(core, sbi, semi, x0)
            xn, xT = sb1("xn", [P, D]), sb1("xT", [P, DC, P])
            w = sb1("w", [P, DC, W])
            gam, bet = sb1("gam", [P, DC]), sb1("bet", [P, DC])
            psX, psY = ps1("x", [P, 512]), ps1("y", [P, 2, 512])
            loaded, x0_done, xn_ready = sem1("loaded"), sem1("x0_done"), sem1("xn_ready")
            x_full, x_read, y_full, y_read = sem1("x_full"), sem1("x_read"), sem1("y_full"), sem1("y_read")
            block = ctx1.enter_context(nc.Block())

            @block.sync
            def _(sp):
                at = 0
                for n in ("Wq", "Wk", "Wv", "Wb", "Wg"):
                    src = ins[pre + n]
                    sp.dma_start(w[:, :, at:at + src.shape[1]], src.rearrange("(c p) n -> p c n", p=P)).then_inc(loaded, 16)
                    at += src.shape[1]
                sp.dma_start(gam[:, :], ins["f2_ln1_g"]).then_inc(loaded, 16)
                sp.dma_start(bet[:, :], ins["f2_ln1_b"]).then_inc(loaded, 16)

            @block.gpsimd
            def _(pool):
                outer.rsqrt(pool)
                inner.rsqrt(pool)

            @block.vector
            def _(dve):
                outer.stats(dve)
                dve.wait_ge(outer.rstd_done, 1)
                with dve.Fori(0, B) as t:
                    outer.normalise(dve, x0[:, t, :], t).then_inc(x0_done, 1)
                dve.wait_ge(x0_done, B)
                inner.stats(dve)
                dve.wait_ge(inner.rstd_done, 1)

                def normal(t):
                    inner.normalise(dve, xn[:, :], t).then_inc(xn_ready, 1)

                def copy(t):
                    dve.wait_ge(y_full, 2 * t + 1)
                    dve.tensor_scalar(tokens[:, Q, t, :], psY[:, 0, 0:D], float(dh) ** -0.5, None, ALU.mult)
                    dve.tensor_scalar(tokens[:, K, t, :], psY[:, 0, D:2 * D], 1.0, None, ALU.mult).then_inc(y_read, 1)
                    dve.wait_ge(y_full, 2 * t + 2)
                    dve.tensor_scalar(tokens[:, V, t, :], psY[:, 1, 0:D], 1.0, None, ALU.mult)
                    dve.tensor_scalar(rates[:, :, t, :], psY[:, 1, D:D + 2 * H].rearrange("p (j h) -> p j h", j=2), 1.0, None,
                                      ALU.mult).then_inc(y_read, 1)

                normal(0)
                with dve.Fori(0, B - 1) as t:
                    dve.wait_ge(x_full, t + 1)
                    normal(t + 1)
                    copy(t)
                copy(B - 1)

            @block.scalar
            def _(act):
                act.wait_ge(loaded, 16 * 7)
                with act.Fori(0, B) as t:
                    act.wait_ge(x_full, t + 1)
                    for c in range(DC):
                        a = act.activation(xT[:, c, :], psX[:, c * P:(c + 1) * P], ACT.Identity,
                                           bias=bet[:, c:c + 1], scale=gam[:, c:c + 1])
                    a.then_inc(x_read, 1)

            @block.tensor
            def _(pe):
                pe.wait_ge(loaded, 16 * 7)

                def project(t, again):
                    pe.wait_ge(xn_ready, t + 1)
                    for c in range(DC):
                        mm = pe.transpose(psX[:, c * P:(c + 1) * P], xn[:, c * P:(c + 1) * P], core.ident[:, :])
                    mm.then_inc(x_full, 1)
                    pe.wait_ge(x_read, t + 1)
                    for bank, a, b in ((0, 0, 2 * D), (1, 2 * D, W)):
                        if again:
                            pe.wait_ge(y_read, 2 * t + bank - 1)
                        for c in range(DC):
                            mm = pe.matmul(psY[:, bank, 0:b - a], xT[:, c, :], w[:, c, a:b], start=c == 0, stop=c == DC - 1)
                        mm.then_inc(y_full, 1)

                project(0, False)
                with pe.Fori(1, B) as t:
                    project(t, True)

        ctx2, sb2, ps2, sem2 = stage(nc, "dn2")
        with ctx2:
            sq = sb2("sq", [P, B, D])
            nrm = sb2("nrm", [P, B * H])
            psT = ps2("t", [P, 4, 512])
            chained, squared, rooted, gated, ready = sem2("chained"), sem2("squared"), sem2("rooted"), sem2("gated"), sem2("ready")
            t_full, t_read = sem2("t_full"), [sem2("t_read0"), sem2("t_read1")]
            block = ctx2.enter_context(nc.Block())
            keys = tokens[:, K]
            vals = tokens[:, V]
            heads = lambda a: a.rearrange("p b (h d) -> p (b h) d", d=dh)
            beta, gate = (rates[:, j].rearrange("p b h -> p (b h)") for j in range(2))
            views = []
            for s in range(S2):
                for off, dst in ((K, pairs_kq[:, s, 0]), (Q, pairs_kq[:, s, 1]), (V, pairs_bv[:, s])):
                    for d0 in range(0, dh, 4):
                        srcs = [heads(tokens[:, off])[:, s * P:(s + 1) * P, d0 + i] for i in range(4)]
                        views.append((srcs, dst[:, d0:d0 + 4, :]))
                views.append(([r[:, s * P:(s + 1) * P] for r in (beta, gate)], pairs_g[:, s]))

            @block.vector
            def _(dve):
                chain = Chain(dve, chained)
                dve.tensor_tensor(sq[:, :, :], keys, keys, ALU.mult).then_inc(squared, 1)
                dve.wait_ge(squared, 1)
                dve.tensor_reduce(nrm[:, :], heads(sq[:, :, :]), AX.X, ALU.add).then_inc(squared, 1)
                dve.wait_ge(rooted, 1)
                chain.step(dve.tensor_scalar(nrm[:, :], nrm[:, :], 1e-6, None, ALU.add))
                chain.step(dve.reciprocal(nrm[:, :], nrm[:, :]))
                wide = [P, B * H, dh]
                dve.tensor_tensor(heads(keys), heads(keys), nrm[:, :].unsqueeze(2).to_broadcast(wide), ALU.mult)
                dve.wait_ge(gated, 1)
                chain.step(dve.tensor_tensor(heads(vals), heads(vals), beta.unsqueeze(2).to_broadcast(wide), ALU.mult))
                dve.tensor_tensor(beta, beta, gate, ALU.mult).then_inc(ready, 1)
                for n in range(1, len(views), 2):
                    srcs, dst = views[n]
                    dve.wait_ge(t_full, n + 1)
                    dve.tensor_copy(dst, psT[:, n % 4, 0:len(srcs) * P].rearrange("p (a t) -> p a t", t=P)).then_inc(t_read[1], 1)

            @block.scalar
            def _(act):
                act.activation(rates[:, :, :, :], rates[:, :, :, :], ACT.Sigmoid).then_inc(gated, 1)
                act.wait_ge(squared, 2)
                act.activation(nrm[:, :], nrm[:, :], ACT.Sqrt).then_inc(rooted, 1)
                for n in range(0, len(views), 2):
                    srcs, dst = views[n]
                    act.wait_ge(t_full, n + 1)
                    act.copy(dst, psT[:, n % 4, 0:len(srcs) * P].rearrange("p (a t) -> p a t", t=P)).then_inc(t_read[0], 1)

            @block.tensor
            def _(pe):
                pe.wait_ge(ready, 1)
                for n, (srcs, dst) in enumerate(views):
                    if n >= 4:
                        pe.wait_ge(t_read[n % 2], (n - 4) // 2 + 1)
                    for i, src in enumerate(srcs):
                        mm = pe.transpose(psT[:, n % 4, i * P:(i + 1) * P], src, core.ident[:, :])
                    mm.then_inc(t_full, 1)

        ctx3, sb3, ps3, sem3 = stage(nc, "dn3")
        with ctx3:
            state = sb3("state", [P, S2, dh, dh])
            prod = sb3("prod", [P, S2, 2, dh, dh])
            red = sb3("red", [P, S2, 2, dh])
            outp = sb3("outp", [P, S2, dh, dh])
            hist_a = tokens[:, 0:2].rearrange("p q b w -> p (q b w)").rearrange(
                "p (s j v t) -> p s j v t", s=S2, j=2, v=dh)
            hist_u = sb3("hist_u", [P, S2, dh, P])
            qk = sb3("qk", [P, S2, P])
            chained = sem3("chained")
            block = ctx3.enter_context(nc.Block())

            @block.vector
            def _(dve):
                chain = Chain(dve, chained)
                kq = pairs_kq
                chain.step(dve.tensor_tensor(hist_u[:, :, :, :], kq[:, :, 0], kq[:, :, 1], ALU.mult))
                chain.step(dve.tensor_reduce(qk[:, :, :], hist_u[:, :, :, :].rearrange("p s d t -> p s t d"), AX.X, ALU.add))
                chain.step(dve.memset(state[:, :, :, :], 0.0))
                first, steps = chain.count, 6
                with dve.Fori(0, P) as t:
                    chain.begin(t * steps + first)
                    for s in range(S2):
                        i_ = dve.tensor_tensor(prod[:, s], state[:, s].unsqueeze(1).to_broadcast([P, 2, dh, dh]),
                                               kq[:, s, :, :, t].unsqueeze(2).to_broadcast([P, 2, dh, dh]), ALU.mult)
                    chain.step(i_)
                    chain.step(dve.tensor_reduce(red[:, :, :, :], prod[:, :, :, :, :], AX.X, ALU.add))
                    chain.step(dve.tensor_tensor(hist_a[:, :, :, :, t], red[:, :, :, :],
                                                 pairs_g[:, :, :, t].unsqueeze(3).to_broadcast([P, S2, 2, dh]), ALU.mult))
                    chain.step(dve.tensor_tensor(hist_u[:, :, :, t], pairs_bv[:, :, :, t], hist_a[:, :, 0, :, t], ALU.subtract))
                    dve.tensor_tensor(outp[:, :, :, :], hist_u[:, :, :, t].unsqueeze(3).to_broadcast([P, S2, dh, dh]),
                                      kq[:, :, 0, :, t].unsqueeze(2).to_broadcast([P, S2, dh, dh]), ALU.mult).then_inc(chained, 1)
                    chain.count += 1
                    dve.wait_ge(chained, chain.base + chain.count)
                    for s in range(S2):
                        i_ = dve.scalar_tensor_tensor(out=state[:, s], in0=state[:, s], scalar=pairs_g[:, s, 1, t].unsqueeze(1),
                                                      in1=outp[:, s], op0=ALU.mult, op1=ALU.add)
                    chain.step(i_)
                    assert chain.count == 6
                chain.begin(6 * P + first)
                chain.step(dve.tensor_tensor(hist_u[:, :, :, :], hist_u[:, :, :, :], qk[:, :, :].unsqueeze(2).to_broadcast([P, S2, dh, P]), ALU.mult))
                chain.step(dve.tensor_tensor(hist_u[:, :, :, :], hist_u[:, :, :, :], hist_a[:, :, 1], ALU.add))
                dve.tensor_copy(pairs_bv[:, :, :, :], hist_u[:, :, :, :])

        ctx4, sb4, ps4, sem4 = stage(nc, "dn4")
        with ctx4:
            att = sb4("att", [P, B, D])
            xcur = sb4("xcur", [P, 2, D])
            aT = sb4("aT", [P, 2, DC, P])
            wo, bo = sb4("wo", [P, DC, D]), sb4("bo", [1, D])
            psT, psA, psO = ps4("t", [P, 4, 512]), ps4("a", [P, 2, 512]), ps4("o", [P, 2, 512])
            loaded, t_full, t_read0, t_read1 = sem4("loaded"), sem4("t_full"), sem4("t_read0"), sem4("t_read1")
            a_full, a_read, o_full, o_added, x_added = sem4("a_full"), sem4("a_read"), sem4("o_full"), sem4("o_added"), sem4("x_added")
            t_read = [t_read0, t_read1]
            att_ready = sem4("att_ready")
            block = ctx4.enter_context(nc.Block())
            views = [(s, v0) for s in range(S2) for v0 in range(0, dh, 4)]

            def spread(n):
                s, v0 = views[n]
                src = psT[:, n % 4, :].rearrange("p (v b h) -> p b h v", v=4, b=BL)
                dst = heads4(att[:, s * BL:(s + 1) * BL, :])[:, :, :, v0:v0 + 4]
                return dst, src

            heads4 = lambda a: a.rearrange("p b (h d) -> p b h d", d=dh)

            @block.sync
            def _(sp):
                sp.dma_start(wo[:, :, :], ins[pre + "Wo"].rearrange("(c p) n -> p c n", p=P)).then_inc(loaded, 16)
                sp.dma_start(bo[:, :], ins[pre + "bo"].unsqueeze(0)).then_inc(loaded, 16)

            def spread_all(eng, par):
                for n in range(par, len(views), 2):
                    eng.wait_ge(t_full, n + 1)
                    dst, src = spread(n)
                    for v in range(4):
                        if par:
                            i_ = eng.tensor_copy(dst[:, :, :, v], src[:, :, :, v])
                        else:
                            i_ = eng.copy(dst[:, :, :, v], src[:, :, :, v])
                    i_.then_inc(t_read[par], 1)

            @block.scalar
            def _(act):
                spread_all(act, 0)
                with act.Fori(0, B // 2) as i:
                    for u in range(2):
                        act.wait_ge(a_full, 2 * i + u + 1)
                        act.copy(aT[:, u, :, :], psA[:, u, 0:D].rearrange("p (c t) -> p c t", c=DC)).then_inc(a_read, 1)

            @block.vector
            def _(dve):
                spread_all(dve, 1)
                with dve.Fori(0, B // 2) as i:
                    for u in range(2):
                        t = 2 * i + u
                        dve.wait_ge(t_read[0], 4)
                        dve.tensor_scalar(xcur[:, u, :], att[:, t, :], 1.0, None, ALU.mult).then_inc(att_ready, 1)
                    for u in range(2):
                        t = 2 * i + u
                        dve.wait_ge(o_full, 2 * i + u + 1)
                        dve.tensor_tensor(x0[:, t, :], x0[:, t, :], psO[:, u, 0:D], ALU.add).then_inc(o_added, 1)
                        dve.wait_ge(o_added, 2 * i + u + 1)
                        dve.tensor_tensor(h[:, t, :], h[:, t, :], x0[:, t, :], ALU.add).then_inc(x_added, 1)

            @block.tensor
            def _(pe):
                for n, (s, v0) in enumerate(views):
                    if n >= 4:
                        pe.wait_ge(t_read[n % 2], (n - 4) // 2 + 1)
                    for i in range(4):
                        mm = pe.transpose(psT[:, n % 4, i * P:(i + 1) * P], pairs_bv[:, s, v0 + i, :], core.ident[:, :])
                    mm.then_inc(t_full, 1)
                pe.wait_ge(loaded, 32)
                with pe.Fori(0, B // 2) as i:
                    for u in range(2):
                        t = 2 * i + u
                        pe.wait_ge(att_ready, t + 1)
                        for c in range(DC):
                            mm = pe.transpose(psA[:, u, c * P:(c + 1) * P], xcur[:, u, c * P:(c + 1) * P], core.ident[:, :])
                        mm.then_inc(a_full, 1)
                    for u in range(2):
                        pe.wait_ge(a_read, 2 * i + u + 1)
                        pe.matmul(psO[:, u, 0:D], core.ones[0:1, :], bo[:, :], start=True, stop=False)
                        for c in range(DC):
                            mm = pe.matmul(psO[:, u, 0:D], aT[:, u, c, :], wo[:, c, :], start=False, stop=c == DC - 1)
                        mm.then_inc(o_full, 1)


MIDS_HALF = (0.25, 0.75, 1.25, 1.75)
MIDS_ONE = (2.5, 3.5)
MID_TWO = 5.0
FP4_BLOCK = 16


class Fp4:

    def __init__(self, sb, name, width):
        self.width, self.n = width, width // FP4_BLOCK
        self.mag = sb(f"{name}_mag", [P, width])
        self.half, self.one = sb(f"{name}_half", [P, width]), sb(f"{name}_one", [P, width])
        self.scale, self.inv = sb(f"{name}_scale", [P, self.n]), sb(f"{name}_inv", [P, self.n])

    def magnitude(self, act, x):
        return act.activation(self.mag[:, :], x, ACT.Abs)

    def steps(self, dve, chain, x, out):
        blocks = lambda a: a.rearrange("p (n k) -> p n k", k=FP4_BLOCK)
        wide = [P, self.n, FP4_BLOCK]
        mag, half, one = self.mag[:, :], self.half[:, :], self.one[:, :]
        chain.step(dve.tensor_reduce(self.scale[:, :], blocks(mag), AX.X, ALU.max))
        chain.step(dve.tensor_scalar(self.scale[:, :], self.scale[:, :], 1.0 / 6.0, 1e-12, ALU.mult, ALU.max))
        chain.step(dve.reciprocal(self.inv[:, :], self.scale[:, :]))
        chain.step(dve.tensor_tensor(blocks(mag), blocks(mag), self.inv[:, :].unsqueeze(2).to_broadcast(wide), ALU.mult))
        chain.step(dve.tensor_scalar(half, mag, MIDS_HALF[0], None, ALU.is_gt))
        for m in MIDS_HALF[1:]:
            chain.step(dve.scalar_tensor_tensor(out=half, in0=mag, scalar=m, in1=half, op0=ALU.is_gt, op1=ALU.add))
        chain.step(dve.tensor_scalar(one, mag, MID_TWO, 2.0, ALU.is_gt, ALU.mult))
        for m in MIDS_ONE:
            chain.step(dve.scalar_tensor_tensor(out=one, in0=mag, scalar=m, in1=one, op0=ALU.is_gt, op1=ALU.add))
        chain.step(dve.scalar_tensor_tensor(out=half, in0=half, scalar=0.5, in1=one, op0=ALU.mult, op1=ALU.add))
        chain.step(dve.scalar_tensor_tensor(out=half.bitcast(U32), in0=x.bitcast(U32), scalar=0x80000000, in1=half.bitcast(U32),
                                            op0=ALU.bitwise_and, op1=ALU.bitwise_or))
        return dve.tensor_tensor(blocks(out), blocks(half), self.scale[:, :].unsqueeze(2).to_broadcast(wide), ALU.mult)


def fp4_ffn(core):
    nc, ins, h = core.nc, core.ins, core.h
    I = 704
    IC = -(-I // P)
    IP = IC * P
    HALF = I // 2
    ctx, sb, ps, sem = stage(nc, "f4")
    with ctx:
        wT = sb("wT", [P, DC, 2 * IP])
        dT = sb("dT", [P, IC, D])
        ctx1, sb1, ps1, sem1 = stage(nc, "f4w")
        with ctx1:
            NP = 3
            raw = sb1("raw", [P, 2 * IC, D])
            raw_d = sb1("raw_d", [P, DC, IP])
            fq = Fp4(sb1, "q", IC * D)
            psT = ps1("t", [P, 4, 512])
            loaded, mag_done, rounded, chained = sem1("loaded"), sem1("mag_done"), sem1("rounded"), sem1("chained")
            t_full, t_read = sem1("t_full"), sem1("t_read")
            flat = lambda a: a.rearrange("p a b -> p (a b)")
            parts = [flat(raw[:, 0:IC, :]), flat(raw[:, IC:2 * IC, :]), flat(raw_d[:, :, :])]
            views = []
            for side in range(2):
                for c in range(DC):
                    for a in range(0, IC, 3):
                        views.append((side, [raw[:, side * IC + a + i, c * P:(c + 1) * P] for i in range(3)],
                                      wT[:, c, side * IP + a * P:side * IP + (a + 3) * P]))
            for j in range(0, IC, 2):
                views.append((2, [raw_d[:, c, (j + i) * P:(j + i + 1) * P] for i in range(2) for c in range(DC)],
                              flat(dT[:, j:j + 2, :])))
            block = ctx1.enter_context(nc.Block())

            @block.sync
            def _(sp):
                sp.dma_start(raw[:, 0:IC, :], ins["f4_gate"].rearrange("(a p) n -> p a n", p=P)).then_inc(loaded, 16)
                sp.dma_start(raw[:, IC:2 * IC, :], ins["f4_up"].rearrange("(a p) n -> p a n", p=P)).then_inc(loaded, 16)
                sp.dma_start(raw_d[:, :, :], ins["f4_down"].rearrange("(a p) n -> p a n", p=P)).then_inc(loaded, 16)

            @block.scalar
            def _(act):
                act.wait_ge(loaded, 48)
                for i, part in enumerate(parts):
                    if i:
                        act.wait_ge(rounded, i)
                    fq.magnitude(act, part).then_inc(mag_done, 1)
                for n, (_, srcs, dst) in enumerate(views):
                    act.wait_ge(t_full, n + 1)
                    act.copy(dst, psT[:, n % 4, 0:len(srcs) * P]).then_inc(t_read, 1)

            @block.vector
            def _(dve):
                chain = Chain(dve, chained)
                for i, part in enumerate(parts):
                    dve.wait_ge(mag_done, i + 1)
                    fq.steps(dve, chain, part, part).then_inc(rounded, 1)

            @block.tensor
            def _(pe):
                for n, (part, srcs, _) in enumerate(views):
                    pe.wait_ge(rounded, part + 1)
                    if n >= 4:
                        pe.wait_ge(t_read, n - 3)
                    for i, src in enumerate(srcs):
                        mm = pe.transpose(psT[:, n % 4, i * P:(i + 1) * P], src, core.ident[:, :])
                    mm.then_inc(t_full, 1)

        ctx2, sb2, ps2, sem2 = stage(nc, "f4t")
        with ctx2:
            norm = TokenNorm(core, sb2, sem2, h)
            xn, xq, xT = sb2("xn", [P, D]), sb2("xq", [P, D]), sb2("xT", [P, DC, P])
            gate, hid, hq, hT = sb2("gate", [P, I]), sb2("hid", [P, I]), sb2("hq", [P, IP]), sb2("hT", [P, IC, P])
            fx, fh = Fp4(sb2, "x", D), Fp4(sb2, "h", I)
            psX, psU, psH, psO = ps2("x", [P, 512]), ps2("u", [P, 4, 512]), ps2("h", [P, 2, 512]), ps2("o", [P, 512])
            names = ("xn_ready", "x_mag", "xq_ready", "x_full", "x_read", "gate_full", "up_full", "gate_read", "hid_ready",
                     "h_mag", "hq_ready", "h_full", "h_read", "o_full", "o_added", "padded", "chained")
            (xn_ready, x_mag, xq_ready, x_full, x_read, gate_full, up_full, gate_read, hid_ready,
             h_mag, hq_ready, h_full, h_read, o_full, o_added, padded, chained) = (sem2(n) for n in names)
            banks = lambda a: a.rearrange("p (j n) -> p j n", j=2)
            block = ctx2.enter_context(nc.Block())

            @block.gpsimd
            def _(pool):
                pool.memset(hq[:, I:IP], 0.0).then_inc(padded, 1)
                norm.rsqrt(pool)

            @block.vector
            def _(dve):
                chain = Chain(dve, chained)
                norm.stats(dve)
                dve.wait_ge(norm.rstd_done, 1)
                per_quant = 13

                def front(t, links):
                    norm.normalise(dve, xn[:, :], t).then_inc(xn_ready, 1)
                    dve.wait_ge(x_mag, t + 1)
                    chain.begin(links)
                    fx.steps(dve, chain, xn[:, :], xq[:, :]).then_inc(xq_ready, 1)
                    assert chain.count == per_quant

                def back(t, links):
                    dve.wait_ge(gate_read, t + 1)
                    dve.wait_ge(up_full, t + 1)
                    dve.tensor_tensor(banks(hid[:, :]), banks(gate[:, :]), psU[:, 2:4, 0:HALF], ALU.mult).then_inc(hid_ready, 1)
                    dve.wait_ge(h_mag, t + 1)
                    chain.begin(links)
                    fh.steps(dve, chain, hid[:, :], hq[:, 0:I]).then_inc(hq_ready, 1)
                    dve.wait_ge(o_full, t + 1)
                    dve.tensor_tensor(h[:, t, :], h[:, t, :], psO[:, 0:D], ALU.add).then_inc(o_added, 1)

                front(0, 0)
                with dve.Fori(0, B - 1) as t:
                    front(t + 1, (2 * t + 1) * per_quant)
                    back(t, (2 * t + 2) * per_quant)
                back(B - 1, (2 * B - 1) * per_quant)

            @block.scalar
            def _(act):
                def front(t):
                    act.wait_ge(xn_ready, t + 1)
                    fx.magnitude(act, xn[:, :]).then_inc(x_mag, 1)
                    act.wait_ge(x_full, t + 1)
                    act.copy(xT[:, :, :], psX[:, 0:D].rearrange("p (c t) -> p c t", c=DC)).then_inc(x_read, 1)

                def back(t):
                    act.wait_ge(hid_ready, t + 1)
                    fh.magnitude(act, hid[:, :]).then_inc(h_mag, 1)
                    act.wait_ge(h_full, t + 1)
                    for j in range(2):
                        a = act.copy(hT[:, 3 * j:3 * j + 3, :], psH[:, j, 0:3 * P].rearrange("p (c t) -> p c t", c=3))
                    a.then_inc(h_read, 1)

                def silu(t):
                    act.wait_ge(gate_full, t + 1)
                    act.activation(banks(gate[:, :]), psU[:, 0:2, 0:HALF], ACT.Silu).then_inc(gate_read, 1)

                front(0)
                silu(0)
                with act.Fori(0, B - 1) as t:
                    front(t + 1)
                    back(t)
                    silu(t + 1)
                back(B - 1)

            @block.tensor
            def _(pe):
                def front(t, again=True):
                    pe.wait_ge(xq_ready, t + 1)
                    for c in range(DC):
                        mm = pe.transpose(psX[:, c * P:(c + 1) * P], xq[:, c * P:(c + 1) * P], core.ident[:, :])
                    mm.then_inc(x_full, 1)
                    pe.wait_ge(x_read, t + 1)
                    if again:
                        pe.wait_ge(hid_ready, t)
                    for side, full in ((0, gate_full), (1, up_full)):
                        for j in range(2):
                            for c in range(DC):
                                mm = pe.matmul(psU[:, 2 * side + j, 0:HALF], xT[:, c, :],
                                               wT[:, c, side * IP + j * HALF:side * IP + (j + 1) * HALF], start=c == 0, stop=c == DC - 1)
                        mm.then_inc(full, 1)

                def back(t):
                    pe.wait_ge(hq_ready, t + 1)
                    for j in range(IC):
                        mm = pe.transpose(psH[:, j // 3, (j % 3) * P:(j % 3 + 1) * P], hq[:, j * P:(j + 1) * P], core.ident[:, :])
                    mm.then_inc(h_full, 1)
                    pe.wait_ge(h_read, t + 1)
                    if not isinstance(t, int) or t > 0:
                        pe.wait_ge(o_added, t)
                    for j in range(IC):
                        mm = pe.matmul(psO[:, 0:D], hT[:, j, :], dT[:, j, :], start=j == 0, stop=j == IC - 1)
                    mm.then_inc(o_full, 1)

                pe.wait_ge(padded, 1)
                front(0, False)
                with pe.Fori(0, B - 1) as t:
                    front(t + 1)
                    back(t)
                back(B - 1)


def layer2_block(core):
    with core.nc.sbuf_tensor("x0", [P, B, D], F32) as x0:
        delta_net(core, x0)
        ffn(core, "dense", src=x0)


def lm_tower(nc, ins, out):
    core = Core(nc, ins, out)
    ctx = ExitStack()
    with ctx:
        core.h = ctx.enter_context(nc.sbuf_tensor("h", [P, B, D], F32))
        core.ident = ctx.enter_context(nc.sbuf_tensor("ident", [P, P], F32))
        core.ident_bf = ctx.enter_context(nc.sbuf_tensor("ident_bf", [P, P], BF16))
        core.causal = ctx.enter_context(nc.sbuf_tensor("causal", [P, 4 * P], BF16))
        core.ones = ctx.enter_context(nc.sbuf_tensor("ones", [P, P], F32))
        core.minus_half = ctx.enter_context(nc.sbuf_tensor("minus_half", [P, 2 * B], F32))
        stages = [lambda: embed(core), lambda: attention(core, "headnorm"), lambda: ffn(core, "swiglu"), lambda: attention(core, "nd"),
                  lambda: ffn(core, "gelu"), lambda: layer2_block(core), lambda: fp4_ffn(core), lambda: attention(core, "rel"), lambda: ffn(core, "silu")]
        for run in stages:
            run()
        done = ctx.enter_context(nc.semaphore("out_done"))
        block = ctx.enter_context(nc.Block())

        @block.sync
        def _(sp):
            sp.dma_start(out.rearrange("b t d -> t b d"), core.h[:, :, :]).then_inc(done, 16)
            sp.wait_ge(done, 16)


def layouts(inputs):
    a = {k: np.ascontiguousarray(v) for k, v in inputs.items()}
    a["token_ids"] = np.ascontiguousarray(a.pop("x").T)
    a["ident"] = np.eye(P, dtype=np.float32)
    tri = np.where(np.arange(P)[:, None] >= np.arange(P)[None, :], 0.0, -1e30).astype(np.float32)
    a["causal"] = np.tile(tri, (1, 4))
    a["masked"] = np.full((16, P), -1e9, np.float32)

    def strips(w, width, strip):
        w = w.reshape(w.shape[0], -1, width)
        o = np.zeros((*w.shape[:2], strip), w.dtype)
        o[:, :, :width] = w
        return o.reshape(w.shape[0], -1)

    def by_partition(v, n):
        return np.ascontiguousarray(v.reshape(n, P).T)

    for s in ("q", "k"):
        a[f"L3_attn_W{s}_strips"] = strips(a.pop(f"L3_attn_W{s}"), 16, 32)
        a[f"L3_attn_b{s}_strips"] = by_partition(strips(a.pop(f"L3_attn_b{s}")[None], 16, 32), 4)
    a["L1_attn_Wq_strips"] = a.pop("L1_attn_Wq")
    a["L1_attn_Wk_strips"] = a.pop("L1_attn_Wk")
    a["L1_attn_bq_strips"] = by_partition(a.pop("L1_attn_bq"), 8)
    order = [8 * (s // 2) + 2 * c + s % 2 for c in range(4) for s in range(4)]
    for n in ("Wr", "br"):
        w = a.pop(f"L1_attn_{n}").reshape(-1, 16, 10)[:, order].reshape(-1, 160)
        a[f"L1_attn_{n}_strips"] = strips(w, 10, 32)
    a["L1_attn_br_strips"] = by_partition(a["L1_attn_br_strips"], 4)
    d = np.zeros((P, P), np.float32)
    rel = np.zeros((P, 2 * P), np.float32)
    b_nd, emb = a.pop("L1_attn_b_nd"), a.pop("L3_attn_rel_emb")
    mid = emb.shape[0] // 2
    for s in range(4):
        d[32 * s:32 * s + 10] = b_nd[:, 0:P][:, ::-1]
        rel[32 * s:32 * s + 16, 0:2 * P - 1] = emb[mid - P + 1:mid + P][::-1].T
    a["L1_attn_dist"], a["L3_attn_dist"] = d, rel

    def chunked_bias(v, n):
        return np.ascontiguousarray(v.reshape(v.shape[0], n, P).transpose(0, 2, 1))

    a["f0_w1"], a["f0_w2"] = a.pop("L0_ffn_gate_up_proj"), a.pop("L0_ffn_down_proj")
    a["f0_b1"], a["f0_b2"] = chunked_bias(a.pop("L0_ffn_gate_up_bias"), 4), a.pop("L0_ffn_down_bias")
    a["f0_wr"], a["f0_rb"] = np.ascontiguousarray(a.pop("L0_ffn_router_weight").T), a.pop("L0_ffn_router_bias")
    a["f1_w1"], a["f1_w2"] = a.pop("L1_ffn_W1"), a.pop("L1_ffn_W2")
    a["f1_b1"], a["f1_b2"] = chunked_bias(a.pop("L1_ffn_b1"), 8), a.pop("L1_ffn_b2")
    a["f1_wr"], a["f1_rb"] = a.pop("L1_ffn_Wr"), a.pop("L1_ffn_br")
    a["f2_w1"] = np.ascontiguousarray(a.pop("L2_attn_w1").reshape(D, 2, 512).transpose(1, 0, 2))
    a["f2_w2"], a["f2_b1"] = a.pop("L2_attn_w2").reshape(2, 512, D), chunked_bias(a.pop("L2_attn_b1").reshape(2, 512), 4)
    a["f2_ln1_g"], a["f2_ln1_b"] = by_partition(a.pop("L2_attn_ln1_g"), 2), by_partition(a.pop("L2_attn_ln1_b"), 2)
    pad = 6 * P - 704
    for n in ("gate", "up"):
        a[f"f4_{n}"] = np.pad(a.pop(f"L2_ffn_w_{n}"), ((0, pad), (0, 0)))
    a["f4_down"] = np.pad(a.pop("L2_ffn_w_down"), ((0, 0), (0, pad)))
    a["f2_b2"] = a.pop("L2_attn_b2")[None]
    a["f2_g"], a["f2_b"] = by_partition(a.pop("L2_attn_ln2_g"), 2), by_partition(a.pop("L2_attn_ln2_b"), 2)
    I3 = 352
    side = {}
    for n in ("gate", "up"):
        side[n] = np.concatenate([a.pop(f"L3_ffn_{n}_proj"), a.pop(f"L3_ffn_shared_{n}_w").reshape(2, I3, D)])
    a["f3_w1"] = np.concatenate([side["gate"].transpose(0, 2, 1), side["up"].transpose(0, 2, 1)], axis=2)
    down = np.concatenate([a.pop("L3_ffn_down_proj").transpose(0, 2, 1), a.pop("L3_ffn_shared_down_w").T.reshape(2, I3, D)])
    a["f3_w2"] = np.concatenate([down, np.zeros((18, 3 * P - I3, D), down.dtype)], axis=1)
    a["f3_wr"], a["f3_rb"] = np.ascontiguousarray(a.pop("L3_ffn_gate_w").T), a.pop("L3_ffn_gate_bias")
    for n in (4, 8, 16):
        a[f"rank{n}"] = np.tile(np.arange(n, 0, -1, dtype=np.float32), 1 if n == 4 else B)
    return a


def kernel(**inputs):
    from concourse import bacc
    from concourse.bass_utils import run_bass_kernel_spmd

    nc = bacc.Bacc("TRN2", target_bir_lowering=False, num_devices=1)
    arrays, ins = {}, {}
    for name, v in layouts(inputs).items():
        arrays["in_" + name] = v
        ins[name] = nc.dram_tensor("in_" + name, v.shape, mybir.dt.from_np(v.dtype), kind="ExternalInput").ap()
    out = nc.dram_tensor("out_0_dram", (B, P, D), F32, kind="ExternalOutput").ap()
    lm_tower(nc, ins, out)
    r = run_bass_kernel_spmd(nc, [arrays], core_ids=[0])
    return r.results[0]["out_0_dram"]
```

```python
from contextlib import ExitStack

import numpy as np

import concourse.bass as bass
import concourse.mybir as mybir

F32 = mybir.dt.float32
BF16 = mybir.dt.bfloat16
I32 = mybir.dt.int32
U32 = mybir.dt.uint32
ALU = mybir.AluOpType
ACT = mybir.ActivationFunctionType
AX = mybir.AxisListType

P = 128
B = 16
D = 256
DC = D // P
LN_EPS = 1e-5


class Core:

    def __init__(self, nc, ins, out):
        self.nc, self.ins, self.out = nc, ins, out


class Chain:

    def __init__(self, eng, sem):
        self.eng, self.sem, self.base, self.count = eng, sem, 0, 0

    def begin(self, base):
        self.base, self.count = base, 0

    def step(self, ins):
        ins.then_inc(self.sem, 1)
        self.count += 1
        self.eng.wait_ge(self.sem, self.base + self.count)


def stage(nc, name):
    ctx = ExitStack()
    sems = []

    def clear():
        if sems:
            nc.clear_and_free_semaphores(sems)
            nc.all_engine_barrier()

    ctx.callback(clear)

    def sb(label, shape, dt=F32):
        return ctx.enter_context(nc.sbuf_tensor(f"{name}_{label}", shape, dt))

    def ps(label, shape, dt=F32):
        return ctx.enter_context(nc.psum_tensor(f"{name}_{label}", shape, dt))

    def sem(label):
        sems.append(nc.alloc_semaphore(name=f"{name}_{label}"))
        return sems[-1]

    return ctx, sb, ps, sem


def embed(core):
    nc, ins = core.nc, core.ins
    ctx, sb, ps, sem = stage(nc, "embed")
    with ctx:
        ids = sb("ids", [P, B], I32)
        causal = sb("causal", [P, 4 * P])
        ids_in, rows_in, consts_in, zeroed = sem("ids_in"), sem("rows_in"), sem("consts_in"), sem("zeroed")
        block = ctx.enter_context(nc.Block())

        @block.sync
        def _(sp):
            sp.dma_start(ids[:, :], ins["token_ids"]).then_inc(ids_in, 16)
            sp.dma_start(core.ident[:, :], ins["ident"]).then_inc(consts_in, 16)
            sp.dma_start(causal[:, :], ins["causal"]).then_inc(consts_in, 16)
            sp.wait_ge(consts_in, 32)
            sp.wait_ge(zeroed, 1)
            sp.wait_ge(rows_in, 16 * B)
            rows = core.slot_rows.ap().rearrange("(n p) d -> p n d", p=P)
            sp.dma_start(rows, core.zeros[:, :].unsqueeze(1).to_broadcast([P, rows.shape[1], D])).then_inc(core.rows_cleared, 16)

        @block.gpsimd
        def _(pool):
            pool.memset(core.minus_half[:, :], -0.5)
            pool.memset(core.ones[:, :], 1.0)
            pool.memset(core.zeros[:, :], 0.0).then_inc(zeroed, 1)
            pool.wait_ge(ids_in, 16)
            for b in range(B):
                pool.indirect_dma_start(
                    out=core.h[:, b, :], out_offset=None, in_=ins["L0_tok_weight"],
                    in_offset=bass.IndirectOffsetOnAxis(ap=ids[:, b:b + 1].bitcast(U32), axis=0),
                ).then_inc(rows_in, 16)
            pool.wait_ge(rows_in, 16 * B)

        @block.vector
        def _(dve):
            dve.wait_ge(consts_in, 32)
            dve.tensor_copy(core.ident_bf[:, :], core.ident[:, :])
            dve.tensor_copy(core.causal[:, :], causal[:, :])
            dve.memset(core.ones_bf[:, :], 1.0)


class TokenNorm:

    def __init__(self, core, sb, sem, src):
        self.core, self.src = core, src
        self.parts = sb("ln_parts", [P, B, 6])
        self.mv = sb("ln_mv", [P, B, 2])
        self.rstd = sb("ln_rstd", [P, B, 1])
        self.parts_done, self.var_done, self.rstd_done = sem("ln_parts"), sem("ln_var"), sem("ln_rstd")

    def stats(self, dve):
        for b in range(B):
            dve.bn_stats(self.parts[:, b, :], self.src[:, b, :]).then_inc(self.parts_done, 1)
        dve.wait_ge(self.parts_done, B)
        for b in range(B):
            dve.bn_aggr(self.mv[:, b, :], self.parts[:, b, :]).then_inc(self.var_done, 1)
        dve.wait_ge(self.var_done, B)
        dve.tensor_scalar(self.rstd[:, :, 0], self.mv[:, :, 1], LN_EPS, None, ALU.add).then_inc(self.var_done, 1)

    def rsqrt(self, pool):
        pool.wait_ge(self.var_done, B + 1)
        pool.tensor_tensor(self.rstd[:, :, 0], self.rstd[:, :, 0], self.core.minus_half[:, 0:B], ALU.pow).then_inc(self.rstd_done, 1)

    def normalise(self, dve, out, b):
        return dve.tensor_scalar(out, self.src[:, b, :], self.mv[:, b, 0:1], self.rstd[:, b, :], ALU.subtract, ALU.mult)


def bias_row(core, sb, name):
    return sb(name, [1, D])


def attention(core, kind, q_name=None):
    nc, ins, h = core.nc, core.ins, core.h
    H = 16
    dh = 64 if kind == "nd" else 16
    strip = 64 if kind == "nd" else 32
    per = P // strip
    QC = H // per
    F = H * dh
    FC = F // P
    pre = {"headnorm": "L0_attn_", "nd": "L1_attn_", "rel": "L3_attn_"}[kind]
    nm = {"headnorm": "a0", "nd": "a1", "rel": "a3"}[kind]
    skewed = kind != "headnorm"
    GW = {"headnorm": 0, "nd": P, "rel": 2 * P}[kind]
    PITCH = 2 * P

    def place(head):
        c, s = head // per, head % per
        if kind == "nd":
            return 2 * (c // 4) + s, c % 4, s * strip, c
        return s, c, s * strip, c

    heads_of = {}
    for head in range(H):
        beta, slot, _, _ = place(head)
        heads_of[beta, slot] = head

    if kind == "headnorm":
        jobs = [("x", "act"), ("qk", "dve"), ("q", "act"), ("k", "act"), ("v", "act")]
    elif kind == "nd":
        jobs = [("x", "act"), ("q0", "act"), ("q1", "act"), ("k0", "act"), ("k1", "act"), ("r", "act")]
        jobs += [(f"g{i}", "act") for i in range(H * GW // 512)]
        jobs += [("v0", "act"), ("v1", "act")]
    else:
        jobs = [("x", "act"), ("q", "act"), ("k", "act")] + [(f"g{i}", "act") for i in range(H * GW // 512)]
        jobs += [("v", "act")]
    NF = len(jobs)
    names = [j[0] for j in jobs]
    NA = sum(j[1] == "act" for j in jobs)

    bank_of = {name: j % 2 for j, name in enumerate(names)}

    per_o = 512 // (dh + 1)
    o_jobs = [list(range(a, min(a + per_o, H))) for a in range(0, H, per_o)]
    t_jobs = [list(range(a, min(a + 4, FC))) for a in range(0, FC, 4)]
    NBK = len(o_jobs) + len(t_jobs) + 1

    ctx, sb, ps, sem = stage(nc, nm)
    with ctx:
        norm = TokenNorm(core, sb, sem, h)
        xn = sb("xn", [P, D])
        xT = sb("xT", [P, DC, P])
        qT = sb("qT", [P, QC, P])
        kT = sb("kT", [P, QC, P])
        va = sb("va", [P, H, dh + 1])
        prob = sb("prob", [P, 4, 512])
        probT = sb("probT", [P, 4, 512])
        top = sb("top", [P, H])
        inv = sb("inv", [P, H])
        o = sb("o", [P, F])
        oT = sb("oT", [P, FC, P])
        wo = sb("wo", [P, FC, D])
        bo = sb("bo", [1, D])
        wv = sb("wv", [P, DC, F])
        psS = ps("scores", [P, 4, 512])
        psF = ps("front", [P, 2, 512])
        psB = ps("back", [P, 2, 512])
        weights_in = sem("weights_in")
        xn_ready = sem("xn_ready")
        front_full = sem("front_full")
        front_act = sem("front_act")
        back_full = sem("back_full")
        back_read = sem("back_read")
        scores_full = sem("scores_full")
        shifted = sem("shifted")
        expd = sem("expd")
        probT_full = sem("probT_full")
        probT_read = sem("probT_read")
        ones_set = sem("ones_set")
        dve_chain = sem("dve_chain")
        n_weights = 3
        if kind == "headnorm":
            wqk = sb("wqk", [P, DC, 2 * F])
            qk = sb("qk", [P, 2 * H, 2 * dh])
            hsum = sb("hsum", [P, 2 * H])
            hvar = sb("hvar", [P, 2 * H])
            cen = sb("cen", [P, 2 * H, dh])
            sq = sb("sq", [P, 2 * H, dh])
            hw = sb("hw", [P, 2, dh])
            hb = sb("hb", [P, 2, dh])
            hv_done, hr_done, qk_ready = sem("hv_done"), sem("hr_done"), sem("qk_ready")
            n_weights += 5
        else:
            wq = sb("wq", [P, DC, QC * P])
            wk = sb("wk", [P, DC, QC * P])
            bq = sb("bq", [P, QC])
            g_sb = sb("g", [P, H, GW])
            e_sb = sb("e", [P, 4, 4, P])
            skew = nc.dram_tensor(f"{nm}_skew", [P, H, PITCH], F32, kind="Internal").ap()
            skew_read = bass.AP(skew.tensor, P - 1, [[H * PITCH - 1, P], [PITCH, H], [1, P]])
            g_out, e_in, g_set = sem("g_out"), sem("e_in"), sem("g_set")
            g_ready = front_act
            n_weights += 3
            dist = sb("dist", [P, GW])
            n_weights += 1
            if kind == "nd":
                wr = sb("wr", [P, DC, 4 * P])
                br = sb("br", [P, 4])
                rT = sb("rT", [P, 4, P])
                n_weights += 3
            else:
                bk = sb("bk", [P, QC])
                bv = sb("bv", [1, F])
                n_weights += 2

        block = ctx.enter_context(nc.Block())

        @block.sync
        def _(sp):
            n = 0

            def load(dst, src):
                nonlocal n
                n += 1
                sp.dma_start(dst, src).then_inc(weights_in, 16)

            def chunks(src):
                return src.rearrange("(c p) n -> p c n", p=P)

            load(wv[:, :, :], chunks(ins[pre + "Wv"]))
            load(wo[:, :, :], chunks(ins[pre + ("Wproj" if kind == "nd" else "Wo")]))
            load(bo[:, :], ins[pre + ("bproj" if kind == "nd" else "bo")].unsqueeze(0))
            if kind == "headnorm":
                load(wqk[:, :, 0:F], chunks(ins[pre + "Wq"]))
                load(wqk[:, :, F:2 * F], chunks(ins[pre + "Wk"]))
                for i, side in enumerate("qk"):
                    load(hw[:, i, :], ins[f"{pre}{side}ln_w"].partition_broadcast(P))
                load(hb[:, 0, :], ins[f"{pre}qln_b"].partition_broadcast(P))
                load(hb[:, 1, :], ins[f"{pre}kln_b"].partition_broadcast(P))
                n_load = n
            else:
                load(wq[:, :, :], chunks(ins[pre + "Wq_strips"]))
                load(wk[:, :, :], chunks(ins[pre + "Wk_strips"]))
                load(bq[:, :], ins[pre + "bq_strips"])
                load(dist[:, :], ins[pre + "dist"])
                if kind == "nd":
                    load(wr[:, :, :], chunks(ins[pre + "Wr_strips"]))
                    load(br[:, :], ins[pre + "br_strips"])
                    load(skew[:, :, P:PITCH], ins["masked"].partition_broadcast(P))
                else:
                    load(bk[:, :], ins[pre + "bk_strips"])
                    load(bv[:, :], ins[pre + "bv"].unsqueeze(0))
            core.n_weights = n
            if skewed:
                last_g = names.index(f"g{H * GW // 512 - 1}")
                def skewing(t):
                    if isinstance(t, int):
                        tables, loads = t * NA + last_g + 1, 16 * t + 16
                    else:
                        tables, loads = sp.to_reg(t * NA + last_g + 1), sp.to_reg(16 * t + 16)
                        previous, read = sp.to_reg(4 * t), sp.to_reg(16 * t)
                        sp.wait_ge(e_in, read)
                        sp.wait_ge(shifted, previous)
                    sp.wait_ge(front_act, tables)
                    sp.dma_start(skew[:, :, 0:GW], g_sb[:, :, :]).then_inc(g_out, 16)
                    sp.wait_ge(g_out, loads)
                    if isinstance(t, int):
                        sp.wait_ge(weights_in, 16 * n)
                    sp.dma_start(e_sb[:, :, :, :].rearrange("p b a k -> p (b a) k"), skew_read).then_inc(e_in, 16)

                skewing(0)
                with sp.Fori(1, B) as t:
                    skewing(t)
                sp.wait_ge(e_in, 16 * B)

        n_weights = core.n_weights

        @block.gpsimd
        def _(pool):
            pool.memset(va[:, :, dh:dh + 1], 1.0).then_inc(ones_set, 1)
            if kind == "headnorm":
                pool.memset(qk[:, :, :], 0.0).then_inc(ones_set, 1)
            norm.rsqrt(pool)
            if kind == "headnorm":
                def head_rsqrt(t):
                    pool.wait_ge(hv_done, t + 1)
                    pool.tensor_tensor(hvar[:, :], hvar[:, :], core.minus_half[:, 0:2 * H], ALU.pow).then_inc(hr_done, 1)

                with pool.Fori(0, B) as t:
                    head_rsqrt(t)

        @block.scalar
        def _(act):
            na = 0

            def front_read(t, name, out, **kw):
                j = names.index(name)
                act.wait_ge(front_full, t * NF + j + 1)
                return psF[:, bank_of[name], :]

            def done(i):
                i.then_inc(front_act, 1)

            def copy_x(t):
                src = front_read(t, "x", None)
                done(act.copy(xT[:, :, :], src[:, 0:D].rearrange("p (c t) -> p c t", c=DC)))

            def copy_v(t):
                if kind == "nd":
                    for i in range(2):
                        src = front_read(t, f"v{i}", None)
                        done(act.copy(va[:, 8 * i:8 * i + 8, 0:dh], src.rearrange("p (a d) -> p a d", d=dh)))
                else:
                    src = front_read(t, "v", None)
                    done(act.copy(va[:, :, 0:dh], src[:, 0:F].rearrange("p (a d) -> p a d", d=dh)))

            def copy_qk(t):
                if kind == "headnorm":
                    for name, dst in (("q", qT), ("k", kT)):
                        src = front_read(t, name, None)
                        done(act.copy(dst[:, :, :], src.rearrange("p (c t) -> p c t", c=4)))
                    return
                for side, dst in (("q", qT), ("k", kT)):
                    n = QC // 4
                    for i in range(n):
                        src = front_read(t, side if n == 1 else f"{side}{i}", None)
                        for c in range(4):
                            b = bq if side == "q" else (bk if kind == "rel" else None)
                            if b is None:
                                if c == 0:
                                    done(act.copy(dst[:, 4 * i:4 * i + 4, :], src.rearrange("p (c t) -> p c t", c=4)))
                            else:
                                ins_ = act.activation(dst[:, 4 * i + c, :], src[:, c * P:(c + 1) * P], ACT.Identity,
                                                      bias=b[:, 4 * i + c:4 * i + c + 1])
                                if c == 3:
                                    done(ins_)
                if kind == "nd":
                    src = front_read(t, "r", None)
                    for c in range(4):
                        ins_ = act.activation(rT[:, c, :], src[:, c * P:(c + 1) * P], ACT.Identity, bias=br[:, c:c + 1])
                    done(ins_)

            def copy_g(t):
                hp = 512 // GW
                for i in range(H // hp):
                    if i == 0 and (not isinstance(t, int) or t > 0):
                        act.wait_ge(g_out, 16 * t)
                    src = front_read(t, f"g{i}", None)
                    done(act.copy(g_sb[:, hp * i:hp * i + hp, :], src.rearrange("p (a d) -> p a d", d=GW)))

            def exp(t):
                for beta in range(4):
                    act.wait_ge(shifted, 4 * t + beta + 1)
                    act.activation(prob[:, beta, :], prob[:, beta, :], ACT.Exp,
                                   scale=1.0 if skewed else float(dh) ** -0.5).then_inc(expd, 1)

            def copy_pT(t):
                for beta in range(4):
                    act.wait_ge(probT_full, 4 * t + beta + 1)
                    act.copy(probT[:, beta, :], psS[:, beta, :]).then_inc(probT_read, 1)

            def front(t):
                copy_x(t)
                if skewed:
                    copy_qk(t)
                    copy_g(t)

            act.wait_ge(weights_in, 16 * n_weights)
            act.wait_ge(ones_set, 1 + (kind == "headnorm"))
            front(0)
            if not skewed:
                copy_qk(0)
            copy_v(0)
            with act.Fori(0, B - 1) as t:
                front(t + 1)
                exp(t)
                copy_pT(t)
                if not skewed:
                    copy_qk(t + 1)
                copy_v(t + 1)
            exp(B - 1)
            copy_pT(B - 1)

        @block.tensor
        def _(pe):
            def front_bank(t, name):
                j = names.index(name)
                bank = bank_of[name]
                prior = [i for i in range(j) if bank_of[names[i]] == bank]
                tt = t
                if not prior:
                    if isinstance(t, int) and t == 0:
                        return psF[:, bank, :]
                    prior = [i for i in range(NF) if bank_of[names[i]] == bank]
                    tt = t - 1
                p = prior[-1]
                if jobs[p][1] == "act":
                    n = sum(jobs[i][1] == "act" for i in range(p + 1))
                    pe.wait_ge(front_act, tt * NA + n)
                else:
                    pe.wait_ge(qk_ready, tt + 1)
                return psF[:, bank, :]

            def evacuated(t, name):
                j = names.index(name)
                n = sum(jobs[i][1] == "act" for i in range(j + 1))
                pe.wait_ge(front_act, t * NA + n)

            def front_x(t):
                bank = front_bank(t, "x")
                pe.wait_ge(xn_ready, t + 1)
                for c in range(DC):
                    mm = pe.transpose(bank[:, c * P:(c + 1) * P], xn[:, c * P:(c + 1) * P], core.ident[:, :])
                mm.then_inc(front_full, 1)

            def front_qk(t):
                evacuated(t, "x")
                if kind == "headnorm":
                    bank = front_bank(t, "qk")
                    for c in range(DC):
                        mm = pe.matmul(bank, xT[:, c, :], wqk[:, c, :], start=c == 0, stop=c == DC - 1)
                    mm.then_inc(front_full, 1)
                    return
                todo = [("q", wq, QC // 4), ("k", wk, QC // 4)] + ([("r", wr, 1)] if kind == "nd" else [])
                for side, w, n in todo:
                    for i in range(n):
                        bank = front_bank(t, side if n == 1 else f"{side}{i}")
                        for m in range(4):
                            for c in range(DC):
                                mm = pe.matmul(bank[:, m * P:(m + 1) * P], w[:, c, (4 * i + m) * P:(4 * i + m + 1) * P],
                                               xT[:, c, :], start=c == 0, stop=c == DC - 1)
                        mm.then_inc(front_full, 1)

            def front_g(t):
                hp = 512 // GW
                evacuated(t, "r" if kind == "nd" else "q")
                for i in range(H // hp):
                    bank = front_bank(t, f"g{i}")
                    for a in range(hp):
                        s, c = (hp * i + a) // 4, (hp * i + a) % 4
                        lhs = (rT if kind == "nd" else qT)[32 * s:32 * s + 16, c, :]
                        mm = pe.matmul(bank[:, a * GW:(a + 1) * GW], lhs, dist[32 * s:32 * s + 16, :], start=True, stop=True)
                    mm.then_inc(front_full, 1)

            def front_qkT(t):
                pe.wait_ge(qk_ready, t + 1)
                for i, name in enumerate(("q", "k")):
                    bank = front_bank(t, name)
                    for c in range(4):
                        src = qk[:, i * H + 4 * c:i * H + 4 * c + 4, :].rearrange("p a d -> p (a d)")
                        mm = pe.transpose(bank[:, c * P:(c + 1) * P], src, core.ident[:, :])
                    mm.then_inc(front_full, 1)

            def front_v(t):
                n = 2 if kind == "nd" else 1
                w = F // n
                for i in range(n):
                    bank = front_bank(t, "v" if n == 1 else f"v{i}")
                    for c in range(DC):
                        mm = pe.matmul(bank[:, 0:w], xT[:, c, :], wv[:, c, i * w:(i + 1) * w], start=c == 0,
                                       stop=c == DC - 1 and kind != "rel")
                    if kind == "rel":
                        mm = pe.matmul(bank[:, 0:w], core.ones[0:1, :], bv[:, :], start=False, stop=True)
                    mm.then_inc(front_full, 1)

            def scores(t):
                evacuated(t, names[NF - 1])
                if not isinstance(t, int) or t > 0:
                    pe.wait_ge(probT_read, 4 * t)
                for beta in range(4):
                    if kind == "headnorm":
                        pe.matmul(psS[:, beta, :], core.ident_bf[:, :], core.causal[:, :], start=True, stop=False)
                    for slot in range(4):
                        head = heads_of[beta, slot]
                        _, _, s0, c = place(head)
                        mm = pe.matmul(psS[:, beta, slot * P:(slot + 1) * P], qT[s0:s0 + dh, c, :], kT[s0:s0 + dh, c, :],
                                       start=kind != "headnorm", stop=slot == 3 or kind != "headnorm")
                    mm.then_inc(scores_full, 1)

            def weightsT(t):
                for beta in range(4):
                    pe.wait_ge(expd, 4 * t + beta + 1)
                    for slot in range(4):
                        mm = pe.transpose(psS[:, beta, slot * P:(slot + 1) * P], prob[:, beta, slot * P:(slot + 1) * P],
                                          core.ident[:, :])
                    mm.then_inc(probT_full, 1)

            def back_bank(t, j):
                if j >= 2:
                    pe.wait_ge(back_read, t * NBK + j - 1)
                elif not isinstance(t, int) or t > 0:
                    pe.wait_ge(back_read, t * NBK)
                return psB[:, j % 2, :]

            def values(t):
                for n, hs in enumerate(o_jobs):
                    bank = back_bank(t, n)
                    for i, head in enumerate(hs):
                        beta, slot, _, _ = place(head)
                        if n == 0 and i == 0:
                            pe.wait_ge(probT_read, 4 * t + 4)
                        mm = pe.matmul(bank[:, i * (dh + 1):(i + 1) * (dh + 1)], probT[:, beta, slot * P:(slot + 1) * P],
                                       va[:, head, :], start=True, stop=True)
                    mm.then_inc(back_full, 1)

            def project(t):
                for n, cs in enumerate(t_jobs):
                    j = len(o_jobs) + n
                    bank = back_bank(t, j)
                    pe.wait_ge(back_read, t * NBK + len(o_jobs))
                    for i, c in enumerate(cs):
                        mm = pe.transpose(bank[:, i * P:(i + 1) * P], o[:, c * P:(c + 1) * P], core.ident[:, :])
                    mm.then_inc(back_full, 1)
                bank = back_bank(t, NBK - 1)
                pe.wait_ge(back_read, t * NBK + NBK - 1)
                pe.matmul(bank[:, 0:D], core.ones[0:1, :], bo[:, :], start=True, stop=False)
                for c in range(FC):
                    mm = pe.matmul(bank[:, 0:D], oT[:, c, :], wo[:, c, :], start=False, stop=c == FC - 1)
                mm.then_inc(back_full, 1)

            def front(t):
                front_x(t)
                front_qk(t)
                if skewed:
                    front_g(t)

            pe.wait_ge(weights_in, 16 * n_weights)
            front(0)
            if not skewed:
                front_qkT(0)
            front_v(0)
            with pe.Fori(0, B - 1) as t:
                scores(t)
                front(t + 1)
                weightsT(t)
                values(t)
                if not skewed:
                    front_qkT(t + 1)
                front_v(t + 1)
                project(t)
            scores(B - 1)
            weightsT(B - 1)
            values(B - 1)
            project(B - 1)

        @block.vector
        def _(dve):
            chain = Chain(dve, dve_chain)
            norm.stats(dve)
            if kind == "headnorm":
                dve.wait_ge(ones_set, 2)
                dve.wait_ge(weights_in, 16 * n_weights)

            def normal(t):
                norm.normalise(dve, xn[:, :], t).then_inc(xn_ready, 1)

            def head_norm(t):
                dve.wait_ge(front_full, t * NF + 2)
                src = psF[:, 1, :].rearrange("p (a d) -> p a d", d=dh)
                chain.step(dve.tensor_reduce(hsum[:, :], src, AX.X, ALU.add))
                chain.step(dve.tensor_scalar(hsum[:, :], hsum[:, :], 1.0 / dh, None, ALU.mult))
                chain.step(dve.tensor_tensor(cen[:, :, :], src, hsum[:, :].unsqueeze(2).to_broadcast([P, 2 * H, dh]), ALU.subtract))
                chain.step(dve.tensor_tensor(sq[:, :, :], cen[:, :, :], cen[:, :, :], ALU.mult))
                chain.step(dve.tensor_reduce(hvar[:, :], sq[:, :, :], AX.X, ALU.add))
                dve.tensor_scalar(hvar[:, :], hvar[:, :], 1.0 / dh, LN_EPS, ALU.mult, ALU.add).then_inc(hv_done, 1)
                dve.wait_ge(hr_done, t + 1)
                chain.step(dve.tensor_tensor(cen[:, :, :], cen[:, :, :], hvar[:, :].unsqueeze(2).to_broadcast([P, 2 * H, dh]), ALU.mult))
                for i in range(2):
                    c2 = cen[:, i * H:(i + 1) * H, :]
                    ins_ = dve.tensor_tensor(sq[:, i * H:(i + 1) * H, :], c2, hw[:, i:i + 1, :].to_broadcast([P, H, dh]), ALU.mult)
                chain.step(ins_)
                for i in range(2):
                    ins_ = dve.tensor_tensor(qk[:, i * H:(i + 1) * H, 0:dh], sq[:, i * H:(i + 1) * H, :],
                                             hb[:, i:i + 1, :].to_broadcast([P, H, dh]), ALU.add)
                ins_.then_inc(qk_ready, 1)

            def shift(t):
                for beta in range(4):
                    dve.wait_ge(scores_full, 4 * t + beta + 1)
                    if beta == 0 and skewed:
                        dve.wait_ge(e_in, 16 * (t + 1))
                    src = psS[:, beta, :].rearrange("p (a k) -> p a k", k=P)
                    dst = prob[:, beta, :].rearrange("p (a k) -> p a k", k=P)
                    tp = top[:, 4 * beta:4 * beta + 4]
                    if skewed:
                        scale = float(dh) ** -0.5
                        chain.step(dve.scalar_tensor_tensor(out=dst, in0=src, scalar=scale, in1=e_sb[:, beta, :, :],
                                                            op0=ALU.mult, op1=ALU.add))
                        src = dst
                    chain.step(dve.tensor_reduce(tp, src, AX.X, ALU.max))
                    dve.tensor_tensor(dst, src, tp.unsqueeze(2).to_broadcast([P, 4, P]), ALU.subtract).then_inc(shifted, 1)

            def back(t):
                for n, hs in enumerate(o_jobs):
                    dve.wait_ge(back_full, t * NBK + n + 1)
                    src = psB[:, n % 2, 0:len(hs) * (dh + 1)].rearrange("p (a d) -> p a d", d=dh + 1)
                    iv = inv[:, hs[0]:hs[-1] + 1]
                    chain.step(dve.reciprocal(iv, src[:, :, dh]))
                    dve.tensor_tensor(o[:, hs[0] * dh:(hs[-1] + 1) * dh].rearrange("p (a d) -> p a d", d=dh),
                                      src[:, :, 0:dh], iv.unsqueeze(2).to_broadcast([P, len(hs), dh]),
                                      ALU.mult).then_inc(back_read, 1)
                for n, cs in enumerate(t_jobs):
                    j = len(o_jobs) + n
                    dve.wait_ge(back_full, t * NBK + j + 1)
                    dve.tensor_copy(oT[:, cs[0]:cs[-1] + 1, :],
                                    psB[:, j % 2, 0:len(cs) * P].rearrange("p (a d) -> p a d", d=P)).then_inc(back_read, 1)
                dve.wait_ge(back_full, t * NBK + NBK)
                dve.tensor_tensor(h[:, t, :], h[:, t, :], psB[:, (NBK - 1) % 2, 0:D], ALU.add).then_inc(back_read, 1)

            dve.wait_ge(norm.rstd_done, 1)
            normal(0)
            if not skewed:
                head_norm(0)
            first = chain.count
            steps = {"headnorm": 4 + 7 + 1, "nd": 8 + 3, "rel": 8 + 1}[kind]
            with dve.Fori(0, B - 1) as t:
                chain.begin(t * steps + first)
                dve.wait_ge(scores_full, 4 * t + 1)
                normal(t + 1)
                shift(t)
                if not skewed:
                    head_norm(t + 1)
                back(t)
                assert chain.count == steps
            chain.begin(first + (B - 1) * steps)
            shift(B - 1)
            back(B - 1)


def pick_first(dve, chain, score, best, mask, tmp, rank, groups, n):
    wide = [P, groups, n]
    chain.step(dve.tensor_reduce(best, score, AX.X, ALU.max))
    chain.step(dve.tensor_tensor(tmp, score, best.unsqueeze(2).to_broadcast(wide), ALU.is_equal))
    chain.step(dve.tensor_tensor(tmp, tmp, rank, ALU.mult))
    chain.step(dve.tensor_reduce(best, tmp, AX.X, ALU.max))
    chain.step(dve.tensor_tensor(mask, tmp, best.unsqueeze(2).to_broadcast(wide), ALU.is_equal))


def pick_masks(dve, chain, score, masks, K, best, tmp, rank, E):
    for k in range(K):
        pick_first(dve, chain, score, best, masks[:, k, :, :], tmp, rank, B, E)
        if k < K - 1:
            chain.step(dve.scalar_tensor_tensor(out=score, in0=masks[:, k, :, :], scalar=-1e30, in1=score, op0=ALU.mult, op1=ALU.add))


def pick_weights(dve, chain, score, masks, w, K, tmp):
    for k in range(K):
        chain.step(dve.tensor_tensor(tmp, masks[:, k, :, :], score, ALU.mult))
        chain.step(dve.tensor_reduce(w[:, :, k], tmp, AX.X, ALU.add))


def route_softmax(dve, act_exp, chain, logits, masks, w, bufs, K, E):
    wide = [P, B, E]
    score, tmp, best, rank, tot = bufs
    chain.step(dve.tensor_reduce(best, logits, AX.X, ALU.max))
    act_exp(dve.tensor_tensor(score, logits, best.unsqueeze(2).to_broadcast(wide), ALU.subtract))
    chain.step(dve.tensor_reduce(tot, score, AX.X, ALU.add))
    chain.step(dve.reciprocal(tot, tot))
    chain.step(dve.tensor_tensor(score, score, tot.unsqueeze(2).to_broadcast(wide), ALU.mult))
    if K == 1:
        pick_masks(dve, chain, logits, masks, K, best, tmp, rank, E)
    else:
        chain.step(dve.tensor_copy(logits, score))
        pick_masks(dve, chain, logits, masks, K, best, tmp, rank, E)
    pick_weights(dve, chain, score, masks, w, K, tmp)


def route_grouped(dve, act_sigmoid, chain, logits, masks, w, bufs, K, E, bias, small):
    G = 4
    N = E // G
    wide, grouped = [P, B, E], [P, B * G, N]
    score, tmp, best, rank, tot = bufs
    mask, sfc, rank4, gbest, gsum, gmask, gtmp, gpick = small
    by_group = lambda a: a.rearrange("p b (g n) -> p (b g) n", n=N)
    act_sigmoid(dve.tensor_copy(score, logits))
    chain.step(dve.tensor_tensor(sfc, score, bias.unsqueeze(1).to_broadcast(wide), ALU.add))
    chain.step(dve.tensor_reduce(gsum, by_group(sfc), AX.X, ALU.max))
    pick_first(dve, chain, by_group(sfc), gbest, by_group(mask), by_group(tmp), rank4.to_broadcast(grouped), B * G, N)
    chain.step(dve.scalar_tensor_tensor(out=tmp, in0=mask, scalar=-1e30, in1=sfc, op0=ALU.mult, op1=ALU.add))
    chain.step(dve.tensor_reduce(gbest, by_group(tmp), AX.X, ALU.max))
    chain.step(dve.tensor_tensor(gsum, gsum, gbest, ALU.add))
    per_row = lambda a: a.rearrange("p (b g) -> p b g", g=G)
    pick_first(dve, chain, per_row(gsum), tot, per_row(gmask), per_row(gtmp), rank4.to_broadcast([P, B, G]), B, G)
    chain.step(dve.scalar_tensor_tensor(out=gsum, in0=gmask, scalar=-1e30, in1=gsum, op0=ALU.mult, op1=ALU.add))
    pick_first(dve, chain, per_row(gsum), tot, per_row(gpick), per_row(gtmp), rank4.to_broadcast([P, B, G]), B, G)
    chain.step(dve.tensor_tensor(gmask, gmask, gpick, ALU.add))
    chain.step(dve.tensor_tensor(by_group(sfc), by_group(sfc), gmask.unsqueeze(2).to_broadcast(grouped), ALU.mult))
    pick_masks(dve, chain, sfc, masks, K, best, tmp, rank, E)
    pick_weights(dve, chain, score, masks, w, K, tmp)
    chain.step(dve.tensor_reduce(tot, w, AX.X, ALU.add))
    chain.step(dve.tensor_scalar(tot, tot, 1e-20, None, ALU.add))
    chain.step(dve.reciprocal(tot, tot))
    chain.step(dve.tensor_tensor(w, w, tot.unsqueeze(2).to_broadcast([P, B, K]), ALU.mult))


def moe_tiles(K, E):
    return E + (B * P * K - 1) // P


def moe(core, kind):
    nc, ins, h = core.nc, core.ins, core.h
    nm = {"swiglu": "f0", "gelu": "f1", "silu": "f3"}[kind]
    E = {"swiglu": 8, "gelu": 8, "silu": 16}[kind]
    K = {"swiglu": 2, "gelu": 1, "silu": 4}[kind]
    I = {"swiglu": 256, "gelu": 1024, "silu": 352}[kind]
    ES = 2 if kind == "silu" else 0
    gated = kind != "gelu"
    biased = kind != "silu"
    W1 = 2 * I if gated else I
    NI = -(-I // P)
    width = [min(P, I - j * P) for j in range(NI)]
    NT = moe_tiles(K, E)
    if NT % 2 == 0:
        NT += 1
    banks = {"swiglu": [(0, 512)], "gelu": [(0, 512), (512, 1024)], "silu": [(0, I), (I, 2 * I)]}[kind]
    xd, yd = core.slot_rows.ap(), core.slot_outputs.ap()

    ctx, sb, ps, sem = stage(nc, nm)
    with ctx:
        norm = TokenNorm(core, sb, sem, h)
        up_w = sb("up_w", [P, E + ES // 2, DC, W1])
        down_w = sb("down_w", [P, E + ES // 2, NI, D])
        xn = sb("xn", [P, B, D])
        xTr = sb("xTr", [P, 2, DC, P])
        wr, r_b, rank = sb("wr", [P, DC, E]), sb("r_b", [P, E]), sb("rank", [P, 1, E])
        before, earlier, thr = sb("before", [P, P]), sb("earlier", [P, E, E]), sb("thr", [P, 1, 16])
        tile_id = sb("tile_id", [1, NT, 1])
        consts = [(wr[:, :, :], ins[nm + "_wr"].rearrange("(c p) n -> p c n", p=P)),
                  (r_b[:, :], ins[nm + "_rb"].partition_broadcast(P)),
                  (rank[:, 0, :], ins[f"rank{E}"].partition_broadcast(P)),
                  (before[:, :], ins["before"]),
                  (earlier[:, :, :].rearrange("p a b -> p (a b)"), ins[f"earlier{E}"].partition_broadcast(P)),
                  (thr[:, 0, :], ins["tile_starts"].partition_broadcast(P)),
                  (tile_id[:, :, 0], ins["tile_ids"][:, 0:NT])]
        logits, score, tmp = (sb(n_, [P, B, E]) for n_ in ("logits", "score", "tmp"))
        hT = sb("hT", [P, NI, P])
        y = sb("y", [P, 2, D])
        yg = sb("yg", [P, 2 * K, D])
        lent_hT, lent_y = hT[:, :, :].rearrange("p n t -> p (n t)"), y[:, :, :].rearrange("p u d -> p (u d)")
        lent_yg = yg[:, :, :].rearrange("p k d -> p (k d)")
        masks = lent_yg[:, 0:K * B * E].rearrange("p (k b e) -> p k b e", k=K, b=B)
        best, tot = sb("best", [P, B]), sb("tot", [P, B])
        wts = sb("wts", [P, B, K, 1])
        w3 = wts[:, :, :, 0]
        bufs = [score[:, :, :], tmp[:, :, :], best[:, :], rank[:, :, :].to_broadcast([P, B, E]), tot[:, :]]
        if kind == "silu":
            rank4 = sb("rank4", [P, 1, 4])
            consts.append((rank4[:, 0, :], ins["rank4"].partition_broadcast(P)))
            small = [lent_y[:, u * B * E:(u + 1) * B * E].rearrange("p (b e) -> p b e", e=E) for u in range(2)] + [rank4[:, :, :]]
            small += [sb(n_, [P, B * 4])[:, :] for n_ in ("gbest", "gsum", "gmask", "gtmp", "gpick")]
        earlier_tiles = sb("earlier_tiles", [P, B + 1, E])
        tiles, start = sb("tiles", [P, E]), sb("start", [P, 1, E])
        tiles_cmp = lent_hT[:, 0:E * 16].rearrange("p (e n) -> p e n", e=E)
        start_cmp = lent_hT[:, 0:E * E].rearrange("p (e n) -> p e n", e=E)
        slot_f, slot = sb("slot_f", [P, B, K]), sb("slot", [P, B, K], I32)
        eid_cmp = lent_yg[0:1, 0:NT * E].rearrange("p (n e) -> p n e", e=E)
        eid_f, eid = sb("eid_f", [1, NT]), sb("eid", [1, NT], I32)
        xs = xTr[:, :, :, :].rearrange("p u c t -> p u (c t)")
        xT = sb("xT", [P, DC, P])
        hid = sb("hid", [P, I])
        if gated:
            gate = sb("gate", [P, I])
        if kind == "swiglu":
            clip = sb("clip", [P, 2 * I])
        if biased:
            NB = E * (W1 + D) // P
            b_f, b_parts, bias = sb("b_f", [P, NB]), sb("b_parts", [P, 3, NB], BF16), sb("bias", [3, E, W1 + D], BF16)
        psU = ps("up_ps", [P, 2, 512])
        psH = ps("hT_ps", [P, 2, 4, P])
        psX = ps("x", [P, 2, 512])
        psY = ps("y_ps", [P, 512])
        psL = ps("logits_ps", [P, 512])

        consts_in, xn_ready = sem("consts_in"), sem("xn_ready")
        xTr_full, xTr_read, logits_full = sem("xTr_full"), sem("xTr_read"), sem("logits_full")
        routed, act_done, dve_chain = sem("routed"), sem("act_done"), sem("dve_chain")
        picks_ready, ranks_full, slots_ready, eid_ready = sem("picks_ready"), sem("ranks_full"), sem("slots_ready"), sem("eid_ready")
        w_in = [sem(f"w_in{e}") for e in range(E + ES)]
        w_ready = sem("w_ready")
        scattered = sem("scattered")
        x_in = [sem("x_in0"), sem("x_in1")]
        xT_full, xT_ready, up_full, act_full, hid_ready = sem("xT_full"), sem("xT_ready"), sem("up_full"), sem("act_full"), sem("hid_ready")
        hT_full, hT_ready, y_full, y_ready = sem("hT_full"), sem("hT_ready"), sem("y_full"), sem("y_ready")
        clip_chain = sem("clip_chain")
        stored = [sem("stored0"), sem("stored1")]
        gathered = [sem("gathered0"), sem("gathered1")]
        pick_added, added = sem("pick_added"), sem("added")
        bias_raw, bias_split, bias_out, bias_in = sem("bias_raw"), sem("bias_split"), sem("bias_out"), sem("bias_in")

        phases = [("routed", 0, NT)]
        if ES:
            phases = [("before", 0, B), ("routed", B, NT), ("after", B + NT, B)]

        block = ctx.enter_context(nc.Block())

        @block.sync
        def _(sp):
            for dst, s in consts:
                sp.dma_start(dst, s).then_inc(consts_in, 16)
            if biased:
                sp.dma_start(b_f[:, :], ins[nm + "_biases"].rearrange("(p n) -> p n", p=P)).then_inc(bias_raw, 16)
                flat = core.bias_parts.ap()[:, 0:P * NB]
                sp.wait_ge(bias_split, 1)
                for k in range(3):
                    sp.dma_start(flat[k].rearrange("(p n) -> p n", p=P), b_parts[:, k, :]).then_inc(bias_out, 16)
                sp.wait_ge(bias_out, 48)
                sp.dma_start(bias[:, :, :].rearrange("k e n -> k (e n)"), flat).then_inc(bias_in, 16)
            for name, base, count in phases:
                def load(n, par):
                    if not (isinstance(n, int) and base + n < 2):
                        sp.wait_ge(xT_full, n + (base - 1))
                    src = xd[bass.ts(n, P), :] if name == "routed" else xn[:, n, :]
                    sp.dma_start(xs[:, par, :], src).then_inc(x_in[par], 16)

                def store(n, par):
                    if name == "routed":
                        sp.wait_ge(y_ready, n + (base + 1))
                        sp.dma_start(yd[bass.ts(n, P), :], y[:, par, :]).then_inc(stored[par], 16)

                if name == "routed":
                    sp.wait_ge(scattered, 16 * B * K)
                elif name == "before":
                    sp.wait_ge(logits_full, B)
                for n in range(4):
                    load(n, n % 2)
                pairs = (count - 4) // 2
                with sp.Fori(0, pairs) as i:
                    for u in range(2):
                        load(2 * i + (u + 4), u)
                        store(2 * i + u, u)
                for n in range(2 * pairs + 4, count):
                    load(n, n % 2)
                for n in range(2 * pairs, count):
                    store(n, n % 2)
                if name == "before":
                    sp.wait_ge(y_full, B)
                    sp.dma_start(up_w[:, E, :, :], ins[nm + "_w1"][E + 1].rearrange("(c p) n -> p c n", p=P)).then_inc(w_in[E + 1], 16)
                    sp.dma_start(down_w[:, E, :, :], ins[nm + "_w2"][E + 1].rearrange("(c p) n -> p c n", p=P)).then_inc(w_in[E + 1], 16)

        @block.gpsimd
        def _(pool):
            norm.rsqrt(pool)
            pool.wait_ge(core.rows_cleared, 16)
            pool.wait_ge(slots_ready, 1)
            for b in range(B):
                for k in range(K):
                    pool.indirect_dma_start(
                        out=xd[0:NT * P, :], out_offset=bass.IndirectOffsetOnAxis(ap=slot[:, b, k:k + 1].bitcast(U32), axis=0),
                        in_=xn[:, b, :], in_offset=None,
                    ).then_inc(scattered, 16)
            for e in range(E):
                pool.wait_ge(w_in[e], 32)
                pool.sem_inc(w_ready, 1)
            pool.sem_inc(w_ready, NT)
            pool.wait_ge(stored[0], 16 * ((NT + 1) // 2 + 1))
            pool.wait_ge(stored[1], 16 * (NT // 2 + 1))
            for b in range(B):
                if b >= 2:
                    pool.wait_ge(added, b - 1)
                for k in range(K):
                    pool.indirect_dma_start(
                        out=yg[:, (b % 2) * K + k, :], out_offset=None, in_=yd[0:NT * P, :],
                        in_offset=bass.IndirectOffsetOnAxis(ap=slot[:, b, k:k + 1].bitcast(U32), axis=0),
                    ).then_inc(gathered[b % 2], 16)

        @block.scalar
        def _(act):
            order = list(range(E, E + ES // 2)) + list(range(E))
            for e in order:
                act.dma_start(up_w[:, e, :, :], ins[nm + "_w1"][e].rearrange("(c p) n -> p c n", p=P)).then_inc(w_in[e], 16)
                act.dma_start(down_w[:, e, :, :], ins[nm + "_w2"][e].rearrange("(c p) n -> p c n", p=P)).then_inc(w_in[e], 16)
            with act.Fori(0, B // 2) as i:
                for u in range(2):
                    act.wait_ge(xTr_full, 2 * i + (u + 1))
                    act.copy(xTr[:, u, :, :], psX[:, u, 0:D].rearrange("p (c t) -> p c t", c=DC)).then_inc(xTr_read, 1)
            act.sem_inc(stored[0], 16)
            act.sem_inc(stored[1], 16)
            act.wait_ge(routed, 1)
            act.activation(score[:, :, :], score[:, :, :], ACT.Sigmoid if kind == "silu" else ACT.Exp).then_inc(act_done, 1)

            def xcopy(n, first):
                act.wait_ge(xT_full, n + 1)
                act.copy(xT[:, :, :], psX[:, 0, 0:D].rearrange("p (c t) -> p c t", c=DC)).then_inc(xT_ready, 1)

            def hidden(n):
                if kind == "gelu":
                    act.wait_ge(up_full, n + 1)
                    for c, (lo, hi) in enumerate(banks):
                        i_ = act.activation(hid[:, lo:hi], psU[:, c, :], ACT.Gelu)
                    i_.then_inc(hid_ready, 1)
                elif kind == "swiglu":
                    act.wait_ge(clip_chain, 3 * n + 1)
                    act.activation(gate[:, :], clip[:, 0:I], ACT.Sigmoid, scale=1.702).then_inc(act_full, 1)
                else:
                    act.wait_ge(up_full, n + 1)
                    act.activation(gate[:, :], psU[:, 0, 0:I], ACT.Silu).then_inc(act_full, 1)

            for name, base, count in phases:
                xcopy(base, True)
                hidden(base)
                xcopy(base + 1, True)

                def turn(n, par, has_next, has_second):
                    if has_next:
                        hidden(n + (base + 1))
                    if has_second:
                        xcopy(n + (base + 2), False)
                    if name == "routed":
                        act.wait_ge(y_full, n + (base + 1))
                        act.wait_ge(stored[par], 16 * ((n - par) // 2 + 1) if isinstance(n, int) else store_count[0])
                        act.copy(y[:, par, :], psY[:, 0:D]).then_inc(y_ready, 1)

                turn(0, 0, True, True)
                pairs = (count - 3) // 2
                with act.Fori(0, pairs) as i:
                    for u in range(2):
                        store_count = [16 * (i + (u + 1))]
                        turn(2 * i + (1 + u), (1 + u) % 2, True, True)
                for n in range(1 + 2 * pairs, count):
                    turn(n, n % 2, n + 1 < count, n + 2 < count)

        @block.tensor
        def _(pe):
            pe.wait_ge(consts_in, 16 * len(consts))

            def rows(t, u):
                pe.wait_ge(xn_ready, t + 1)
                for c in range(DC):
                    mm = pe.transpose(psX[:, u, c * P:(c + 1) * P], xn[:, t, c * P:(c + 1) * P], core.ident[:, :])
                mm.then_inc(xTr_full, 1)

            for t in range(2):
                rows(t, t)
            for t in range(B):
                pe.wait_ge(xTr_read, t + 1)
                for c in range(DC):
                    mm = pe.matmul(psL[:, t * E:(t + 1) * E], xTr[:, t % 2, c, :], wr[:, c, :], start=c == 0, stop=c == DC - 1)
                mm.then_inc(logits_full, 1)
                if t + 2 < B:
                    rows(t + 2, t % 2)
            pe.wait_ge(picks_ready, 1)
            picks = tmp[:, :, :].rearrange("p b e -> p (b e)")
            pe.matmul(psL[:, 0:B * E], before[:, :], picks, start=True, stop=True)
            pe.matmul(psL[:, B * E:2 * B * E], core.ones[:, :], picks, start=True, stop=True).then_inc(ranks_full, 1)

            loaded = [0, 0]
            for name, base, count in phases:
                def expert(n):
                    if name == "before":
                        return E
                    if name == "after":
                        return E
                    return pe.value_load(eid[0:1, n:n + 1] if isinstance(n, int) else eid[0:1, bass.ts(n, 1)], min_val=0, max_val=E - 1)

                def tr_x(n, par):
                    pe.wait_ge(x_in[par], 16 * (n // 2 + 1 + loaded[par]) if isinstance(n, int) else x_count[0])
                    if not (isinstance(n, int) and n + base < 1):
                        pe.wait_ge(xT_ready, n + base)
                    for c in range(DC):
                        mm = pe.transpose(psX[:, 0, c * P:(c + 1) * P], xs[:, par, c * P:(c + 1) * P], core.ident[:, :])
                    mm.then_inc(xT_full, 1)

                def up(n):
                    if name == "routed":
                        pe.wait_ge(w_ready, n + 1)
                    e = expert(n)
                    pe.wait_ge(xT_ready, n + (base + 1))
                    for b, (lo, hi) in enumerate(banks):
                        out = psU[:, b, 0:hi - lo]
                        if biased:
                            pe.matmul(out, core.ones_bf[0:3, :], bias[:, e, lo:hi], start=True, stop=False)
                        for c in range(DC):
                            mm = pe.matmul(out, xT[:, c, :], up_w[:, e, c, lo:hi], start=c == 0 and not biased, stop=c == DC - 1)
                    mm.then_inc(up_full, 1)

                def tr_h(n):
                    pe.wait_ge(hid_ready, n + (base + 1))
                    for j, m in enumerate(width):
                        mm = pe.transpose(psH[0:m, j // 4, j % 4, :], hid[:, j * P:j * P + m], core.ident[:, :])
                    mm.then_inc(hT_full, 1)

                def down(n):
                    e = expert(n)
                    pe.wait_ge(hT_ready, n + (base + 1))
                    if not (isinstance(n, int) and n + base < 1):
                        pe.wait_ge(y_ready, n + base)
                    if biased:
                        pe.matmul(psY[:, 0:D], core.ones_bf[0:3, :], bias[:, e, W1:W1 + D], start=True, stop=False)
                    for j, m in enumerate(width):
                        mm = pe.matmul(psY[:, 0:D], hT[0:m, j, :], down_w[0:m, e, j, :], start=j == 0 and not biased, stop=j == NI - 1)
                    mm.then_inc(y_full, 1)

                if name == "before":
                    pe.wait_ge(w_in[E], 32)
                elif name == "after":
                    pe.wait_ge(w_in[E + 1], 32)
                else:
                    pe.wait_ge(eid_ready, 1)
                    if biased:
                        pe.wait_ge(bias_in, 16)
                tr_x(0, 0)
                up(0)
                tr_x(1, 1)

                def turn(n, par, has_next, has_second):
                    tr_h(n)
                    if has_next:
                        up(n + 1)
                    if has_second:
                        tr_x(n + 2, par)
                    down(n)

                turn(0, 0, True, True)
                pairs = (count - 3) // 2
                with pe.Fori(0, pairs) as i:
                    for u in range(2):
                        x_count = [16 * (i + (u + 2 + loaded[(1 + u) % 2]))]
                        turn(2 * i + (1 + u), (1 + u) % 2, True, True)
                for n in range(1 + 2 * pairs, count):
                    turn(n, n % 2, n + 1 < count, n + 2 < count)
                loaded = [loaded[0] + (count + 1) // 2, loaded[1] + count // 2]

        @block.vector
        def _(dve):
            chain = Chain(dve, dve_chain)
            if biased:
                dve.wait_ge(bias_raw, 16)
                for k in range(3):
                    chain.step(dve.tensor_copy(b_parts[:, k, :], b_f[:, :]))
                    if k < 2:
                        chain.step(dve.tensor_tensor(b_f[:, :], b_f[:, :], b_parts[:, k, :], ALU.subtract))
                dve.sem_inc(bias_split, 1)
            norm.stats(dve)
            dve.wait_ge(norm.rstd_done, 1)
            for t in range(B):
                norm.normalise(dve, xn[:, t, :], t).then_inc(xn_ready, 1)
            dve.wait_ge(consts_in, 16 * len(consts))
            dve.wait_ge(logits_full, B)
            ps_l = psL[:, 0:B * E].rearrange("p (b e) -> p b e", e=E)

            def by_act(last):
                last.then_inc(routed, 1)
                dve.wait_ge(act_done, 1)

            if kind == "silu":
                chain.step(dve.tensor_copy(logits[:, :, :], ps_l))
                route_grouped(dve, by_act, chain, logits[:, :, :], masks, w3, bufs, K, E, r_b[:, :], small)
            else:
                chain.step(dve.tensor_tensor(logits[:, :, :], ps_l, r_b[:, :].unsqueeze(1).to_broadcast([P, B, E]), ALU.add))
                route_softmax(dve, by_act, chain, logits[:, :, :], masks, w3, bufs, K, E)
            last = dve.tensor_copy(tmp[:, :, :], masks[:, 0, :, :])
            for k in range(1, K):
                chain.step(last)
                last = dve.tensor_tensor(tmp[:, :, :], tmp[:, :, :], masks[:, k, :, :], ALU.add)
            last.then_inc(picks_ready, 1)
            dve.wait_ge(ranks_full, 1)
            ps_t = psL[:, B * E:2 * B * E].rearrange("p (b e) -> p b e", e=E)
            chain.step(dve.memset(earlier_tiles[:, 0, :], 0.0))
            for b in range(B):
                chain.step(dve.tensor_tensor(earlier_tiles[:, b + 1, :], earlier_tiles[:, b, :], ps_t[:, b, :], ALU.add))
            chain.step(dve.tensor_tensor(tiles_cmp[:, :, :], earlier_tiles[:, B, :].unsqueeze(2).to_broadcast([P, E, 16]),
                                         thr[:, :, :].to_broadcast([P, E, 16]), ALU.is_gt))
            chain.step(dve.tensor_reduce(tiles[:, :], tiles_cmp[:, :, :], AX.X, ALU.add))
            chain.step(dve.tensor_tensor(start_cmp[:, :, :], earlier[:, :, :], tiles[:, :].unsqueeze(1).to_broadcast([P, E, E]), ALU.mult))
            chain.step(dve.tensor_reduce(start[:, 0, :], start_cmp[:, :, :], AX.X, ALU.add))
            chain.step(dve.tensor_tensor(score[:, :, :], earlier_tiles[:, 0:B, :], ps_l, ALU.add))
            chain.step(dve.scalar_tensor_tensor(out=score[:, :, :], in0=start[:, :, :].to_broadcast([P, B, E]), scalar=float(P),
                                                in1=score[:, :, :], op0=ALU.mult, op1=ALU.add))
            for k in range(K):
                chain.step(dve.tensor_tensor(tmp[:, :, :], masks[:, k, :, :], score[:, :, :], ALU.mult))
                chain.step(dve.tensor_reduce(slot_f[:, :, k], tmp[:, :, :], AX.X, ALU.add))
            dve.tensor_copy(slot[:, :, :], slot_f[:, :, :]).then_inc(slots_ready, 1)
            chain.step(dve.tensor_tensor(eid_cmp[:, :, :], tile_id[:, :, :].to_broadcast([1, NT, E]), start[0:1, :, :].to_broadcast([1, NT, E]), ALU.is_ge))
            chain.step(dve.tensor_reduce(eid_f[:, :], eid_cmp[:, :, :], AX.X, ALU.add))
            dve.tensor_scalar(eid[:, :], eid_f[:, :], -1.0, None, ALU.add).then_inc(eid_ready, 1)

            def combine(b, par, turn_of_pair):
                dve.wait_ge(gathered[par], turn_of_pair)
                for k in range(K):
                    i_ = dve.scalar_tensor_tensor(out=h[:, b, :], in0=yg[:, par * K + k, :], scalar=wts[:, b, k, :],
                                                  in1=h[:, b, :], op0=ALU.mult, op1=ALU.add)
                    if k < K - 1:
                        i_.then_inc(pick_added, 1)
                        dve.wait_ge(pick_added, b * (K - 1) + (k + 1))
                i_.then_inc(added, 1)

            for name, base, count in phases:
                def hidden(n):
                    n = n + base
                    if kind == "swiglu":
                        dve.wait_ge(up_full, n + 1)
                        dve.tensor_scalar(clip[:, 0:I], psU[:, 0, 0:I], 7.0, None, ALU.min).then_inc(clip_chain, 1)
                        dve.tensor_scalar(clip[:, I:2 * I], psU[:, 0, I:2 * I], 7.0, -7.0, ALU.min, ALU.max).then_inc(clip_chain, 1)
                        dve.wait_ge(act_full, n + 1)
                        dve.wait_ge(clip_chain, 3 * n + 2)
                        dve.tensor_tensor(gate[:, :], gate[:, :], clip[:, 0:I], ALU.mult).then_inc(clip_chain, 1)
                        dve.wait_ge(clip_chain, 3 * n + 3)
                        dve.scalar_tensor_tensor(out=hid[:, :], in0=clip[:, I:2 * I], scalar=1.0, in1=gate[:, :],
                                                 op0=ALU.add, op1=ALU.mult).then_inc(hid_ready, 1)
                    elif kind == "silu":
                        dve.wait_ge(act_full, n + 1)
                        dve.tensor_tensor(hid[:, :], gate[:, :], psU[:, 1, 0:I], ALU.mult).then_inc(hid_ready, 1)

                hidden(0)

                def turn(n, par, has_next, has_second):
                    dve.wait_ge(hT_full, n + (base + 1))
                    full = sum(m == P for m in width)
                    for c in range(-(-full // 4)):
                        lo, hi = 4 * c, min(4 * c + 4, full)
                        i_ = dve.tensor_scalar(hT[:, lo:hi, :], psH[:, c, 0:hi - lo, :], 1.0, None, ALU.mult)
                    if full < NI:
                        i_ = dve.tensor_scalar(hT[0:width[-1], full, :], psH[0:width[-1], full // 4, full % 4, :], 1.0, None, ALU.mult)
                    i_.then_inc(hT_ready, 1)
                    if has_next:
                        hidden(n + 1)
                    if name != "routed":
                        dve.wait_ge(y_full, n + (base + 1))
                        dve.tensor_tensor(h[:, n, :], h[:, n, :], psY[:, 0:D], ALU.add).then_inc(y_ready, 1)
                    if name == "after":
                        dve.wait_ge(y_ready, n + (base + 1))
                        combine(n, par, 16 * K * (n // 2 + 1) if isinstance(n, int) else pair_count[0])

                turn(0, 0, True, True)
                pairs = (count - 3) // 2
                with dve.Fori(0, pairs) as i:
                    for u in range(2):
                        pair_count = [16 * K * (i + (u + 1))]
                        turn(2 * i + (1 + u), (1 + u) % 2, True, True)
                for n in range(1 + 2 * pairs, count):
                    turn(n, n % 2, n + 1 < count, n + 2 < count)
            if phases[-1][0] == "routed":
                with dve.Fori(0, B // 2) as i:
                    for u in range(2):
                        combine(2 * i + u, u, 16 * K * (i + 1))
            dve.wait_ge(added, B)


def mlp(core, src):
    nc, ins, h = core.nc, core.ins, core.h
    nm, E, I, G = "f2", 2, 512, 4
    w1, w2 = ins[nm + "_w1"], ins[nm + "_w2"]
    NI = I // P
    TG = B // G
    N = TG * P

    ctx, sb, ps, sem = stage(nc, nm)
    with ctx:
        norm = TokenNorm(core, sb, sem, src)
        xn = sb("xn", [P, 2, D])
        xT = sb("xT", [P, DC, B * P])
        hid = sb("hid", [P, 2, NI, N])
        up_w = sb("up_w", [P, E, DC, I])
        down_w = sb("down_w", [P, E, NI, D])
        up_b = sb("up_b", [P, E, NI])
        b2 = sb("b2", [P, D])
        psU = ps("up_ps", [P, 4, 512])
        psD = ps("down_ps", [P, 4, 512])
        xn_ready, x_full, x_read = sem("xn_ready"), sem("x_full"), sem("x_read")
        w_in, b2_in = sem("w_in"), sem("b2_in")
        up_full, hid_ready, down_full, h_added = sem("up_full"), sem("hid_ready"), sem("down_full"), sem("h_added")
        b_added = sem("b_added")
        gam, bet = sb("gam", [P, DC]), sb("bet", [P, DC])
        loads = [(gam[:, :], ins[nm + "_g"]), (bet[:, :], ins[nm + "_b"])]
        for e in range(E):
            loads += [(up_w[:, e, :, :], w1[e].rearrange("(c p) n -> p c n", p=P)),
                      (down_w[:, e, :, :], w2[e].rearrange("(c p) n -> p c n", p=P)), (up_b[:, e, :], ins[nm + "_b1"][e])]
        units = [(e, g) for e in range(E) for g in range(G)]
        block = ctx.enter_context(nc.Block())

        @block.sync
        def _(sp):
            sp.dma_start(b2[:, :], ins[nm + "_b2"][0].partition_broadcast(P)).then_inc(b2_in, 16)
            for dst, s in loads:
                sp.dma_start(dst, s).then_inc(w_in, 16)

        @block.gpsimd
        def _(pool):
            norm.rsqrt(pool)
            pool.wait_ge(b2_in, 16)
            for b in range(B):
                pool.tensor_tensor(h[:, b, :], h[:, b, :], b2[:, :], ALU.add).then_inc(b_added, 1)

        @block.scalar
        def _(act):
            act.wait_ge(w_in, 16 * len(loads))
            for n, (e, g) in enumerate(units):
                for j in range(NI):
                    act.wait_ge(up_full, n * NI + j + 1)
                    act.activation(hid[:, n % 2, j, :], psU[:, (n * NI + j) % 4, :], ACT.Gelu, bias=up_b[:, e, j:j + 1]).then_inc(hid_ready, 1)

        @block.tensor
        def _(pe):
            for t in range(B):
                pe.wait_ge(xn_ready, t + 1)
                if t >= 2:
                    pe.wait_ge(x_read, t - 1)
                for c in range(DC):
                    mm = pe.transpose(psD[:, t % 2, c * P:(c + 1) * P], xn[:, t % 2, c * P:(c + 1) * P], core.ident[:, :])
                mm.then_inc(x_full, 1)
            pe.wait_ge(w_in, 16 * len(loads))
            pe.wait_ge(x_read, B)

            def up(n):
                e, g = units[n]
                for j in range(NI):
                    p = n * NI + j
                    if p >= 4:
                        pe.wait_ge(hid_ready, p - 3)
                    for c in range(DC):
                        mm = pe.matmul(psU[:, p % 4, :], up_w[:, e, c, j * P:(j + 1) * P], xT[:, c, g * N:(g + 1) * N],
                                       start=c == 0, stop=c == DC - 1)
                    mm.then_inc(up_full, 1)

            def down(n):
                e, g = units[n]
                pe.wait_ge(hid_ready, (n + 1) * NI)
                for k in range(TG):
                    if n:
                        pe.wait_ge(h_added, 4 * (n - 1) + k + 1)
                    for j in range(NI):
                        mm = pe.matmul(psD[:, k, 0:D], hid[:, n % 2, j, k * P:(k + 1) * P], down_w[:, e, j, :],
                                       start=j == 0, stop=j == NI - 1)
                    mm.then_inc(down_full, 1)

            up(0)
            for n in range(len(units)):
                if n + 1 < len(units):
                    up(n + 1)
                down(n)

        @block.vector
        def _(dve):
            norm.stats(dve)
            dve.wait_ge(w_in, 16 * len(loads))
            dve.wait_ge(norm.rstd_done, 1)
            for t in range(B + 1):
                if t < B:
                    if t >= 2:
                        dve.wait_ge(x_full, t - 1)
                    norm.normalise(dve, xn[:, t % 2, :], t).then_inc(xn_ready, 1)
                if t > 0:
                    dve.wait_ge(x_full, t)
                    for c in range(DC):
                        i_ = dve.tensor_scalar(xT[:, c, (t - 1) * P:t * P], psD[:, (t - 1) % 2, c * P:(c + 1) * P], gam[:, c:c + 1], bet[:, c:c + 1],
                                               ALU.mult, ALU.add)
                    i_.then_inc(x_read, 1)
            dve.wait_ge(b_added, B)
            for n, (e, g) in enumerate(units):
                for k in range(TG):
                    dve.wait_ge(down_full, 4 * n + k + 1)
                    t = g * TG + k
                    if n >= G:
                        dve.wait_ge(h_added, 4 * (n - G) + k + 1)
                    dve.tensor_tensor(h[:, t, :], h[:, t, :], psD[:, k, 0:D], ALU.add).then_inc(h_added, 1)


def delta_net(core, x0):
    nc, ins, h = core.nc, core.ins, core.h
    pre = "L2_attn_"
    H, dh, S2, BL = 16, 16, 2, B // 2
    W = 3 * D + 2 * H
    Q, K, V = range(3)
    ctx, sb, ps, sem = stage(nc, "dn")
    with ctx:
        pairs_kq = sb("kq", [P, S2, 2, dh, P])
        pairs_bv = sb("bv", [P, S2, dh, P])
        pairs_g = sb("gates", [P, S2, 2, P])
        tokens = sb("tokens", [P, 3, B, D])
        rates = sb("rates", [P, 2, B, H])
        proj_in = ExitStack()
        ctx1, sb1, ps1, sem1 = stage(nc, "dn1")
        with ctx1:
            outer = TokenNorm(core, sb1, sem1, h)
            ctx_i, sbi, _, semi = stage(nc, "dn1i")
            ctx1.enter_context(ctx_i)
            inner = TokenNorm(core, sbi, semi, x0)
            xn, xT = sb1("xn", [P, D]), sb1("xT", [P, DC, P])
            w = sb1("w", [P, DC, W])
            gam, bet = sb1("gam", [P, DC]), sb1("bet", [P, DC])
            psX, psY = ps1("x", [P, 512]), ps1("y", [P, 2, 512])
            loaded, x0_done, xn_ready = sem1("loaded"), sem1("x0_done"), sem1("xn_ready")
            x_full, x_read, y_full, y_read = sem1("x_full"), sem1("x_read"), sem1("y_full"), sem1("y_read")
            block = ctx1.enter_context(nc.Block())

            @block.sync
            def _(sp):
                at = 0
                for n in ("Wq", "Wk", "Wv", "Wb", "Wg"):
                    src = ins[pre + n]
                    sp.dma_start(w[:, :, at:at + src.shape[1]], src.rearrange("(c p) n -> p c n", p=P)).then_inc(loaded, 16)
                    at += src.shape[1]
                sp.dma_start(gam[:, :], ins["f2_ln1_g"]).then_inc(loaded, 16)
                sp.dma_start(bet[:, :], ins["f2_ln1_b"]).then_inc(loaded, 16)

            @block.gpsimd
            def _(pool):
                outer.rsqrt(pool)
                inner.rsqrt(pool)

            @block.vector
            def _(dve):
                outer.stats(dve)
                dve.wait_ge(outer.rstd_done, 1)
                with dve.Fori(0, B) as t:
                    outer.normalise(dve, x0[:, t, :], t).then_inc(x0_done, 1)
                dve.wait_ge(x0_done, B)
                inner.stats(dve)
                dve.wait_ge(inner.rstd_done, 1)

                def normal(t):
                    inner.normalise(dve, xn[:, :], t).then_inc(xn_ready, 1)

                def copy(t):
                    dve.wait_ge(y_full, 2 * t + 1)
                    dve.tensor_scalar(tokens[:, Q, t, :], psY[:, 0, 0:D], float(dh) ** -0.5, None, ALU.mult)
                    dve.tensor_scalar(tokens[:, K, t, :], psY[:, 0, D:2 * D], 1.0, None, ALU.mult).then_inc(y_read, 1)
                    dve.wait_ge(y_full, 2 * t + 2)
                    dve.tensor_scalar(tokens[:, V, t, :], psY[:, 1, 0:D], 1.0, None, ALU.mult)
                    dve.tensor_scalar(rates[:, :, t, :], psY[:, 1, D:D + 2 * H].rearrange("p (j h) -> p j h", j=2), 1.0, None,
                                      ALU.mult).then_inc(y_read, 1)

                normal(0)
                with dve.Fori(0, B - 1) as t:
                    dve.wait_ge(x_full, t + 1)
                    normal(t + 1)
                    copy(t)
                copy(B - 1)

            @block.scalar
            def _(act):
                act.wait_ge(loaded, 16 * 7)
                with act.Fori(0, B) as t:
                    act.wait_ge(x_full, t + 1)
                    for c in range(DC):
                        a = act.activation(xT[:, c, :], psX[:, c * P:(c + 1) * P], ACT.Identity,
                                           bias=bet[:, c:c + 1], scale=gam[:, c:c + 1])
                    a.then_inc(x_read, 1)

            @block.tensor
            def _(pe):
                pe.wait_ge(loaded, 16 * 7)

                def project(t, again):
                    pe.wait_ge(xn_ready, t + 1)
                    for c in range(DC):
                        mm = pe.transpose(psX[:, c * P:(c + 1) * P], xn[:, c * P:(c + 1) * P], core.ident[:, :])
                    mm.then_inc(x_full, 1)
                    pe.wait_ge(x_read, t + 1)
                    for bank, a, b in ((0, 0, 2 * D), (1, 2 * D, W)):
                        if again:
                            pe.wait_ge(y_read, 2 * t + bank - 1)
                        for c in range(DC):
                            mm = pe.matmul(psY[:, bank, 0:b - a], xT[:, c, :], w[:, c, a:b], start=c == 0, stop=c == DC - 1)
                        mm.then_inc(y_full, 1)

                project(0, False)
                with pe.Fori(1, B) as t:
                    project(t, True)

        ctx2, sb2, ps2, sem2 = stage(nc, "dn2")
        with ctx2:
            sq = sb2("sq", [P, B, D])
            nrm = sb2("nrm", [P, B * H])
            psT = ps2("t", [P, 4, 512])
            chained, squared, rooted, gated, ready = sem2("chained"), sem2("squared"), sem2("rooted"), sem2("gated"), sem2("ready")
            t_full, t_read = sem2("t_full"), [sem2("t_read0"), sem2("t_read1")]
            block = ctx2.enter_context(nc.Block())
            keys = tokens[:, K]
            vals = tokens[:, V]
            heads = lambda a: a.rearrange("p b (h d) -> p (b h) d", d=dh)
            beta, gate = (rates[:, j].rearrange("p b h -> p (b h)") for j in range(2))
            views = []
            for s in range(S2):
                for off, dst in ((K, pairs_kq[:, s, 0]), (Q, pairs_kq[:, s, 1]), (V, pairs_bv[:, s])):
                    for d0 in range(0, dh, 4):
                        srcs = [heads(tokens[:, off])[:, s * P:(s + 1) * P, d0 + i] for i in range(4)]
                        views.append((srcs, dst[:, d0:d0 + 4, :]))
                views.append(([r[:, s * P:(s + 1) * P] for r in (beta, gate)], pairs_g[:, s]))

            @block.vector
            def _(dve):
                chain = Chain(dve, chained)
                dve.tensor_tensor(sq[:, :, :], keys, keys, ALU.mult).then_inc(squared, 1)
                dve.wait_ge(squared, 1)
                dve.tensor_reduce(nrm[:, :], heads(sq[:, :, :]), AX.X, ALU.add).then_inc(squared, 1)
                dve.wait_ge(rooted, 1)
                chain.step(dve.tensor_scalar(nrm[:, :], nrm[:, :], 1e-6, None, ALU.add))
                chain.step(dve.reciprocal(nrm[:, :], nrm[:, :]))
                wide = [P, B * H, dh]
                dve.tensor_tensor(heads(keys), heads(keys), nrm[:, :].unsqueeze(2).to_broadcast(wide), ALU.mult)
                dve.wait_ge(gated, 1)
                chain.step(dve.tensor_tensor(heads(vals), heads(vals), beta.unsqueeze(2).to_broadcast(wide), ALU.mult))
                dve.tensor_tensor(beta, beta, gate, ALU.mult).then_inc(ready, 1)
                for n in range(1, len(views), 2):
                    srcs, dst = views[n]
                    dve.wait_ge(t_full, n + 1)
                    dve.tensor_copy(dst, psT[:, n % 4, 0:len(srcs) * P].rearrange("p (a t) -> p a t", t=P)).then_inc(t_read[1], 1)

            @block.scalar
            def _(act):
                act.activation(rates[:, :, :, :], rates[:, :, :, :], ACT.Sigmoid).then_inc(gated, 1)
                act.wait_ge(squared, 2)
                act.activation(nrm[:, :], nrm[:, :], ACT.Sqrt).then_inc(rooted, 1)
                for n in range(0, len(views), 2):
                    srcs, dst = views[n]
                    act.wait_ge(t_full, n + 1)
                    act.copy(dst, psT[:, n % 4, 0:len(srcs) * P].rearrange("p (a t) -> p a t", t=P)).then_inc(t_read[0], 1)

            @block.tensor
            def _(pe):
                pe.wait_ge(ready, 1)
                for n, (srcs, dst) in enumerate(views):
                    if n >= 4:
                        pe.wait_ge(t_read[n % 2], (n - 4) // 2 + 1)
                    for i, src in enumerate(srcs):
                        mm = pe.transpose(psT[:, n % 4, i * P:(i + 1) * P], src, core.ident[:, :])
                    mm.then_inc(t_full, 1)

        ctx3, sb3, ps3, sem3 = stage(nc, "dn3")
        with ctx3:
            state = sb3("state", [P, S2, dh, dh])
            prod = sb3("prod", [P, S2, 2, dh, dh])
            red = sb3("red", [P, S2, 2, dh])
            outp = sb3("outp", [P, S2, dh, dh])
            hist_a = tokens[:, 0:2].rearrange("p q b w -> p (q b w)").rearrange(
                "p (s j v t) -> p s j v t", s=S2, j=2, v=dh)
            hist_u = sb3("hist_u", [P, S2, dh, P])
            qk = sb3("qk", [P, S2, P])
            chained = sem3("chained")
            block = ctx3.enter_context(nc.Block())

            @block.vector
            def _(dve):
                chain = Chain(dve, chained)
                kq = pairs_kq
                chain.step(dve.tensor_tensor(hist_u[:, :, :, :], kq[:, :, 0], kq[:, :, 1], ALU.mult))
                chain.step(dve.tensor_reduce(qk[:, :, :], hist_u[:, :, :, :].rearrange("p s d t -> p s t d"), AX.X, ALU.add))
                chain.step(dve.memset(state[:, :, :, :], 0.0))
                first, steps = chain.count, 6
                with dve.Fori(0, P) as t:
                    chain.begin(t * steps + first)
                    for s in range(S2):
                        i_ = dve.tensor_tensor(prod[:, s], state[:, s].unsqueeze(1).to_broadcast([P, 2, dh, dh]),
                                               kq[:, s, :, :, t].unsqueeze(2).to_broadcast([P, 2, dh, dh]), ALU.mult)
                    chain.step(i_)
                    chain.step(dve.tensor_reduce(red[:, :, :, :], prod[:, :, :, :, :], AX.X, ALU.add))
                    chain.step(dve.tensor_tensor(hist_a[:, :, :, :, t], red[:, :, :, :],
                                                 pairs_g[:, :, :, t].unsqueeze(3).to_broadcast([P, S2, 2, dh]), ALU.mult))
                    chain.step(dve.tensor_tensor(hist_u[:, :, :, t], pairs_bv[:, :, :, t], hist_a[:, :, 0, :, t], ALU.subtract))
                    dve.tensor_tensor(outp[:, :, :, :], hist_u[:, :, :, t].unsqueeze(3).to_broadcast([P, S2, dh, dh]),
                                      kq[:, :, 0, :, t].unsqueeze(2).to_broadcast([P, S2, dh, dh]), ALU.mult).then_inc(chained, 1)
                    chain.count += 1
                    dve.wait_ge(chained, chain.base + chain.count)
                    for s in range(S2):
                        i_ = dve.scalar_tensor_tensor(out=state[:, s], in0=state[:, s], scalar=pairs_g[:, s, 1, t].unsqueeze(1),
                                                      in1=outp[:, s], op0=ALU.mult, op1=ALU.add)
                    chain.step(i_)
                    assert chain.count == 6
                chain.begin(6 * P + first)
                chain.step(dve.tensor_tensor(hist_u[:, :, :, :], hist_u[:, :, :, :], qk[:, :, :].unsqueeze(2).to_broadcast([P, S2, dh, P]), ALU.mult))
                chain.step(dve.tensor_tensor(hist_u[:, :, :, :], hist_u[:, :, :, :], hist_a[:, :, 1], ALU.add))
                dve.tensor_copy(pairs_bv[:, :, :, :], hist_u[:, :, :, :])

        ctx4, sb4, ps4, sem4 = stage(nc, "dn4")
        with ctx4:
            att = sb4("att", [P, B, D])
            xcur = sb4("xcur", [P, 2, D])
            aT = sb4("aT", [P, 2, DC, P])
            wo, bo = sb4("wo", [P, DC, D]), sb4("bo", [1, D])
            psT, psA, psO = ps4("t", [P, 4, 512]), ps4("a", [P, 2, 512]), ps4("o", [P, 2, 512])
            loaded, t_full, t_read0, t_read1 = sem4("loaded"), sem4("t_full"), sem4("t_read0"), sem4("t_read1")
            a_full, a_read, o_full, o_added, x_added = sem4("a_full"), sem4("a_read"), sem4("o_full"), sem4("o_added"), sem4("x_added")
            t_read = [t_read0, t_read1]
            att_ready = sem4("att_ready")
            block = ctx4.enter_context(nc.Block())
            views = [(s, v0) for s in range(S2) for v0 in range(0, dh, 4)]

            def spread(n):
                s, v0 = views[n]
                src = psT[:, n % 4, :].rearrange("p (v b h) -> p b h v", v=4, b=BL)
                dst = heads4(att[:, s * BL:(s + 1) * BL, :])[:, :, :, v0:v0 + 4]
                return dst, src

            heads4 = lambda a: a.rearrange("p b (h d) -> p b h d", d=dh)

            @block.sync
            def _(sp):
                sp.dma_start(wo[:, :, :], ins[pre + "Wo"].rearrange("(c p) n -> p c n", p=P)).then_inc(loaded, 16)
                sp.dma_start(bo[:, :], ins[pre + "bo"].unsqueeze(0)).then_inc(loaded, 16)

            def spread_all(eng, par):
                for n in range(par, len(views), 2):
                    eng.wait_ge(t_full, n + 1)
                    dst, src = spread(n)
                    for v in range(4):
                        if par:
                            i_ = eng.tensor_copy(dst[:, :, :, v], src[:, :, :, v])
                        else:
                            i_ = eng.copy(dst[:, :, :, v], src[:, :, :, v])
                    i_.then_inc(t_read[par], 1)

            @block.scalar
            def _(act):
                spread_all(act, 0)
                with act.Fori(0, B // 2) as i:
                    for u in range(2):
                        act.wait_ge(a_full, 2 * i + u + 1)
                        act.copy(aT[:, u, :, :], psA[:, u, 0:D].rearrange("p (c t) -> p c t", c=DC)).then_inc(a_read, 1)

            @block.vector
            def _(dve):
                spread_all(dve, 1)
                with dve.Fori(0, B // 2) as i:
                    for u in range(2):
                        t = 2 * i + u
                        dve.wait_ge(t_read[0], 4)
                        dve.tensor_scalar(xcur[:, u, :], att[:, t, :], 1.0, None, ALU.mult).then_inc(att_ready, 1)
                    for u in range(2):
                        t = 2 * i + u
                        dve.wait_ge(o_full, 2 * i + u + 1)
                        dve.tensor_tensor(x0[:, t, :], x0[:, t, :], psO[:, u, 0:D], ALU.add).then_inc(o_added, 1)
                        dve.wait_ge(o_added, 2 * i + u + 1)
                        dve.tensor_tensor(h[:, t, :], h[:, t, :], x0[:, t, :], ALU.add).then_inc(x_added, 1)

            @block.tensor
            def _(pe):
                for n, (s, v0) in enumerate(views):
                    if n >= 4:
                        pe.wait_ge(t_read[n % 2], (n - 4) // 2 + 1)
                    for i in range(4):
                        mm = pe.transpose(psT[:, n % 4, i * P:(i + 1) * P], pairs_bv[:, s, v0 + i, :], core.ident[:, :])
                    mm.then_inc(t_full, 1)
                pe.wait_ge(loaded, 32)
                with pe.Fori(0, B // 2) as i:
                    for u in range(2):
                        t = 2 * i + u
                        pe.wait_ge(att_ready, t + 1)
                        for c in range(DC):
                            mm = pe.transpose(psA[:, u, c * P:(c + 1) * P], xcur[:, u, c * P:(c + 1) * P], core.ident[:, :])
                        mm.then_inc(a_full, 1)
                    for u in range(2):
                        pe.wait_ge(a_read, 2 * i + u + 1)
                        pe.matmul(psO[:, u, 0:D], core.ones[0:1, :], bo[:, :], start=True, stop=False)
                        for c in range(DC):
                            mm = pe.matmul(psO[:, u, 0:D], aT[:, u, c, :], wo[:, c, :], start=False, stop=c == DC - 1)
                        mm.then_inc(o_full, 1)


MIDS_HALF = (0.25, 0.75, 1.25, 1.75)
MIDS_ONE = (2.5, 3.5)
MID_TWO = 5.0
FP4_BLOCK = 16


class Fp4:

    def __init__(self, sb, name, width):
        self.width, self.n = width, width // FP4_BLOCK
        self.mag = sb(f"{name}_mag", [P, width])
        self.half, self.one = sb(f"{name}_half", [P, width]), sb(f"{name}_one", [P, width])
        self.scale, self.inv = sb(f"{name}_scale", [P, self.n]), sb(f"{name}_inv", [P, self.n])

    def magnitude(self, act, x):
        return act.activation(self.mag[:, :], x, ACT.Abs)

    def steps(self, dve, chain, x, out):
        blocks = lambda a: a.rearrange("p (n k) -> p n k", k=FP4_BLOCK)
        wide = [P, self.n, FP4_BLOCK]
        mag, half, one = self.mag[:, :], self.half[:, :], self.one[:, :]
        chain.step(dve.tensor_reduce(self.scale[:, :], blocks(mag), AX.X, ALU.max))
        chain.step(dve.tensor_scalar(self.scale[:, :], self.scale[:, :], 1.0 / 6.0, 1e-12, ALU.mult, ALU.max))
        chain.step(dve.reciprocal(self.inv[:, :], self.scale[:, :]))
        chain.step(dve.tensor_tensor(blocks(mag), blocks(mag), self.inv[:, :].unsqueeze(2).to_broadcast(wide), ALU.mult))
        chain.step(dve.tensor_scalar(half, mag, MIDS_HALF[0], None, ALU.is_gt))
        for m in MIDS_HALF[1:]:
            chain.step(dve.scalar_tensor_tensor(out=half, in0=mag, scalar=m, in1=half, op0=ALU.is_gt, op1=ALU.add))
        chain.step(dve.tensor_scalar(one, mag, MID_TWO, 2.0, ALU.is_gt, ALU.mult))
        for m in MIDS_ONE:
            chain.step(dve.scalar_tensor_tensor(out=one, in0=mag, scalar=m, in1=one, op0=ALU.is_gt, op1=ALU.add))
        chain.step(dve.scalar_tensor_tensor(out=half, in0=half, scalar=0.5, in1=one, op0=ALU.mult, op1=ALU.add))
        chain.step(dve.scalar_tensor_tensor(out=half.bitcast(U32), in0=x.bitcast(U32), scalar=0x80000000, in1=half.bitcast(U32),
                                            op0=ALU.bitwise_and, op1=ALU.bitwise_or))
        return dve.tensor_tensor(blocks(out), blocks(half), self.scale[:, :].unsqueeze(2).to_broadcast(wide), ALU.mult)


def fp4_ffn(core):
    nc, ins, h = core.nc, core.ins, core.h
    I = 704
    IC = -(-I // P)
    IP = IC * P
    HALF = I // 2
    ctx, sb, ps, sem = stage(nc, "f4")
    with ctx:
        wT = sb("wT", [P, DC, 2 * IP])
        dT = sb("dT", [P, IC, D])
        ctx1, sb1, ps1, sem1 = stage(nc, "f4w")
        with ctx1:
            NP = 3
            raw = sb1("raw", [P, 2 * IC, D])
            raw_d = sb1("raw_d", [P, DC, IP])
            fq = Fp4(sb1, "q", IC * D)
            psT = ps1("t", [P, 4, 512])
            loaded, mag_done, rounded, chained = sem1("loaded"), sem1("mag_done"), sem1("rounded"), sem1("chained")
            t_full, t_read = sem1("t_full"), sem1("t_read")
            flat = lambda a: a.rearrange("p a b -> p (a b)")
            parts = [flat(raw[:, 0:IC, :]), flat(raw[:, IC:2 * IC, :]), flat(raw_d[:, :, :])]
            views = []
            for side in range(2):
                for c in range(DC):
                    for a in range(0, IC, 3):
                        views.append((side, [raw[:, side * IC + a + i, c * P:(c + 1) * P] for i in range(3)],
                                      wT[:, c, side * IP + a * P:side * IP + (a + 3) * P]))
            for j in range(0, IC, 2):
                views.append((2, [raw_d[:, c, (j + i) * P:(j + i + 1) * P] for i in range(2) for c in range(DC)],
                              flat(dT[:, j:j + 2, :])))
            block = ctx1.enter_context(nc.Block())

            @block.sync
            def _(sp):
                sp.dma_start(raw[:, 0:IC, :], ins["f4_gate"].rearrange("(a p) n -> p a n", p=P)).then_inc(loaded, 16)
                sp.dma_start(raw[:, IC:2 * IC, :], ins["f4_up"].rearrange("(a p) n -> p a n", p=P)).then_inc(loaded, 16)
                sp.dma_start(raw_d[:, :, :], ins["f4_down"].rearrange("(a p) n -> p a n", p=P)).then_inc(loaded, 16)

            @block.scalar
            def _(act):
                act.wait_ge(loaded, 48)
                for i, part in enumerate(parts):
                    if i:
                        act.wait_ge(rounded, i)
                    fq.magnitude(act, part).then_inc(mag_done, 1)
                for n, (_, srcs, dst) in enumerate(views):
                    act.wait_ge(t_full, n + 1)
                    act.copy(dst, psT[:, n % 4, 0:len(srcs) * P]).then_inc(t_read, 1)

            @block.vector
            def _(dve):
                chain = Chain(dve, chained)
                for i, part in enumerate(parts):
                    dve.wait_ge(mag_done, i + 1)
                    fq.steps(dve, chain, part, part).then_inc(rounded, 1)

            @block.tensor
            def _(pe):
                for n, (part, srcs, _) in enumerate(views):
                    pe.wait_ge(rounded, part + 1)
                    if n >= 4:
                        pe.wait_ge(t_read, n - 3)
                    for i, src in enumerate(srcs):
                        mm = pe.transpose(psT[:, n % 4, i * P:(i + 1) * P], src, core.ident[:, :])
                    mm.then_inc(t_full, 1)

        ctx2, sb2, ps2, sem2 = stage(nc, "f4t")
        with ctx2:
            norm = TokenNorm(core, sb2, sem2, h)
            xn, xq, xT = sb2("xn", [P, D]), sb2("xq", [P, D]), sb2("xT", [P, DC, P])
            gate, hid, hq, hT = sb2("gate", [P, I]), sb2("hid", [P, I]), sb2("hq", [P, IP]), sb2("hT", [P, IC, P])
            fx, fh = Fp4(sb2, "x", D), Fp4(sb2, "h", I)
            psX, psU, psH, psO = ps2("x", [P, 512]), ps2("u", [P, 4, 512]), ps2("h", [P, 2, 512]), ps2("o", [P, 512])
            names = ("xn_ready", "x_mag", "xq_ready", "x_full", "x_read", "gate_full", "up_full", "gate_read", "hid_ready",
                     "h_mag", "hq_ready", "h_full", "h_read", "o_full", "o_added", "padded", "chained")
            (xn_ready, x_mag, xq_ready, x_full, x_read, gate_full, up_full, gate_read, hid_ready,
             h_mag, hq_ready, h_full, h_read, o_full, o_added, padded, chained) = (sem2(n) for n in names)
            banks = lambda a: a.rearrange("p (j n) -> p j n", j=2)
            block = ctx2.enter_context(nc.Block())

            @block.gpsimd
            def _(pool):
                pool.memset(hq[:, I:IP], 0.0).then_inc(padded, 1)
                norm.rsqrt(pool)

            @block.vector
            def _(dve):
                chain = Chain(dve, chained)
                norm.stats(dve)
                dve.wait_ge(norm.rstd_done, 1)
                per_quant = 13

                def front(t, links):
                    norm.normalise(dve, xn[:, :], t).then_inc(xn_ready, 1)
                    dve.wait_ge(x_mag, t + 1)
                    chain.begin(links)
                    fx.steps(dve, chain, xn[:, :], xq[:, :]).then_inc(xq_ready, 1)
                    assert chain.count == per_quant

                def back(t, links):
                    dve.wait_ge(gate_read, t + 1)
                    dve.wait_ge(up_full, t + 1)
                    dve.tensor_tensor(banks(hid[:, :]), banks(gate[:, :]), psU[:, 2:4, 0:HALF], ALU.mult).then_inc(hid_ready, 1)
                    dve.wait_ge(h_mag, t + 1)
                    chain.begin(links)
                    fh.steps(dve, chain, hid[:, :], hq[:, 0:I]).then_inc(hq_ready, 1)
                    dve.wait_ge(o_full, t + 1)
                    dve.tensor_tensor(h[:, t, :], h[:, t, :], psO[:, 0:D], ALU.add).then_inc(o_added, 1)

                front(0, 0)
                with dve.Fori(0, B - 1) as t:
                    front(t + 1, (2 * t + 1) * per_quant)
                    back(t, (2 * t + 2) * per_quant)
                back(B - 1, (2 * B - 1) * per_quant)

            @block.scalar
            def _(act):
                def front(t):
                    act.wait_ge(xn_ready, t + 1)
                    fx.magnitude(act, xn[:, :]).then_inc(x_mag, 1)
                    act.wait_ge(x_full, t + 1)
                    act.copy(xT[:, :, :], psX[:, 0:D].rearrange("p (c t) -> p c t", c=DC)).then_inc(x_read, 1)

                def back(t):
                    act.wait_ge(hid_ready, t + 1)
                    fh.magnitude(act, hid[:, :]).then_inc(h_mag, 1)
                    act.wait_ge(h_full, t + 1)
                    for j in range(2):
                        a = act.copy(hT[:, 3 * j:3 * j + 3, :], psH[:, j, 0:3 * P].rearrange("p (c t) -> p c t", c=3))
                    a.then_inc(h_read, 1)

                def silu(t):
                    act.wait_ge(gate_full, t + 1)
                    act.activation(banks(gate[:, :]), psU[:, 0:2, 0:HALF], ACT.Silu).then_inc(gate_read, 1)

                front(0)
                silu(0)
                with act.Fori(0, B - 1) as t:
                    front(t + 1)
                    back(t)
                    silu(t + 1)
                back(B - 1)

            @block.tensor
            def _(pe):
                def front(t, again=True):
                    pe.wait_ge(xq_ready, t + 1)
                    for c in range(DC):
                        mm = pe.transpose(psX[:, c * P:(c + 1) * P], xq[:, c * P:(c + 1) * P], core.ident[:, :])
                    mm.then_inc(x_full, 1)
                    pe.wait_ge(x_read, t + 1)
                    if again:
                        pe.wait_ge(hid_ready, t)
                    for side, full in ((0, gate_full), (1, up_full)):
                        for j in range(2):
                            for c in range(DC):
                                mm = pe.matmul(psU[:, 2 * side + j, 0:HALF], xT[:, c, :],
                                               wT[:, c, side * IP + j * HALF:side * IP + (j + 1) * HALF], start=c == 0, stop=c == DC - 1)
                        mm.then_inc(full, 1)

                def back(t):
                    pe.wait_ge(hq_ready, t + 1)
                    for j in range(IC):
                        mm = pe.transpose(psH[:, j // 3, (j % 3) * P:(j % 3 + 1) * P], hq[:, j * P:(j + 1) * P], core.ident[:, :])
                    mm.then_inc(h_full, 1)
                    pe.wait_ge(h_read, t + 1)
                    if not isinstance(t, int) or t > 0:
                        pe.wait_ge(o_added, t)
                    for j in range(IC):
                        mm = pe.matmul(psO[:, 0:D], hT[:, j, :], dT[:, j, :], start=j == 0, stop=j == IC - 1)
                    mm.then_inc(o_full, 1)

                pe.wait_ge(padded, 1)
                front(0, False)
                with pe.Fori(0, B - 1) as t:
                    front(t + 1)
                    back(t)
                back(B - 1)


def layer2_block(core):
    with core.nc.sbuf_tensor("x0", [P, B, D], F32) as x0:
        delta_net(core, x0)
        mlp(core, x0)


def lm_tower(nc, ins, out):
    core = Core(nc, ins, out)
    ctx = ExitStack()
    with ctx:
        core.h = ctx.enter_context(nc.sbuf_tensor("h", [P, B, D], F32))
        core.ident = ctx.enter_context(nc.sbuf_tensor("ident", [P, P], F32))
        core.ident_bf = ctx.enter_context(nc.sbuf_tensor("ident_bf", [P, P], BF16))
        core.causal = ctx.enter_context(nc.sbuf_tensor("causal", [P, 4 * P], BF16))
        core.ones = ctx.enter_context(nc.sbuf_tensor("ones", [P, P], F32))
        core.minus_half = ctx.enter_context(nc.sbuf_tensor("minus_half", [P, 2 * B], F32))
        core.ones_bf = ctx.enter_context(nc.sbuf_tensor("ones_bf", [P, P], BF16))
        core.zeros = ctx.enter_context(nc.sbuf_tensor("zeros", [P, D], F32))
        core.rows_cleared = ctx.enter_context(nc.semaphore("rows_cleared"))
        slots = P * moe_tiles(4, 16)
        core.slot_rows = nc.dram_tensor("slot_rows", (slots, D), F32)
        core.slot_outputs = nc.dram_tensor("slot_outputs", (slots, D), F32)
        core.bias_parts = nc.dram_tensor("bias_parts", (3, 8 * (1024 + D)), BF16)
        stages = [lambda: embed(core), lambda: attention(core, "headnorm"), lambda: moe(core, "swiglu"), lambda: attention(core, "nd"),
                  lambda: moe(core, "gelu"), lambda: layer2_block(core), lambda: fp4_ffn(core), lambda: attention(core, "rel"), lambda: moe(core, "silu")]
        for run in stages:
            run()
        done = ctx.enter_context(nc.semaphore("out_done"))
        block = ctx.enter_context(nc.Block())

        @block.sync
        def _(sp):
            sp.dma_start(out.rearrange("b t d -> t b d"), core.h[:, :, :]).then_inc(done, 16)
            sp.wait_ge(done, 16)


def layouts(inputs):
    a = {k: np.ascontiguousarray(v) for k, v in inputs.items()}
    a["token_ids"] = np.ascontiguousarray(a.pop("x").T)
    a["ident"] = np.eye(P, dtype=np.float32)
    tri = np.where(np.arange(P)[:, None] >= np.arange(P)[None, :], 0.0, -1e30).astype(np.float32)
    a["causal"] = np.tile(tri, (1, 4))
    a["masked"] = np.full((16, P), -1e9, np.float32)

    def strips(w, width, strip):
        w = w.reshape(w.shape[0], -1, width)
        o = np.zeros((*w.shape[:2], strip), w.dtype)
        o[:, :, :width] = w
        return o.reshape(w.shape[0], -1)

    def by_partition(v, n):
        return np.ascontiguousarray(v.reshape(n, P).T)

    for s in ("q", "k"):
        a[f"L3_attn_W{s}_strips"] = strips(a.pop(f"L3_attn_W{s}"), 16, 32)
        a[f"L3_attn_b{s}_strips"] = by_partition(strips(a.pop(f"L3_attn_b{s}")[None], 16, 32), 4)
    a["L1_attn_Wq_strips"] = a.pop("L1_attn_Wq")
    a["L1_attn_Wk_strips"] = a.pop("L1_attn_Wk")
    a["L1_attn_bq_strips"] = by_partition(a.pop("L1_attn_bq"), 8)
    order = [8 * (s // 2) + 2 * c + s % 2 for c in range(4) for s in range(4)]
    for n in ("Wr", "br"):
        w = a.pop(f"L1_attn_{n}").reshape(-1, 16, 10)[:, order].reshape(-1, 160)
        a[f"L1_attn_{n}_strips"] = strips(w, 10, 32)
    a["L1_attn_br_strips"] = by_partition(a["L1_attn_br_strips"], 4)
    d = np.zeros((P, P), np.float32)
    rel = np.zeros((P, 2 * P), np.float32)
    b_nd, emb = a.pop("L1_attn_b_nd"), a.pop("L3_attn_rel_emb")
    mid = emb.shape[0] // 2
    for s in range(4):
        d[32 * s:32 * s + 10] = b_nd[:, 0:P][:, ::-1]
        rel[32 * s:32 * s + 16, 0:2 * P - 1] = emb[mid - P + 1:mid + P][::-1].T
    a["L1_attn_dist"], a["L3_attn_dist"] = d, rel

    def chunked_bias(v, n):
        return np.ascontiguousarray(v.reshape(v.shape[0], n, P).transpose(0, 2, 1))

    a["f0_w1"], a["f0_w2"] = a.pop("L0_ffn_gate_up_proj"), a.pop("L0_ffn_down_proj")
    a["f0_biases"] = np.concatenate([a.pop("L0_ffn_gate_up_bias"), a.pop("L0_ffn_down_bias")], axis=1).reshape(-1)
    a["f0_wr"], a["f0_rb"] = np.ascontiguousarray(a.pop("L0_ffn_router_weight").T), a.pop("L0_ffn_router_bias")
    a["f1_w1"], a["f1_w2"] = a.pop("L1_ffn_W1"), a.pop("L1_ffn_W2")
    a["f1_biases"] = np.concatenate([a.pop("L1_ffn_b1"), a.pop("L1_ffn_b2")], axis=1).reshape(-1)
    a["f1_wr"], a["f1_rb"] = a.pop("L1_ffn_Wr"), a.pop("L1_ffn_br")
    a["f2_w1"] = np.ascontiguousarray(a.pop("L2_attn_w1").reshape(D, 2, 512).transpose(1, 0, 2))
    a["f2_w2"], a["f2_b1"] = a.pop("L2_attn_w2").reshape(2, 512, D), chunked_bias(a.pop("L2_attn_b1").reshape(2, 512), 4)
    a["f2_ln1_g"], a["f2_ln1_b"] = by_partition(a.pop("L2_attn_ln1_g"), 2), by_partition(a.pop("L2_attn_ln1_b"), 2)
    pad = 6 * P - 704
    for n in ("gate", "up"):
        a[f"f4_{n}"] = np.pad(a.pop(f"L2_ffn_w_{n}"), ((0, pad), (0, 0)))
    a["f4_down"] = np.pad(a.pop("L2_ffn_w_down"), ((0, 0), (0, pad)))
    a["f2_b2"] = a.pop("L2_attn_b2")[None]
    a["f2_g"], a["f2_b"] = by_partition(a.pop("L2_attn_ln2_g"), 2), by_partition(a.pop("L2_attn_ln2_b"), 2)
    I3 = 352
    side = {}
    for n in ("gate", "up"):
        side[n] = np.concatenate([a.pop(f"L3_ffn_{n}_proj"), a.pop(f"L3_ffn_shared_{n}_w").reshape(2, I3, D)])
    a["f3_w1"] = np.concatenate([side["gate"].transpose(0, 2, 1), side["up"].transpose(0, 2, 1)], axis=2)
    down = np.concatenate([a.pop("L3_ffn_down_proj").transpose(0, 2, 1), a.pop("L3_ffn_shared_down_w").T.reshape(2, I3, D)])
    a["f3_w2"] = np.concatenate([down, np.zeros((18, 3 * P - I3, D), down.dtype)], axis=1)
    a["f3_wr"], a["f3_rb"] = np.ascontiguousarray(a.pop("L3_ffn_gate_w").T), a.pop("L3_ffn_gate_bias")
    a["before"] = (np.arange(P)[:, None] < np.arange(P)[None, :]).astype(np.float32)
    for n in (8, 16):
        a[f"earlier{n}"] = (np.arange(n)[:, None] > np.arange(n)[None, :]).astype(np.float32).reshape(-1)
    a["tile_starts"] = np.array([-1.0] + [P * j for j in range(1, B)], np.float32)
    a["tile_ids"] = np.arange(moe_tiles(4, 16), dtype=np.float32)[None]
    for n in (4, 8, 16):
        a[f"rank{n}"] = np.arange(n, 0, -1, dtype=np.float32)
    return a


def kernel(**inputs):
    from concourse import bacc
    from concourse.bass_utils import run_bass_kernel_spmd

    nc = bacc.Bacc("TRN2", target_bir_lowering=False, num_devices=1)
    arrays, ins = {}, {}
    for name, v in layouts(inputs).items():
        arrays["in_" + name] = v
        ins[name] = nc.dram_tensor("in_" + name, v.shape, mybir.dt.from_np(v.dtype), kind="ExternalInput").ap()
    out = nc.dram_tensor("out_0_dram", (B, P, D), F32, kind="ExternalOutput").ap()
    lm_tower(nc, ins, out)
    r = run_bass_kernel_spmd(nc, [arrays], core_ids=[0])
    return r.results[0]["out_0_dram"]
```

```python
from contextlib import ExitStack

import numpy as np

import concourse.bass as bass
import concourse.mybir as mybir

F32 = mybir.dt.float32
BF16 = mybir.dt.bfloat16
I32 = mybir.dt.int32
U32 = mybir.dt.uint32
ALU = mybir.AluOpType
ACT = mybir.ActivationFunctionType
AX = mybir.AxisListType

P = 128
B = 16
D = 256
DC = D // P
LN_EPS = 1e-5


class Core:

    def __init__(self, nc, ins, out):
        self.nc, self.ins, self.out = nc, ins, out


class Chain:

    def __init__(self, eng, sem):
        self.eng, self.sem, self.base, self.count = eng, sem, 0, 0

    def begin(self, base):
        self.base, self.count = base, 0

    def step(self, ins):
        ins.then_inc(self.sem, 1)
        self.count += 1
        self.eng.wait_ge(self.sem, self.base + self.count)


def stage(nc, name):
    ctx = ExitStack()
    sems = []

    def clear():
        if sems:
            nc.clear_and_free_semaphores(sems)
            nc.all_engine_barrier()

    ctx.callback(clear)

    def sb(label, shape, dt=F32):
        return ctx.enter_context(nc.sbuf_tensor(f"{name}_{label}", shape, dt))

    def ps(label, shape, dt=F32):
        return ctx.enter_context(nc.psum_tensor(f"{name}_{label}", shape, dt))

    def sem(label):
        sems.append(nc.alloc_semaphore(name=f"{name}_{label}"))
        return sems[-1]

    return ctx, sb, ps, sem


def embed(core):
    nc, ins = core.nc, core.ins
    ctx, sb, ps, sem = stage(nc, "embed")
    with ctx:
        ids = sb("ids", [P, B], I32)
        causal = sb("causal", [P, 4 * P])
        ids_in, rows_in, consts_in = sem("ids_in"), sem("rows_in"), sem("consts_in")
        block = ctx.enter_context(nc.Block())

        @block.sync
        def _(sp):
            sp.dma_start(ids[:, :], ins["token_ids"]).then_inc(ids_in, 16)
            sp.dma_start(core.ident[:, :], ins["ident"]).then_inc(consts_in, 16)
            sp.dma_start(causal[:, :], ins["causal"]).then_inc(consts_in, 16)
            sp.wait_ge(consts_in, 32)

        @block.gpsimd
        def _(pool):
            pool.memset(core.minus_half[:, :], -0.5)
            pool.memset(core.ones[:, :], 1.0)
            pool.memset(core.zeros[:, :], 0.0)
            pool.wait_ge(ids_in, 16)
            for b in range(B):
                pool.indirect_dma_start(
                    out=core.h[:, b, :], out_offset=None, in_=ins["L0_tok_weight"],
                    in_offset=bass.IndirectOffsetOnAxis(ap=ids[:, b:b + 1].bitcast(U32), axis=0),
                ).then_inc(rows_in, 16)
            pool.wait_ge(rows_in, 16 * B)

        @block.vector
        def _(dve):
            dve.wait_ge(consts_in, 32)
            dve.tensor_copy(core.ident_bf[:, :], core.ident[:, :])
            dve.tensor_copy(core.causal[:, :], causal[:, :])
            dve.memset(core.ones_bf[:, :], 1.0)


class TokenNorm:

    def __init__(self, core, sb, sem, src):
        self.core, self.src = core, src
        self.parts = sb("ln_parts", [P, B, 6])
        self.mv = sb("ln_mv", [P, B, 2])
        self.rstd = sb("ln_rstd", [P, B, 1])
        self.parts_done, self.var_done, self.eps_added, self.rstd_done = (sem(n) for n in ("ln_parts", "ln_var", "ln_eps", "ln_rstd"))

    def stats(self, dve, lo=0, hi=B):
        for b in range(lo, hi):
            dve.bn_stats(self.parts[:, b, :], self.src[:, b, :]).then_inc(self.parts_done, 1)
        dve.wait_ge(self.parts_done, hi)
        for b in range(lo, hi):
            dve.bn_aggr(self.mv[:, b, :], self.parts[:, b, :]).then_inc(self.var_done, 1)
        dve.wait_ge(self.var_done, hi)
        dve.tensor_scalar(self.rstd[:, lo:hi, 0], self.mv[:, lo:hi, 1], LN_EPS, None, ALU.add).then_inc(self.eps_added, 1)

    def rsqrt(self, pool, lo=0, hi=B):
        pool.wait_ge(self.eps_added, 1 + (lo > 0))
        pool.tensor_tensor(self.rstd[:, lo:hi, 0], self.rstd[:, lo:hi, 0], self.core.minus_half[:, lo:hi], ALU.pow).then_inc(self.rstd_done, 1)

    def normalise(self, dve, out, b):
        return dve.tensor_scalar(out, self.src[:, b, :], self.mv[:, b, 0:1], self.rstd[:, b, :], ALU.subtract, ALU.mult)


def attention(core, kind):
    nc, ins, h = core.nc, core.ins, core.h
    H = 16
    dh = 64 if kind == "nd" else 16
    strip = 64 if kind == "nd" else 32
    per = P // strip
    QC = H // per
    F = H * dh
    FC = F // P
    pre = {"headnorm": "L0_attn_", "nd": "L1_attn_", "rel": "L3_attn_"}[kind]
    nm = {"headnorm": "a0", "nd": "a1", "rel": "a3"}[kind]
    skewed = kind != "headnorm"
    GW = {"headnorm": 0, "nd": P, "rel": 2 * P}[kind]
    PITCH = 2 * P

    def place(head):
        c, s = head // per, head % per
        if kind == "nd":
            return 2 * (c // 4) + s, c % 4, s * strip, c
        return s, c, s * strip, c

    heads_of = {}
    for head in range(H):
        beta, slot, _, _ = place(head)
        heads_of[beta, slot] = head

    if kind == "headnorm":
        jobs = [("x", "act"), ("qk", "dve"), ("v", "act"), ("q", "act"), ("k", "act")]
    elif kind == "nd":
        jobs = [("x", "act"), ("r", "act"), ("q0", "act"), ("q1", "act"), ("k0", "act"), ("k1", "act")]
        jobs += [(f"g{i}", "act") for i in range(H * GW // 512)]
        jobs += [("v0", "act"), ("v1", "act")]
    else:
        jobs = [("x", "act"), ("q", "act"), ("k", "act")] + [(f"g{i}", "act") for i in range(H * GW // 512)]
        jobs += [("v", "act")]
    NF = len(jobs)
    names = [j[0] for j in jobs]
    NA = sum(j[1] == "act" for j in jobs)

    bank_of = {name: j % 2 for j, name in enumerate(names)}

    per_o = 512 // (dh + 1)
    o_jobs = [list(range(a, min(a + per_o, H))) for a in range(0, H, per_o)]
    t_jobs = [list(range(a, min(a + 4, FC))) for a in range(0, FC, 4)]
    NBK = len(o_jobs) + len(t_jobs) + 1

    ctx, sb, ps, sem = stage(nc, nm)
    with ctx:
        norm = TokenNorm(core, sb, sem, h)
        xn = sb("xn", [P, D])
        xT = sb("xT", [P, DC, P])
        qT = sb("qT", [P, QC, P])
        kT = sb("kT", [P, QC, P])
        va = sb("va", [P, H, dh + 1])
        prob = sb("prob", [P, 4, 512])
        probT = sb("probT", [P, 4, 512])
        top = sb("top", [P, H])
        inv = sb("inv", [P, H])
        o = sb("o", [P, F])
        oT = sb("oT", [P, FC, P])
        wo = sb("wo", [P, FC, D])
        bo = sb("bo", [1, D])
        wv = sb("wv", [P, DC, F])
        psS = ps("scores", [P, 4, 512])
        psF = ps("front", [P, 2, 512])
        psB = ps("back", [P, 2, 512])
        weights_in, late_weights_in = sem("weights_in"), sem("late_weights_in")
        xn_ready = sem("xn_ready")
        front_full = sem("front_full")
        front_act = sem("front_act")
        back_full = sem("back_full")
        back_read = sem("back_read")
        scores_full = sem("scores_full")
        shifted = sem("shifted")
        expd = sem("expd")
        probT_full = sem("probT_full")
        probT_read = sem("probT_read")
        ones_set = sem("ones_set")
        dve_chain = sem("dve_chain")
        n_weights = 3
        if kind == "headnorm":
            wqk = sb("wqk", [P, DC, 2 * F])
            qk = sb("qk", [P, 2 * H, 2 * dh])
            hsum = sb("hsum", [P, 2 * H])
            hvar = sb("hvar", [P, 2 * H])
            cen = sb("cen", [P, 2 * H, dh])
            sq = sb("sq", [P, 2 * H, dh])
            hw = sb("hw", [P, 2, dh])
            hb = sb("hb", [P, 2, dh])
            hv_done, hr_done, qk_ready = sem("hv_done"), sem("hr_done"), sem("qk_ready")
            n_weights += 5
        else:
            wq = sb("wq", [P, DC, QC * P])
            wk = sb("wk", [P, DC, QC * P])
            bq = sb("bq", [P, QC])
            g_sb = sb("g", [P, H, GW])
            e_sb = sb("e", [P, 4, 4, P])
            skew = nc.dram_tensor(f"{nm}_skew", [P, H, PITCH], F32, kind="Internal").ap()
            skew_read = bass.AP(skew.tensor, P - 1, [[H * PITCH - 1, P], [PITCH, H], [1, P]])
            g_out, e_in, g_set = sem("g_out"), sem("e_in"), sem("g_set")
            n_weights += 3
            dist = sb("dist", [P, GW])
            n_weights += 1
            if kind == "nd":
                wr = sb("wr", [P, DC, 4 * P])
                br = sb("br", [P, 4])
                rT = sb("rT", [P, 4, P])
                n_weights += 3
            else:
                bk = sb("bk", [P, QC])
                bv = sb("bv", [1, F])
                n_weights += 2

        block = ctx.enter_context(nc.Block())

        @block.sync
        def _(sp):
            n = 0

            def load(dst, src):
                nonlocal n
                n += 1
                sp.dma_start(dst, src).then_inc(weights_in, 16)

            def chunks(src):
                return src.rearrange("(c p) n -> p c n", p=P)

            if kind == "headnorm":
                load(wqk[:, :, 0:F], chunks(ins[pre + "Wq"]))
                load(wqk[:, :, F:2 * F], chunks(ins[pre + "Wk"]))
                for i, side in enumerate("qk"):
                    load(hw[:, i, :], ins[f"{pre}{side}ln_w"].partition_broadcast(P))
                load(hb[:, 0, :], ins[f"{pre}qln_b"].partition_broadcast(P))
                load(hb[:, 1, :], ins[f"{pre}kln_b"].partition_broadcast(P))
            else:
                if kind == "nd":
                    load(wr[:, :, :], chunks(ins[pre + "Wr_strips"]))
                    load(br[:, :], ins[pre + "br_strips"])
                load(wq[:, :, :], chunks(ins[pre + "Wq_strips"]))
                load(wk[:, :, :], chunks(ins[pre + "Wk_strips"]))
                load(bq[:, :], ins[pre + "bq_strips"])
                load(dist[:, :], ins[pre + "dist"])
                if kind == "nd":
                    load(skew[:, :, P:PITCH], ins["masked"].partition_broadcast(P))
                else:
                    load(bk[:, :], ins[pre + "bk_strips"])
                    load(bv[:, :], ins[pre + "bv"].unsqueeze(0))
            core.n_weights = n
            sp.dma_start(wv[:, :, :], chunks(ins[pre + "Wv"])).then_inc(late_weights_in, 16)
            sp.dma_start(wo[:, :, :], chunks(ins[pre + ("Wproj" if kind == "nd" else "Wo")])).then_inc(late_weights_in, 16)
            sp.dma_start(bo[:, :], ins[pre + ("bproj" if kind == "nd" else "bo")].unsqueeze(0)).then_inc(late_weights_in, 16)
            if kind == "headnorm":
                sp.wait_ge(late_weights_in, 48)
                rows = core.slot_rows.ap().rearrange("(n p) d -> p n d", p=P)
                sp.dma_start(rows, core.zeros[:, :].unsqueeze(1).to_broadcast([P, rows.shape[1], D])).then_inc(core.rows_cleared, 16)
            if skewed:
                last_g = names.index(f"g{H * GW // 512 - 1}")
                def skewing(t):
                    if isinstance(t, int):
                        tables, loads = t * NA + last_g + 1, 16 * t + 16
                    else:
                        tables, loads = sp.to_reg(t * NA + last_g + 1), sp.to_reg(16 * t + 16)
                        previous, read = sp.to_reg(4 * t), sp.to_reg(16 * t)
                        sp.wait_ge(e_in, read)
                        sp.wait_ge(shifted, previous)
                    sp.wait_ge(front_act, tables)
                    sp.dma_start(skew[:, :, 0:GW], g_sb[:, :, :]).then_inc(g_out, 16)
                    sp.wait_ge(g_out, loads)
                    if isinstance(t, int):
                        sp.wait_ge(weights_in, 16 * n)
                    sp.dma_start(e_sb[:, :, :, :].rearrange("p b a k -> p (b a) k"), skew_read).then_inc(e_in, 16)

                skewing(0)
                with sp.Fori(1, B) as t:
                    skewing(t)
                sp.wait_ge(e_in, 16 * B)

        n_weights = core.n_weights

        @block.gpsimd
        def _(pool):
            pool.memset(va[:, :, dh:dh + 1], 1.0).then_inc(ones_set, 1)
            if kind == "headnorm":
                pool.memset(qk[:, :, :], 0.0).then_inc(ones_set, 1)
            norm.rsqrt(pool, 0, 2)
            if kind != "headnorm":
                norm.rsqrt(pool, 2)
            else:
                def head_rsqrt(t):
                    pool.wait_ge(hv_done, t + 1)
                    pool.tensor_tensor(hvar[:, :], hvar[:, :], core.minus_half[:, 0:2 * H], ALU.pow).then_inc(hr_done, 1)

                head_rsqrt(0)
                norm.rsqrt(pool, 2)
                with pool.Fori(1, B) as t:
                    head_rsqrt(t)

        @block.scalar
        def _(act):
            na = 0

            def front_read(t, name, out, **kw):
                j = names.index(name)
                act.wait_ge(front_full, t * NF + j + 1)
                return psF[:, bank_of[name], :]

            def done(i):
                i.then_inc(front_act, 1)

            def copy_x(t):
                src = front_read(t, "x", None)
                done(act.copy(xT[:, :, :], src[:, 0:D].rearrange("p (c t) -> p c t", c=DC)))

            def values_used(t):
                if not isinstance(t, int) or t > 0:
                    act.wait_ge(back_full, t * NBK + (len(o_jobs) - NBK))

            def copy_v(t, i=0):
                src = front_read(t, f"v{i}" if kind == "nd" else "v", None)
                if i == 0:
                    values_used(t)
                if kind == "nd":
                    done(act.copy(va[:, 8 * i:8 * i + 8, 0:dh], src.rearrange("p (a d) -> p a d", d=dh)))
                else:
                    done(act.copy(va[:, :, 0:dh], src[:, 0:F].rearrange("p (a d) -> p a d", d=dh)))

            def with_bias(out, src, b):
                for c in range(4):
                    ins_ = act.activation(out[:, c, :], src[:, c * P:(c + 1) * P], ACT.Identity, bias=b[:, c:c + 1])
                done(ins_)

            def copy_side(t, name):
                src = front_read(t, name, None)
                side, at = name[0], 4 * int(name[1:] or 0)
                dst = {"q": qT, "k": kT, "r": rT if kind == "nd" else None}[side][:, at:at + 4, :]
                b = None
                if skewed and (side != "k" or kind == "rel"):
                    b = {"q": bq, "k": bk if kind == "rel" else None, "r": br if kind == "nd" else None}[side][:, at:at + 4]
                if b is None:
                    done(act.copy(dst, src.rearrange("p (c t) -> p c t", c=4)))
                else:
                    with_bias(dst, src, b)

            def copy_g(t, i):
                if i == 0 and (not isinstance(t, int) or t > 0):
                    act.wait_ge(g_out, 16 * t)
                src = front_read(t, f"g{i}", None)
                hp = 512 // GW
                done(act.copy(g_sb[:, hp * i:hp * i + hp, :], src.rearrange("p (a d) -> p a d", d=GW)))

            def exp(t, beta):
                act.wait_ge(shifted, 4 * t + beta + 1)
                act.activation(prob[:, beta, :], prob[:, beta, :], ACT.Exp,
                               scale=1.0 if skewed else float(dh) ** -0.5).then_inc(expd, 1)

            def copy_pT(t):
                for beta in range(4):
                    act.wait_ge(probT_full, 4 * t + beta + 1)
                    act.copy(probT[:, beta, :], psS[:, beta, :]).then_inc(probT_read, 1)

            def front(t, before):
                def exp_before(beta):
                    if before is not None:
                        exp(before, beta)

                if kind == "nd":
                    for name in ("r", "q0", "q1"):
                        copy_side(t, name)
                    exp_before(0)
                    copy_side(t, "k0")
                    exp_before(1)
                    copy_side(t, "k1")
                    exp_before(2)
                    copy_g(t, 0)
                    exp_before(3)
                    for i in range(1, H * GW // 512):
                        copy_g(t, i)
                elif kind == "rel":
                    for name in ("q", "k"):
                        copy_side(t, name)
                    for i in range(H * GW // 512):
                        copy_g(t, i)
                        if i % 2 == 0:
                            exp_before(i // 2)
                else:
                    for beta in range(4):
                        exp_before(beta)

            act.wait_ge(weights_in, 16 * n_weights)
            act.wait_ge(ones_set, 1 + (kind == "headnorm"))
            copy_x(0)
            front(0, None)
            copy_v(0)
            if kind == "nd":
                copy_v(0, 1)
            if not skewed:
                copy_side(0, "q")
                copy_side(0, "k")
            copy_x(1)

            def turn(t, more, more2):
                if more:
                    front(t + 1, t)
                else:
                    for beta in range(4):
                        exp(t, beta)
                copy_pT(t)
                if more:
                    copy_v(t + 1)
                    if kind == "nd":
                        copy_v(t + 1, 1)
                    if not skewed:
                        copy_side(t + 1, "q")
                        copy_side(t + 1, "k")
                if more2:
                    copy_x(t + 2)

            turn(0, True, True)
            with act.Fori(1, B - 2) as t:
                turn(t, True, True)
            turn(B - 2, True, False)
            turn(B - 1, False, False)

        @block.tensor
        def _(pe):
            def front_bank(t, name):
                j = names.index(name)
                bank = bank_of[name]
                prior = [i for i in range(j) if bank_of[names[i]] == bank]
                tt = t
                if not prior:
                    if isinstance(t, int) and t == 0:
                        return psF[:, bank, :]
                    prior = [i for i in range(NF) if bank_of[names[i]] == bank]
                    tt = t - 1
                p = prior[-1]
                if jobs[p][1] == "act":
                    n = sum(jobs[i][1] == "act" for i in range(p + 1))
                    pe.wait_ge(front_act, tt * NA + n)
                else:
                    pe.wait_ge(qk_ready, tt + 1)
                return psF[:, bank, :]

            def evacuated(t, name):
                j = names.index(name)
                n = sum(jobs[i][1] == "act" for i in range(j + 1))
                pe.wait_ge(front_act, t * NA + n)

            def front_x(t):
                bank = front_bank(t, "x")
                pe.wait_ge(xn_ready, t + 1)
                for c in range(DC):
                    mm = pe.transpose(bank[:, c * P:(c + 1) * P], xn[:, c * P:(c + 1) * P], core.ident[:, :])
                mm.then_inc(front_full, 1)

            def front_qk(t):
                evacuated(t, "x")
                if kind == "headnorm":
                    bank = front_bank(t, "qk")
                    for c in range(DC):
                        mm = pe.matmul(bank, xT[:, c, :], wqk[:, c, :], start=c == 0, stop=c == DC - 1)
                    mm.then_inc(front_full, 1)
                    return
                todo = ([("r", wr, 1)] if kind == "nd" else []) + [("q", wq, QC // 4), ("k", wk, QC // 4)]
                for side, w, n in todo:
                    for i in range(n):
                        bank = front_bank(t, side if n == 1 else f"{side}{i}")
                        for m in range(4):
                            for c in range(DC):
                                mm = pe.matmul(bank[:, m * P:(m + 1) * P], w[:, c, (4 * i + m) * P:(4 * i + m + 1) * P],
                                               xT[:, c, :], start=c == 0, stop=c == DC - 1)
                        mm.then_inc(front_full, 1)

            def front_g(t):
                hp = 512 // GW
                evacuated(t, "r" if kind == "nd" else "q")
                for i in range(H // hp):
                    bank = front_bank(t, f"g{i}")
                    for a in range(hp):
                        s, c = (hp * i + a) // 4, (hp * i + a) % 4
                        lhs = (rT if kind == "nd" else qT)[32 * s:32 * s + 16, c, :]
                        mm = pe.matmul(bank[:, a * GW:(a + 1) * GW], lhs, dist[32 * s:32 * s + 16, :], start=True, stop=True)
                    mm.then_inc(front_full, 1)

            def front_qkT(t):
                pe.wait_ge(qk_ready, t + 1)
                for i, name in enumerate(("q", "k")):
                    bank = front_bank(t, name)
                    for c in range(4):
                        src = qk[:, i * H + 4 * c:i * H + 4 * c + 4, :].rearrange("p a d -> p (a d)")
                        mm = pe.transpose(bank[:, c * P:(c + 1) * P], src, core.ident[:, :])
                    mm.then_inc(front_full, 1)

            def front_v(t, i=0):
                n = 2 if kind == "nd" else 1
                w = F // n
                bank = front_bank(t, "v" if n == 1 else f"v{i}")
                for c in range(DC):
                    mm = pe.matmul(bank[:, 0:w], xT[:, c, :], wv[:, c, i * w:(i + 1) * w], start=c == 0,
                                   stop=c == DC - 1 and kind != "rel")
                if kind == "rel":
                    mm = pe.matmul(bank[:, 0:w], core.ones[0:1, :], bv[:, :], start=False, stop=True)
                mm.then_inc(front_full, 1)

            def scores(t):
                evacuated(t, names[NF - 1])
                if not isinstance(t, int) or t > 0:
                    pe.wait_ge(probT_read, 4 * t + 1)
                for beta in range(4):
                    if kind == "headnorm":
                        pe.matmul(psS[:, beta, :], core.ident_bf[:, :], core.causal[:, :], start=True, stop=False)
                    for slot in range(4):
                        head = heads_of[beta, slot]
                        _, _, s0, c = place(head)
                        mm = pe.matmul(psS[:, beta, slot * P:(slot + 1) * P], qT[s0:s0 + dh, c, :], kT[s0:s0 + dh, c, :],
                                       start=kind != "headnorm", stop=slot == 3 or kind != "headnorm")
                    mm.then_inc(scores_full, 1)

            def weightsT(t):
                for beta in range(4):
                    pe.wait_ge(expd, 4 * t + beta + 1)
                    for slot in range(4):
                        mm = pe.transpose(psS[:, beta, slot * P:(slot + 1) * P], prob[:, beta, slot * P:(slot + 1) * P],
                                          core.ident[:, :])
                    mm.then_inc(probT_full, 1)

            def back_bank(t, j):
                if j >= 2:
                    pe.wait_ge(back_read, t * NBK + j)
                elif not isinstance(t, int) or t > 0:
                    pe.wait_ge(back_read, t * NBK + 1)
                return psB[:, j % 2, :]

            def values(t):
                for n, hs in enumerate(o_jobs):
                    bank = back_bank(t, n)
                    for i, head in enumerate(hs):
                        beta, slot, _, _ = place(head)
                        if n == 0 and i == 0:
                            pe.wait_ge(probT_read, 4 * t + 5)
                        mm = pe.matmul(bank[:, i * (dh + 1):(i + 1) * (dh + 1)], probT[:, beta, slot * P:(slot + 1) * P],
                                       va[:, head, :], start=True, stop=True)
                    mm.then_inc(back_full, 1)

            def outputsT(t):
                for n, cs in enumerate(t_jobs):
                    j = len(o_jobs) + n
                    bank = back_bank(t, j)
                    pe.wait_ge(back_read, t * NBK + len(o_jobs) + 1)
                    for i, c in enumerate(cs):
                        mm = pe.transpose(bank[:, i * P:(i + 1) * P], o[:, c * P:(c + 1) * P], core.ident[:, :])
                    mm.then_inc(back_full, 1)

            def project(t):
                bank = back_bank(t, NBK - 1)
                pe.wait_ge(back_read, t * NBK + NBK)
                pe.matmul(bank[:, 0:D], core.ones[0:1, :], bo[:, :], start=True, stop=False)
                for c in range(FC):
                    mm = pe.matmul(bank[:, 0:D], oT[:, c, :], wo[:, c, :], start=False, stop=c == FC - 1)
                mm.then_inc(back_full, 1)

            pe.sem_inc(probT_read, 1)
            pe.sem_inc(back_read, 1)
            pe.wait_ge(weights_in, 16 * n_weights)
            front_x(0)
            front_qk(0)
            if skewed:
                front_g(0)
            pe.wait_ge(late_weights_in, 48)
            front_v(0)
            if kind == "nd":
                front_v(0, 1)
            if not skewed:
                front_qkT(0)
            front_x(1)

            def turn(t, first, more, more2):
                if more and not skewed:
                    front_qk(t + 1)
                scores(t)
                if more and skewed:
                    front_qk(t + 1)
                if not first:
                    project(t - 1)
                if more and skewed:
                    front_g(t + 1)
                weightsT(t)
                if more:
                    front_v(t + 1)
                values(t)
                if more:
                    if kind == "nd":
                        front_v(t + 1, 1)
                    if not skewed:
                        front_qkT(t + 1)
                if more2:
                    front_x(t + 2)
                outputsT(t)

            turn(0, True, True, True)
            with pe.Fori(1, B - 2) as t:
                turn(t, False, True, True)
            turn(B - 2, False, True, False)
            turn(B - 1, False, False, False)
            project(B - 1)

        @block.vector
        def _(dve):
            chain = Chain(dve, dve_chain)
            norm.stats(dve, 0, 2)
            if kind == "headnorm":
                dve.wait_ge(ones_set, 2)
                dve.wait_ge(weights_in, 16 * n_weights)

            def normal(t):
                norm.normalise(dve, xn[:, :], t).then_inc(xn_ready, 1)

            def head_stats(t):
                dve.wait_ge(front_full, t * NF + 2)
                src = psF[:, 1, :].rearrange("p (a d) -> p a d", d=dh)
                chain.step(dve.tensor_reduce(hsum[:, :], src, AX.X, ALU.add))
                chain.step(dve.tensor_scalar(hsum[:, :], hsum[:, :], 1.0 / dh, None, ALU.mult))
                chain.step(dve.tensor_tensor(cen[:, :, :], src, hsum[:, :].unsqueeze(2).to_broadcast([P, 2 * H, dh]), ALU.subtract))
                chain.step(dve.tensor_tensor(sq[:, :, :], cen[:, :, :], cen[:, :, :], ALU.mult))
                chain.step(dve.tensor_reduce(hvar[:, :], sq[:, :, :], AX.X, ALU.add))
                dve.tensor_scalar(hvar[:, :], hvar[:, :], 1.0 / dh, LN_EPS, ALU.mult, ALU.add).then_inc(hv_done, 1)

            def head_norm(t):
                dve.wait_ge(hr_done, t + 1)
                chain.step(dve.tensor_tensor(cen[:, :, :], cen[:, :, :], hvar[:, :].unsqueeze(2).to_broadcast([P, 2 * H, dh]), ALU.mult))
                for i in range(2):
                    c2 = cen[:, i * H:(i + 1) * H, :]
                    ins_ = dve.tensor_tensor(sq[:, i * H:(i + 1) * H, :], c2, hw[:, i:i + 1, :].to_broadcast([P, H, dh]), ALU.mult)
                chain.step(ins_)
                for i in range(2):
                    ins_ = dve.tensor_tensor(qk[:, i * H:(i + 1) * H, 0:dh], sq[:, i * H:(i + 1) * H, :],
                                             hb[:, i:i + 1, :].to_broadcast([P, H, dh]), ALU.add)
                ins_.then_inc(qk_ready, 1)

            def shift(t, beta):
                dve.wait_ge(scores_full, 4 * t + beta + 1)
                if beta == 0 and skewed:
                    dve.wait_ge(e_in, 16 * (t + 1))
                src = psS[:, beta, :].rearrange("p (a k) -> p a k", k=P)
                dst = prob[:, beta, :].rearrange("p (a k) -> p a k", k=P)
                tp = top[:, 4 * beta:4 * beta + 4]
                if skewed:
                    scale = float(dh) ** -0.5
                    chain.step(dve.scalar_tensor_tensor(out=dst, in0=src, scalar=scale, in1=e_sb[:, beta, :, :],
                                                        op0=ALU.mult, op1=ALU.add))
                    src = dst
                chain.step(dve.tensor_reduce(tp, src, AX.X, ALU.max))
                dve.tensor_tensor(dst, src, tp.unsqueeze(2).to_broadcast([P, 4, P]), ALU.subtract).then_inc(shifted, 1)

            def outputs(t):
                for n, hs in enumerate(o_jobs):
                    dve.wait_ge(back_full, t * NBK + n + 1)
                    src = psB[:, n % 2, 0:len(hs) * (dh + 1)].rearrange("p (a d) -> p a d", d=dh + 1)
                    iv = inv[:, hs[0]:hs[-1] + 1]
                    chain.step(dve.reciprocal(iv, src[:, :, dh]))
                    dve.tensor_tensor(o[:, hs[0] * dh:(hs[-1] + 1) * dh].rearrange("p (a d) -> p a d", d=dh),
                                      src[:, :, 0:dh], iv.unsqueeze(2).to_broadcast([P, len(hs), dh]),
                                      ALU.mult).then_inc(back_read, 1)

            def copy_oT(t):
                for n, cs in enumerate(t_jobs):
                    j = len(o_jobs) + n
                    dve.wait_ge(back_full, t * NBK + j + 1)
                    dve.tensor_copy(oT[:, cs[0]:cs[-1] + 1, :],
                                    psB[:, j % 2, 0:len(cs) * P].rearrange("p (a d) -> p a d", d=P)).then_inc(back_read, 1)

            def add(t):
                dve.wait_ge(back_full, t * NBK + NBK)
                dve.tensor_tensor(h[:, t, :], h[:, t, :], psB[:, (NBK - 1) % 2, 0:D], ALU.add).then_inc(back_read, 1)

            dve.wait_ge(norm.rstd_done, 1)
            normal(0)
            if skewed:
                norm.stats(dve, 2)
            dve.wait_ge(front_full, 1)
            normal(1)
            if not skewed:
                head_stats(0)
                norm.stats(dve, 2)
                head_norm(0)
            dve.wait_ge(norm.rstd_done, 2)
            dve.wait_ge(front_full, NF + 1)
            first = chain.count
            steps = {"headnorm": 4 + 7 + 1, "nd": 8 + 3, "rel": 8 + 1}[kind]

            def turn(t, again, more, more2):
                chain.begin(t * steps + first)
                if more and not skewed:
                    head_stats(t + 1)
                shift(t, 0)
                if more2:
                    normal(t + 2)
                for beta in range(1, 4):
                    shift(t, beta)
                if again:
                    add(t - 1)
                if more and not skewed:
                    head_norm(t + 1)
                outputs(t)
                copy_oT(t)
                assert chain.count == steps or not more

            turn(0, False, True, True)
            with dve.Fori(1, B - 2) as t:
                turn(t, True, True, True)
            turn(B - 2, True, True, False)
            turn(B - 1, True, False, False)
            add(B - 1)


def pick_first(dve, chain, score, best, mask, tmp, rank, groups, n):
    wide = [P, groups, n]
    chain.step(dve.tensor_reduce(best, score, AX.X, ALU.max))
    chain.step(dve.tensor_tensor(tmp, score, best.unsqueeze(2).to_broadcast(wide), ALU.is_equal))
    chain.step(dve.tensor_tensor(tmp, tmp, rank, ALU.mult))
    chain.step(dve.tensor_reduce(best, tmp, AX.X, ALU.max))
    chain.step(dve.tensor_tensor(mask, tmp, best.unsqueeze(2).to_broadcast(wide), ALU.is_equal))


def pick_masks(dve, chain, score, masks, K, best, tmp, rank, E):
    for k in range(K):
        pick_first(dve, chain, score, best, masks[:, k, :, :], tmp, rank, B, E)
        if k < K - 1:
            chain.step(dve.scalar_tensor_tensor(out=score, in0=masks[:, k, :, :], scalar=-1e30, in1=score, op0=ALU.mult, op1=ALU.add))


def pick_weights(dve, chain, score, masks, w, K, tmp):
    for k in range(K):
        chain.step(dve.tensor_tensor(tmp, masks[:, k, :, :], score, ALU.mult))
        chain.step(dve.tensor_reduce(w[:, :, k], tmp, AX.X, ALU.add))


def route_softmax(dve, act_exp, chain, logits, masks, w, bufs, K, E):
    wide = [P, B, E]
    score, tmp, best, rank, tot = bufs
    chain.step(dve.tensor_reduce(best, logits, AX.X, ALU.max))
    act_exp(dve.tensor_tensor(score, logits, best.unsqueeze(2).to_broadcast(wide), ALU.subtract))
    chain.step(dve.tensor_reduce(tot, score, AX.X, ALU.add))
    chain.step(dve.reciprocal(tot, tot))
    chain.step(dve.tensor_tensor(score, score, tot.unsqueeze(2).to_broadcast(wide), ALU.mult))
    if K == 1:
        pick_masks(dve, chain, logits, masks, K, best, tmp, rank, E)
    else:
        chain.step(dve.tensor_copy(logits, score))
        pick_masks(dve, chain, logits, masks, K, best, tmp, rank, E)
    pick_weights(dve, chain, score, masks, w, K, tmp)


def route_grouped(dve, act_sigmoid, chain, logits, masks, w, bufs, K, E, bias, small):
    G = 4
    N = E // G
    wide, grouped = [P, B, E], [P, B * G, N]
    score, tmp, best, rank, tot = bufs
    mask, sfc, rank4, gbest, gsum, gmask, gtmp, gpick = small
    by_group = lambda a: a.rearrange("p b (g n) -> p (b g) n", n=N)
    act_sigmoid(dve.tensor_copy(score, logits))
    chain.step(dve.tensor_tensor(sfc, score, bias.unsqueeze(1).to_broadcast(wide), ALU.add))
    chain.step(dve.tensor_reduce(gsum, by_group(sfc), AX.X, ALU.max))
    pick_first(dve, chain, by_group(sfc), gbest, by_group(mask), by_group(tmp), rank4.to_broadcast(grouped), B * G, N)
    chain.step(dve.scalar_tensor_tensor(out=tmp, in0=mask, scalar=-1e30, in1=sfc, op0=ALU.mult, op1=ALU.add))
    chain.step(dve.tensor_reduce(gbest, by_group(tmp), AX.X, ALU.max))
    chain.step(dve.tensor_tensor(gsum, gsum, gbest, ALU.add))
    per_row = lambda a: a.rearrange("p (b g) -> p b g", g=G)
    pick_first(dve, chain, per_row(gsum), tot, per_row(gmask), per_row(gtmp), rank4.to_broadcast([P, B, G]), B, G)
    chain.step(dve.scalar_tensor_tensor(out=gsum, in0=gmask, scalar=-1e30, in1=gsum, op0=ALU.mult, op1=ALU.add))
    pick_first(dve, chain, per_row(gsum), tot, per_row(gpick), per_row(gtmp), rank4.to_broadcast([P, B, G]), B, G)
    chain.step(dve.tensor_tensor(gmask, gmask, gpick, ALU.add))
    chain.step(dve.tensor_tensor(by_group(sfc), by_group(sfc), gmask.unsqueeze(2).to_broadcast(grouped), ALU.mult))
    pick_masks(dve, chain, sfc, masks, K, best, tmp, rank, E)
    pick_weights(dve, chain, score, masks, w, K, tmp)
    chain.step(dve.tensor_reduce(tot, w, AX.X, ALU.add))
    chain.step(dve.tensor_scalar(tot, tot, 1e-20, None, ALU.add))
    chain.step(dve.reciprocal(tot, tot))
    chain.step(dve.tensor_tensor(w, w, tot.unsqueeze(2).to_broadcast([P, B, K]), ALU.mult))


def moe_tiles(K, E):
    return E + (B * P * K - 1) // P


def moe(core, kind):
    nc, ins, h = core.nc, core.ins, core.h
    nm = {"swiglu": "f0", "gelu": "f1", "silu": "f3"}[kind]
    E = {"swiglu": 8, "gelu": 8, "silu": 16}[kind]
    K = {"swiglu": 2, "gelu": 1, "silu": 4}[kind]
    I = {"swiglu": 256, "gelu": 1024, "silu": 352}[kind]
    ES = 2 if kind == "silu" else 0
    gated = kind != "gelu"
    biased = kind != "silu"
    W1 = 2 * I if gated else I
    NI = -(-I // P)
    width = [min(P, I - j * P) for j in range(NI)]
    NT = moe_tiles(K, E)
    if NT % 2 == 0:
        NT += 1
    banks = {"swiglu": [(0, 512)], "gelu": [(0, 512), (512, 1024)], "silu": [(0, I), (I, 2 * I)]}[kind]
    xd, yd = core.slot_rows.ap(), core.slot_outputs.ap()

    ctx, sb, ps, sem = stage(nc, nm)
    with ctx:
        norm = TokenNorm(core, sb, sem, h)
        up_w = sb("up_w", [P, E + ES // 2, DC, W1])
        down_w = sb("down_w", [P, E + ES // 2, NI, D])
        xn = sb("xn", [P, B, D])
        xTr = sb("xTr", [P, 2, DC, P])
        wr, r_b, rank = sb("wr", [P, DC, E]), sb("r_b", [P, E]), sb("rank", [P, 1, E])
        before, earlier, thr = sb("before", [P, P]), sb("earlier", [P, E, E]), sb("thr", [P, 1, 16])
        tile_id = sb("tile_id", [1, NT, 1])
        consts = [(wr[:, :, :], ins[nm + "_wr"].rearrange("(c p) n -> p c n", p=P)),
                  (r_b[:, :], ins[nm + "_rb"].partition_broadcast(P)),
                  (rank[:, 0, :], ins[f"rank{E}"].partition_broadcast(P)),
                  (before[:, :], ins["before"]),
                  (earlier[:, :, :].rearrange("p a b -> p (a b)"), ins[f"earlier{E}"].partition_broadcast(P)),
                  (thr[:, 0, :], ins["tile_starts"].partition_broadcast(P)),
                  (tile_id[:, :, 0], ins["tile_ids"][:, 0:NT])]
        logits, score, tmp = (sb(n_, [P, B, E]) for n_ in ("logits", "score", "tmp"))
        hT = sb("hT", [P, NI, P])
        y = sb("y", [P, 2, D])
        yg = sb("yg", [P, 2 * K, D])
        lent_hT, lent_y = hT[:, :, :].rearrange("p n t -> p (n t)"), y[:, :, :].rearrange("p u d -> p (u d)")
        lent_yg = yg[:, :, :].rearrange("p k d -> p (k d)")
        masks = lent_yg[:, 0:K * B * E].rearrange("p (k b e) -> p k b e", k=K, b=B)
        best, tot = sb("best", [P, B]), sb("tot", [P, B])
        wts = sb("wts", [P, B, K, 1])
        w3 = wts[:, :, :, 0]
        bufs = [score[:, :, :], tmp[:, :, :], best[:, :], rank[:, :, :].to_broadcast([P, B, E]), tot[:, :]]
        if kind == "silu":
            rank4 = sb("rank4", [P, 1, 4])
            consts.append((rank4[:, 0, :], ins["rank4"].partition_broadcast(P)))
            small = [lent_y[:, u * B * E:(u + 1) * B * E].rearrange("p (b e) -> p b e", e=E) for u in range(2)] + [rank4[:, :, :]]
            small += [sb(n_, [P, B * 4])[:, :] for n_ in ("gbest", "gsum", "gmask", "gtmp", "gpick")]
        earlier_tiles = sb("earlier_tiles", [P, B + 1, E])
        tiles, start = sb("tiles", [P, E]), sb("start", [P, 1, E])
        tiles_cmp = lent_hT[:, 0:E * 16].rearrange("p (e n) -> p e n", e=E)
        start_cmp = lent_hT[:, 0:E * E].rearrange("p (e n) -> p e n", e=E)
        slot_f, slot = sb("slot_f", [P, B, K]), sb("slot", [P, B, K], I32)
        eid_cmp = lent_yg[0:1, 0:NT * E].rearrange("p (n e) -> p n e", e=E)
        eid_f, eid = sb("eid_f", [1, NT]), sb("eid", [1, NT], I32)
        xs = xTr[:, :, :, :].rearrange("p u c t -> p u (c t)")
        xT = sb("xT", [P, DC, P])
        hid = sb("hid", [P, I])
        if gated:
            gate = sb("gate", [P, I])
        if kind == "swiglu":
            clip = sb("clip", [P, 2 * I])
        if biased:
            NB = E * (W1 + D) // P
            b_f, b_parts, bias = sb("b_f", [P, NB]), sb("b_parts", [P, 3, NB], BF16), sb("bias", [3, E, W1 + D], BF16)
        sets = 2 if kind == "swiglu" else 1
        psU = ps("up_ps", [P, max(2, sets * len(banks)), 512])
        psH = ps("hT_ps", [P, -(-NI // 4), 4, P])
        psX = ps("x", [P, 512])
        psY = ps("y_ps", [P, 512])
        psL = ps("logits_ps", [P, 512])

        consts_in, xn_ready = sem("consts_in"), sem("xn_ready")
        xTr_full, xTr_read, logits_full = sem("xTr_full"), sem("xTr_read"), sem("logits_full")
        routed, act_done, dve_chain = sem("routed"), sem("act_done"), sem("dve_chain")
        picks_ready, ranks_full, slots_ready, eid_ready = sem("picks_ready"), sem("ranks_full"), sem("slots_ready"), sem("eid_ready")
        w_in = [sem(f"w_in{e}") for e in range(E + ES)]
        w_ready = sem("w_ready")
        scattered = sem("scattered")
        x_in = [sem("x_in0"), sem("x_in1")]
        xT_full, xT_ready, up_full, act_full, hid_ready = sem("xT_full"), sem("xT_ready"), sem("up_full"), sem("act_full"), sem("hid_ready")
        hT_full, hT_ready, y_full, y_ready = sem("hT_full"), sem("hT_ready"), sem("y_full"), sem("y_ready")
        clip_chain = sem("clip_chain")
        stored = [sem("stored0"), sem("stored1")]
        gathered = [sem("gathered0"), sem("gathered1")]
        pick_added, added = sem("pick_added"), sem("added")
        bias_raw, bias_split, bias_out, bias_in = sem("bias_raw"), sem("bias_split"), sem("bias_out"), sem("bias_in")

        phases = [("routed", 0, NT)]
        if ES:
            phases = [("before", 0, B), ("routed", B, NT), ("after", B + NT, B)]

        block = ctx.enter_context(nc.Block())

        @block.sync
        def _(sp):
            for dst, s in consts:
                sp.dma_start(dst, s).then_inc(consts_in, 16)
            if biased:
                sp.dma_start(b_f[:, :], ins[nm + "_biases"].rearrange("(p n) -> p n", p=P)).then_inc(bias_raw, 16)
                flat = core.bias_parts.ap()[:, 0:P * NB]
                sp.wait_ge(bias_split, 1)
                for k in range(3):
                    sp.dma_start(flat[k].rearrange("(p n) -> p n", p=P), b_parts[:, k, :]).then_inc(bias_out, 16)
                sp.wait_ge(bias_out, 48)
                sp.dma_start(bias[:, :, :].rearrange("k e n -> k (e n)"), flat).then_inc(bias_in, 16)
            for name, base, count in phases:
                def load(n, par):
                    if not (isinstance(n, int) and base + n < 2):
                        sp.wait_ge(xT_full, n + (base - 1))
                    src = xd[bass.ts(n, P), :] if name == "routed" else xn[:, n, :]
                    sp.dma_start(xs[:, par, :], src).then_inc(x_in[par], 16)

                def store(n, par):
                    if name == "routed":
                        sp.wait_ge(y_ready, n + (base + 1))
                        sp.dma_start(yd[bass.ts(n, P), :], y[:, par, :]).then_inc(stored[par], 16)

                if name == "routed":
                    sp.wait_ge(scattered, 16 * B * K)
                elif name == "before":
                    sp.wait_ge(logits_full, B)
                for n in range(4):
                    load(n, n % 2)
                pairs = (count - 4) // 2
                with sp.Fori(0, pairs) as i:
                    for u in range(2):
                        load(2 * i + (u + 4), u)
                        store(2 * i + u, u)
                for n in range(2 * pairs + 4, count):
                    load(n, n % 2)
                for n in range(2 * pairs, count):
                    store(n, n % 2)
                if name == "before":
                    sp.wait_ge(y_full, B)
                    sp.dma_start(up_w[:, E, :, :], ins[nm + "_w1"][E + 1].rearrange("(c p) n -> p c n", p=P)).then_inc(w_in[E + 1], 16)
                    sp.dma_start(down_w[:, E, :, :], ins[nm + "_w2"][E + 1].rearrange("(c p) n -> p c n", p=P)).then_inc(w_in[E + 1], 16)

        @block.gpsimd
        def _(pool):
            norm.rsqrt(pool, 0, 4)
            norm.rsqrt(pool, 4)
            pool.wait_ge(core.rows_cleared, 16)
            pool.wait_ge(slots_ready, 1)
            for b in range(B):
                for k in range(K):
                    pool.indirect_dma_start(
                        out=xd[0:NT * P, :], out_offset=bass.IndirectOffsetOnAxis(ap=slot[:, b, k:k + 1].bitcast(U32), axis=0),
                        in_=xn[:, b, :], in_offset=None,
                    ).then_inc(scattered, 16)
            for e in range(E):
                pool.wait_ge(w_in[e], 32)
                pool.sem_inc(w_ready, 1)
            pool.sem_inc(w_ready, NT)
            pool.wait_ge(stored[0], 16 * ((NT + 1) // 2 + 1))
            pool.wait_ge(stored[1], 16 * (NT // 2 + 1))
            for b in range(B):
                if b >= 2:
                    pool.wait_ge(added, b - 1)
                for k in range(K):
                    pool.indirect_dma_start(
                        out=yg[:, (b % 2) * K + k, :], out_offset=None, in_=yd[0:NT * P, :],
                        in_offset=bass.IndirectOffsetOnAxis(ap=slot[:, b, k:k + 1].bitcast(U32), axis=0),
                    ).then_inc(gathered[b % 2], 16)

        @block.scalar
        def _(act):
            act.wait_ge(consts_in, 16 * len(consts))
            if biased:
                act.wait_ge(bias_raw, 16)
            order = list(range(E, E + ES // 2)) + list(range(E))
            for e in order:
                act.dma_start(up_w[:, e, :, :], ins[nm + "_w1"][e].rearrange("(c p) n -> p c n", p=P)).then_inc(w_in[e], 16)
                act.dma_start(down_w[:, e, :, :], ins[nm + "_w2"][e].rearrange("(c p) n -> p c n", p=P)).then_inc(w_in[e], 16)
            for i in range(B // 2):
                for u in range(2):
                    act.wait_ge(xTr_full, 2 * i + (u + 1))
                    act.copy(xTr[:, u, :, :], psU[:, u, 0:D].rearrange("p (c t) -> p c t", c=DC)).then_inc(xTr_read, 1)
            act.sem_inc(stored[0], 16)
            act.sem_inc(stored[1], 16)
            act.wait_ge(routed, 1)
            act.activation(score[:, :, :], score[:, :, :], ACT.Sigmoid if kind == "silu" else ACT.Exp).then_inc(act_done, 1)

            def xcopy(n):
                act.wait_ge(xT_full, n + 1)
                act.copy(xT[:, :, :], psX[:, 0:D].rearrange("p (c t) -> p c t", c=DC)).then_inc(xT_ready, 1)

            def hidden(n, par):
                if kind == "gelu":
                    act.wait_ge(up_full, n + 1)
                    for c, (lo, hi) in enumerate(banks):
                        i_ = act.activation(hid[:, lo:hi], psU[:, c, :], ACT.Gelu)
                    i_.then_inc(hid_ready, 1)
                elif kind == "swiglu":
                    act.wait_ge(clip_chain, 3 * n + 1)
                    act.activation(gate[:, :], clip[:, 0:I], ACT.Sigmoid, scale=1.702).then_inc(act_full, 1)
                else:
                    act.wait_ge(up_full, n + 1)
                    act.activation(gate[:, :], psU[:, 0, 0:I], ACT.Silu).then_inc(act_full, 1)

            for name, base, count in phases:
                xcopy(base)
                hidden(base, 0)
                xcopy(base + 1)

                def turn(n, par, has_next, has_second):
                    if has_second and kind == "swiglu":
                        xcopy(n + (base + 2))
                    if has_next:
                        hidden(n + (base + 1), 1 - par)
                    if has_second and kind != "swiglu":
                        xcopy(n + (base + 2))
                    if name == "routed":
                        act.wait_ge(y_full, n + (base + 1))
                        act.wait_ge(stored[par], 16 * ((n - par) // 2 + 1) if isinstance(n, int) else store_count[0])
                        act.copy(y[:, par, :], psY[:, 0:D]).then_inc(y_ready, 1)

                turn(0, 0, True, True)
                pairs = (count - 3) // 2
                with act.Fori(0, pairs) as i:
                    for u in range(2):
                        store_count = [16 * (i + (u + 1))]
                        turn(2 * i + (1 + u), (1 + u) % 2, True, True)
                for n in range(1 + 2 * pairs, count):
                    turn(n, n % 2, n + 1 < count, n + 2 < count)

        @block.tensor
        def _(pe):
            pe.wait_ge(consts_in, 16 * len(consts))

            def rows(t, u):
                pe.wait_ge(xn_ready, t + 1)
                for c in range(DC):
                    mm = pe.transpose(psU[:, u, c * P:(c + 1) * P], xn[:, t, c * P:(c + 1) * P], core.ident[:, :])
                mm.then_inc(xTr_full, 1)

            for t in range(2):
                rows(t, t)
            for t in range(B):
                pe.wait_ge(xTr_read, t + 1)
                for c in range(DC):
                    mm = pe.matmul(psL[:, t * E:(t + 1) * E], xTr[:, t % 2, c, :], wr[:, c, :], start=c == 0, stop=c == DC - 1)
                mm.then_inc(logits_full, 1)
                if t + 2 < B:
                    rows(t + 2, t % 2)
            pe.wait_ge(picks_ready, 1)
            picks = tmp[:, :, :].rearrange("p b e -> p (b e)")
            pe.matmul(psL[:, 0:B * E], before[:, :], picks, start=True, stop=True)
            pe.matmul(psL[:, B * E:2 * B * E], core.ones[:, :], picks, start=True, stop=True).then_inc(ranks_full, 1)

            loaded = [0, 0]
            for name, base, count in phases:
                def expert(n):
                    if name == "before":
                        return E
                    if name == "after":
                        return E
                    return pe.value_load(eid[0:1, n:n + 1] if isinstance(n, int) else eid[0:1, bass.ts(n, 1)], min_val=0, max_val=E - 1)

                def tr_x(n, par):
                    pe.wait_ge(x_in[par], 16 * (n // 2 + 1 + loaded[par]) if isinstance(n, int) else x_count[0])
                    if not (isinstance(n, int) and n + base < 1):
                        pe.wait_ge(xT_ready, n + base)
                    for c in range(DC):
                        mm = pe.transpose(psX[:, c * P:(c + 1) * P], xs[:, par, c * P:(c + 1) * P], core.ident[:, :])
                    mm.then_inc(xT_full, 1)

                def up(n, par, e):
                    if name == "routed":
                        pe.wait_ge(w_ready, n + 1)
                    pe.wait_ge(xT_ready, n + (base + 1))
                    for b, (lo, hi) in enumerate(banks):
                        out = psU[:, (par % sets) * len(banks) + b, 0:hi - lo]
                        if biased:
                            pe.matmul(out, core.ones_bf[0:3, :], bias[:, e, lo:hi], start=True, stop=False)
                        for c in range(DC):
                            mm = pe.matmul(out, xT[:, c, :], up_w[:, e, c, lo:hi], start=c == 0 and not biased, stop=c == DC - 1)
                    mm.then_inc(up_full, 1)

                def tr_h(n):
                    pe.wait_ge(hid_ready, n + (base + 1))
                    for j, m in enumerate(width):
                        mm = pe.transpose(psH[0:m, j // 4, j % 4, :], hid[:, j * P:j * P + m], core.ident[:, :])
                    mm.then_inc(hT_full, 1)

                def down(n, e):
                    pe.wait_ge(hT_ready, n + (base + 1))
                    if not (isinstance(n, int) and n + base < 1):
                        pe.wait_ge(y_ready, n + base)
                    if biased:
                        pe.matmul(psY[:, 0:D], core.ones_bf[0:3, :], bias[:, e, W1:W1 + D], start=True, stop=False)
                    for j, m in enumerate(width):
                        mm = pe.matmul(psY[:, 0:D], hT[0:m, j, :], down_w[0:m, e, j, :], start=j == 0 and not biased, stop=j == NI - 1)
                    mm.then_inc(y_full, 1)

                if name == "before":
                    pe.wait_ge(w_in[E], 32)
                elif name == "after":
                    pe.wait_ge(w_in[E + 1], 32)
                else:
                    pe.wait_ge(eid_ready, 1)
                    if biased:
                        pe.wait_ge(bias_in, 16)
                tr_x(0, 0)
                up(0, 0, expert(0))
                tr_x(1, 1)

                def turn(n, par, has_next, has_second):
                    if sets == 2:
                        if has_next:
                            up(n + 1, 1 - par, expert(n + 1))
                        tr_h(n)
                        if has_second:
                            tr_x(n + 2, par)
                        down(n, expert(n))
                        return
                    e, e_next = expert(n), expert(n + 1) if has_next else None
                    tr_h(n)
                    if has_next:
                        up(n + 1, 1 - par, e_next)
                    if has_second:
                        tr_x(n + 2, par)
                    down(n, e)

                turn(0, 0, True, True)
                pairs = (count - 3) // 2
                with pe.Fori(0, pairs) as i:
                    for u in range(2):
                        x_count = [16 * (i + (u + 2 + loaded[(1 + u) % 2]))]
                        turn(2 * i + (1 + u), (1 + u) % 2, True, True)
                for n in range(1 + 2 * pairs, count):
                    turn(n, n % 2, n + 1 < count, n + 2 < count)
                loaded = [loaded[0] + (count + 1) // 2, loaded[1] + count // 2]

        @block.vector
        def _(dve):
            chain = Chain(dve, dve_chain)
            norm.stats(dve, 0, 4)
            dve.wait_ge(norm.rstd_done, 1)
            for t in range(B):
                if t == 4:
                    norm.stats(dve, 4)
                    dve.wait_ge(norm.rstd_done, 2)
                norm.normalise(dve, xn[:, t, :], t).then_inc(xn_ready, 1)
            if biased:
                dve.wait_ge(bias_raw, 16)
                for k in range(3):
                    chain.step(dve.tensor_copy(b_parts[:, k, :], b_f[:, :]))
                    if k < 2:
                        chain.step(dve.tensor_tensor(b_f[:, :], b_f[:, :], b_parts[:, k, :], ALU.subtract))
                dve.sem_inc(bias_split, 1)
            dve.wait_ge(consts_in, 16 * len(consts))
            dve.wait_ge(logits_full, B)
            ps_l = psL[:, 0:B * E].rearrange("p (b e) -> p b e", e=E)

            def by_act(last):
                last.then_inc(routed, 1)
                dve.wait_ge(act_done, 1)

            if kind == "silu":
                chain.step(dve.tensor_copy(logits[:, :, :], ps_l))
                route_grouped(dve, by_act, chain, logits[:, :, :], masks, w3, bufs, K, E, r_b[:, :], small)
            else:
                chain.step(dve.tensor_tensor(logits[:, :, :], ps_l, r_b[:, :].unsqueeze(1).to_broadcast([P, B, E]), ALU.add))
                route_softmax(dve, by_act, chain, logits[:, :, :], masks, w3, bufs, K, E)
            last = dve.tensor_copy(tmp[:, :, :], masks[:, 0, :, :])
            for k in range(1, K):
                chain.step(last)
                last = dve.tensor_tensor(tmp[:, :, :], tmp[:, :, :], masks[:, k, :, :], ALU.add)
            last.then_inc(picks_ready, 1)
            dve.wait_ge(ranks_full, 1)
            ps_t = psL[:, B * E:2 * B * E].rearrange("p (b e) -> p b e", e=E)
            chain.step(dve.memset(earlier_tiles[:, 0, :], 0.0))
            for b in range(B):
                chain.step(dve.tensor_tensor(earlier_tiles[:, b + 1, :], earlier_tiles[:, b, :], ps_t[:, b, :], ALU.add))
            chain.step(dve.tensor_tensor(tiles_cmp[:, :, :], earlier_tiles[:, B, :].unsqueeze(2).to_broadcast([P, E, 16]),
                                         thr[:, :, :].to_broadcast([P, E, 16]), ALU.is_gt))
            chain.step(dve.tensor_reduce(tiles[:, :], tiles_cmp[:, :, :], AX.X, ALU.add))
            chain.step(dve.tensor_tensor(start_cmp[:, :, :], earlier[:, :, :], tiles[:, :].unsqueeze(1).to_broadcast([P, E, E]), ALU.mult))
            chain.step(dve.tensor_reduce(start[:, 0, :], start_cmp[:, :, :], AX.X, ALU.add))
            chain.step(dve.tensor_tensor(score[:, :, :], earlier_tiles[:, 0:B, :], ps_l, ALU.add))
            chain.step(dve.scalar_tensor_tensor(out=score[:, :, :], in0=start[:, :, :].to_broadcast([P, B, E]), scalar=float(P),
                                                in1=score[:, :, :], op0=ALU.mult, op1=ALU.add))
            for k in range(K):
                chain.step(dve.tensor_tensor(tmp[:, :, :], masks[:, k, :, :], score[:, :, :], ALU.mult))
                chain.step(dve.tensor_reduce(slot_f[:, :, k], tmp[:, :, :], AX.X, ALU.add))
            dve.tensor_copy(slot[:, :, :], slot_f[:, :, :]).then_inc(slots_ready, 1)
            chain.step(dve.tensor_tensor(eid_cmp[:, :, :], tile_id[:, :, :].to_broadcast([1, NT, E]), start[0:1, :, :].to_broadcast([1, NT, E]), ALU.is_ge))
            chain.step(dve.tensor_reduce(eid_f[:, :], eid_cmp[:, :, :], AX.X, ALU.add))
            dve.tensor_scalar(eid[:, :], eid_f[:, :], -1.0, None, ALU.add).then_inc(eid_ready, 1)

            def combine(b, par, turn_of_pair):
                dve.wait_ge(gathered[par], turn_of_pair)
                for k in range(K):
                    i_ = dve.scalar_tensor_tensor(out=h[:, b, :], in0=yg[:, par * K + k, :], scalar=wts[:, b, k, :],
                                                  in1=h[:, b, :], op0=ALU.mult, op1=ALU.add)
                    if k < K - 1:
                        i_.then_inc(pick_added, 1)
                        dve.wait_ge(pick_added, b * (K - 1) + (k + 1))
                i_.then_inc(added, 1)

            for name, base, count in phases:
                def hidden(n, par):
                    n = n + base
                    if kind == "swiglu":
                        dve.wait_ge(up_full, n + 1)
                        dve.tensor_scalar(clip[:, 0:I], psU[:, par, 0:I], 7.0, None, ALU.min).then_inc(clip_chain, 1)
                        dve.tensor_scalar(clip[:, I:2 * I], psU[:, par, I:2 * I], 7.0, -7.0, ALU.min, ALU.max).then_inc(clip_chain, 1)
                        dve.wait_ge(act_full, n + 1)
                        dve.wait_ge(clip_chain, 3 * n + 2)
                        dve.tensor_tensor(gate[:, :], gate[:, :], clip[:, 0:I], ALU.mult).then_inc(clip_chain, 1)
                        dve.wait_ge(clip_chain, 3 * n + 3)
                        dve.scalar_tensor_tensor(out=hid[:, :], in0=clip[:, I:2 * I], scalar=1.0, in1=gate[:, :],
                                                 op0=ALU.add, op1=ALU.mult).then_inc(hid_ready, 1)
                    elif kind == "silu":
                        dve.wait_ge(act_full, n + 1)
                        dve.tensor_tensor(hid[:, :], gate[:, :], psU[:, 1, 0:I], ALU.mult).then_inc(hid_ready, 1)

                hidden(0, 0)

                def turn(n, par, has_next, has_second):
                    dve.wait_ge(hT_full, n + (base + 1))
                    full = sum(m == P for m in width)
                    for c in range(-(-full // 4)):
                        lo, hi = 4 * c, min(4 * c + 4, full)
                        i_ = dve.tensor_scalar(hT[:, lo:hi, :], psH[:, c, 0:hi - lo, :], 1.0, None, ALU.mult)
                    if full < NI:
                        i_ = dve.tensor_scalar(hT[0:width[-1], full, :], psH[0:width[-1], full // 4, full % 4, :], 1.0, None, ALU.mult)
                    i_.then_inc(hT_ready, 1)
                    if has_next:
                        hidden(n + 1, 1 - par)
                    if name != "routed":
                        dve.wait_ge(y_full, n + (base + 1))
                        dve.tensor_tensor(h[:, n, :], h[:, n, :], psY[:, 0:D], ALU.add).then_inc(y_ready, 1)
                    if name == "after":
                        dve.wait_ge(y_ready, n + (base + 1))
                        combine(n, par, 16 * K * (n // 2 + 1) if isinstance(n, int) else pair_count[0])

                turn(0, 0, True, True)
                pairs = (count - 3) // 2
                with dve.Fori(0, pairs) as i:
                    for u in range(2):
                        pair_count = [16 * K * (i + (u + 1))]
                        turn(2 * i + (1 + u), (1 + u) % 2, True, True)
                for n in range(1 + 2 * pairs, count):
                    turn(n, n % 2, n + 1 < count, n + 2 < count)
            if phases[-1][0] == "routed":
                with dve.Fori(0, B // 2) as i:
                    for u in range(2):
                        combine(2 * i + u, u, 16 * K * (i + 1))
            dve.wait_ge(added, B)


MIDS_HALF = (0.25, 0.75, 1.25, 1.75)
MIDS_ONE = (2.5, 3.5)
MID_TWO = 5.0
FP4_BLOCK = 16


class Fp4:

    def __init__(self, sb, name, width):
        self.width, self.n = width, width // FP4_BLOCK
        self.mag = sb(f"{name}_mag", [P, width])
        self.half, self.one = sb(f"{name}_half", [P, width]), sb(f"{name}_one", [P, width])
        self.scale, self.inv = sb(f"{name}_scale", [P, self.n]), sb(f"{name}_inv", [P, self.n])

    def magnitude(self, act, x):
        return act.activation(self.mag[:, :], x, ACT.Abs)

    def magnitude_of_bits(self, dve, x):
        return dve.tensor_scalar(self.mag[:, :].bitcast(U32), x.bitcast(U32), 0x7fffffff, None, ALU.bitwise_and)

    def steps(self, dve, chain, x, out):
        last = None
        for n in range(self.STEPS):
            last = self.step(dve, n, x, out)
            if n < self.STEPS - 1:
                chain.step(last)
        return last

    STEPS = 4 + len(MIDS_HALF) + 1 + len(MIDS_ONE) + 3

    def step(self, dve, n, x, out):
        blocks = lambda a: a.rearrange("p (n k) -> p n k", k=FP4_BLOCK)
        wide = [P, self.n, FP4_BLOCK]
        mag, half, one = self.mag[:, :], self.half[:, :], self.one[:, :]
        first_half, first_one = 4, 4 + len(MIDS_HALF)
        last_one = first_one + 1 + len(MIDS_ONE)
        if n == 0:
            return dve.tensor_reduce(self.scale[:, :], blocks(mag), AX.X, ALU.max)
        if n == 1:
            return dve.tensor_scalar(self.scale[:, :], self.scale[:, :], 1.0 / 6.0, 1e-12, ALU.mult, ALU.max)
        if n == 2:
            return dve.reciprocal(self.inv[:, :], self.scale[:, :])
        if n == 3:
            return dve.tensor_tensor(blocks(mag), blocks(mag), self.inv[:, :].unsqueeze(2).to_broadcast(wide), ALU.mult)
        if n == first_half:
            return dve.tensor_scalar(half, mag, MIDS_HALF[0], None, ALU.is_gt)
        if n < first_one:
            return dve.scalar_tensor_tensor(out=half, in0=mag, scalar=MIDS_HALF[n - first_half], in1=half, op0=ALU.is_gt, op1=ALU.add)
        if n == first_one:
            return dve.tensor_scalar(one, mag, MID_TWO, 2.0, ALU.is_gt, ALU.mult)
        if n < last_one:
            return dve.scalar_tensor_tensor(out=one, in0=mag, scalar=MIDS_ONE[n - first_one - 1], in1=one, op0=ALU.is_gt, op1=ALU.add)
        if n == last_one:
            return dve.scalar_tensor_tensor(out=half, in0=half, scalar=0.5, in1=one, op0=ALU.mult, op1=ALU.add)
        if n == last_one + 1:
            return dve.scalar_tensor_tensor(out=half.bitcast(U32), in0=x.bitcast(U32), scalar=0x80000000, in1=half.bitcast(U32),
                                            op0=ALU.bitwise_and, op1=ALU.bitwise_or)
        return dve.tensor_tensor(blocks(out), blocks(half), self.scale[:, :].unsqueeze(2).to_broadcast(wide), ALU.mult)


class Fp4Weights:
    I = 704
    IC = -(-I // P)
    IP = IC * P
    PARTS = 6

    def __init__(self, core, ctx):
        self.ins = core.ins
        self.raw = ctx.enter_context(core.nc.sbuf_tensor("f4_raw", [P, 2 * self.IC, D], F32))
        self.raw_d = ctx.enter_context(core.nc.sbuf_tensor("f4_raw_d", [P, DC, self.IP], F32))

    def parts(self):
        half = self.IC // 2
        out = []
        for side, name in enumerate(("f4_gate", "f4_up")):
            src = self.ins[name].rearrange("(a p) n -> p a n", p=P)
            for at in (0, half):
                out.append((self.raw[:, side * self.IC + at:side * self.IC + at + half, :], src[:, at:at + half, :]))
        src = self.ins["f4_down"].rearrange("(a p) n -> p a n", p=P)
        for c in range(DC):
            out.append((self.raw_d[:, c:c + 1, :], src[:, c:c + 1, :]))
        return out


def mlp(core, src, fp4_weights):
    nc, ins, h = core.nc, core.ins, core.h
    nm, E, I, G = "f2", 2, 512, 4
    w1, w2 = ins[nm + "_w1"], ins[nm + "_w2"]
    NI = I // P
    TG = B // G
    N = TG * P

    ctx, sb, ps, sem = stage(nc, nm)
    with ctx:
        norm = TokenNorm(core, sb, sem, src)
        xn = sb("xn", [P, 2, D])
        xT = sb("xT", [P, DC, B * P])
        hid = sb("hid", [P, 2, NI, N])
        up_w = sb("up_w", [P, E, DC, I])
        down_w = sb("down_w", [P, E, NI, D])
        up_b = sb("up_b", [P, E, NI])
        b2 = sb("b2", [P, D])
        psU = ps("up_ps", [P, 4, 512])
        psD = ps("down_ps", [P, 4, 512])
        xn_ready, x_full, x_read = sem("xn_ready"), sem("x_full"), sem("x_read")
        w_in, b2_in = sem("w_in"), sem("b2_in")
        up_full, hid_ready, down_full, h_added = sem("up_full"), sem("hid_ready"), sem("down_full"), sem("h_added")
        b_added = sem("b_added")
        gam, bet = sb("gam", [P, DC]), sb("bet", [P, DC])
        loads = [(gam[:, :], ins[nm + "_g"]), (bet[:, :], ins[nm + "_b"])]
        for e in range(E):
            loads += [(up_w[:, e, :, :], w1[e].rearrange("(c p) n -> p c n", p=P)),
                      (down_w[:, e, :, :], w2[e].rearrange("(c p) n -> p c n", p=P)), (up_b[:, e, :], ins[nm + "_b1"][e])]
        units = [(e, g) for e in range(E) for g in range(G)]
        fq = Fp4(sb, "q", Fp4Weights.IC // 2 * D)
        f4_in, f4_chain = sem("f4_in"), sem("f4_chain")
        f4_parts = fp4_weights.parts()
        flat = lambda a: a.rearrange("p a b -> p (a b)")
        block = ctx.enter_context(nc.Block())

        @block.sync
        def _(sp):
            sp.dma_start(b2[:, :], ins[nm + "_b2"][0].partition_broadcast(P)).then_inc(b2_in, 16)
            for dst, s in loads:
                sp.dma_start(dst, s).then_inc(w_in, 16)
            for dst, s in f4_parts:
                sp.dma_start(dst, s).then_inc(f4_in, 16)

        @block.gpsimd
        def _(pool):
            norm.rsqrt(pool, 0, 4)
            norm.rsqrt(pool, 4)
            pool.wait_ge(b2_in, 16)
            for b in range(B):
                pool.tensor_tensor(h[:, b, :], h[:, b, :], b2[:, :], ALU.add).then_inc(b_added, 1)

        @block.scalar
        def _(act):
            act.wait_ge(w_in, 16 * len(loads))
            for n, (e, g) in enumerate(units):
                for j in range(NI):
                    act.wait_ge(up_full, n * NI + j + 1)
                    act.activation(hid[:, n % 2, j, :], psU[:, (n * NI + j) % 4, :], ACT.Gelu, bias=up_b[:, e, j:j + 1]).then_inc(hid_ready, 1)

        @block.tensor
        def _(pe):
            for t in range(B):
                pe.wait_ge(xn_ready, t + 1)
                if t >= 2:
                    pe.wait_ge(x_read, t - 1)
                for c in range(DC):
                    mm = pe.transpose(psD[:, t % 2, c * P:(c + 1) * P], xn[:, t % 2, c * P:(c + 1) * P], core.ident[:, :])
                mm.then_inc(x_full, 1)
            pe.wait_ge(w_in, 16 * len(loads))
            pe.wait_ge(x_read, B)

            def up(n):
                e, g = units[n]
                for j in range(NI):
                    p = n * NI + j
                    if p >= 4:
                        pe.wait_ge(hid_ready, p - 3)
                    for c in range(DC):
                        mm = pe.matmul(psU[:, p % 4, :], up_w[:, e, c, j * P:(j + 1) * P], xT[:, c, g * N:(g + 1) * N],
                                       start=c == 0, stop=c == DC - 1)
                    mm.then_inc(up_full, 1)

            def down(n):
                e, g = units[n]
                pe.wait_ge(hid_ready, (n + 1) * NI)
                for k in range(TG):
                    if n:
                        pe.wait_ge(h_added, 4 * (n - 1) + k + 1)
                    for j in range(NI):
                        mm = pe.matmul(psD[:, k, 0:D], hid[:, n % 2, j, k * P:(k + 1) * P], down_w[:, e, j, :],
                                       start=j == 0, stop=j == NI - 1)
                    mm.then_inc(down_full, 1)

            up(0)
            for n in range(len(units)):
                if n + 1 < len(units):
                    up(n + 1)
                down(n)

        @block.vector
        def _(dve):
            norm.stats(dve, 0, 4)
            norm.stats(dve, 4)
            dve.wait_ge(w_in, 16 * len(loads))
            dve.wait_ge(norm.rstd_done, 1)
            for t in range(B + 1):
                if t == 4:
                    dve.wait_ge(norm.rstd_done, 2)
                if t < B:
                    if t >= 2:
                        dve.wait_ge(x_full, t - 1)
                    norm.normalise(dve, xn[:, t % 2, :], t).then_inc(xn_ready, 1)
                if t > 0:
                    dve.wait_ge(x_full, t)
                    for c in range(DC):
                        i_ = dve.tensor_scalar(xT[:, c, (t - 1) * P:t * P], psD[:, (t - 1) % 2, c * P:(c + 1) * P], gam[:, c:c + 1], bet[:, c:c + 1],
                                               ALU.mult, ALU.add)
                    i_.then_inc(x_read, 1)
            dve.wait_ge(b_added, B)
            f4_steps = Chain(dve, f4_chain)
            for n, (e, g) in enumerate(units):
                for k in range(TG):
                    dve.wait_ge(down_full, 4 * n + k + 1)
                    t = g * TG + k
                    if n >= G:
                        dve.wait_ge(h_added, 4 * (n - G) + k + 1)
                    dve.tensor_tensor(h[:, t, :], h[:, t, :], psD[:, k, 0:D], ALU.add).then_inc(h_added, 1)
                if n < len(f4_parts):
                    part = flat(f4_parts[n][0])
                    if n == 0:
                        dve.wait_ge(f4_in, 16 * len(f4_parts))
                    f4_steps.step(fq.magnitude_of_bits(dve, part))
                    f4_steps.step(fq.steps(dve, f4_steps, part, part))


def delta_net(core, x0):
    nc, ins, h = core.nc, core.ins, core.h
    pre = "L2_attn_"
    H, dh, S2, BL = 16, 16, 2, B // 2
    W = 3 * D + 2 * H
    Q, K, V = range(3)
    ctx, sb, ps, sem = stage(nc, "dn")
    with ctx:
        pairs_kq = sb("kq", [P, S2, 2, dh, P])
        pairs_bv = sb("bv", [P, S2, dh, P])
        pairs_g = sb("gates", [P, S2, 2, P])
        tokens = sb("tokens", [P, 3, B, D])
        rates = sb("rates", [P, 2, B, H])
        ctx1, sb1, ps1, sem1 = stage(nc, "dn1")
        with ctx1:
            outer = TokenNorm(core, sb1, sem1, h)
            ctx_i, sbi, _, semi = stage(nc, "dn1i")
            ctx1.enter_context(ctx_i)
            inner = TokenNorm(core, sbi, semi, x0)
            xn, xT = sb1("xn", [P, 2, D]), sb1("xT", [P, 2, DC, P])
            w = sb1("w", [P, DC, W])
            gam, bet = sb1("gam", [P, DC]), sb1("bet", [P, DC])
            psX, psY = ps1("x", [P, 2, 512]), ps1("y", [P, 4, 512])
            loaded, x0_done, xn_ready = sem1("loaded"), sem1("x0_done"), sem1("xn_ready")
            x_full, x_read, y_full, y_read = sem1("x_full"), sem1("x_read"), sem1("y_full"), sem1("y_read")
            block = ctx1.enter_context(nc.Block())

            @block.sync
            def _(sp):
                at = 0
                for n in ("Wq", "Wk", "Wv", "Wb", "Wg"):
                    src = ins[pre + n]
                    sp.dma_start(w[:, :, at:at + src.shape[1]], src.rearrange("(c p) n -> p c n", p=P)).then_inc(loaded, 16)
                    at += src.shape[1]
                sp.dma_start(gam[:, :], ins["f2_ln1_g"]).then_inc(loaded, 16)
                sp.dma_start(bet[:, :], ins["f2_ln1_b"]).then_inc(loaded, 16)

            @block.gpsimd
            def _(pool):
                for norm in (outer, inner):
                    norm.rsqrt(pool, 0, 4)
                    norm.rsqrt(pool, 4)

            @block.vector
            def _(dve):
                outer.stats(dve, 0, 4)
                outer.stats(dve, 4)
                dve.wait_ge(outer.rstd_done, 1)
                for t in range(B):
                    if t == 4:
                        dve.wait_ge(outer.rstd_done, 2)
                    outer.normalise(dve, x0[:, t, :], t).then_inc(x0_done, 1)
                dve.wait_ge(x0_done, B)
                inner.stats(dve, 0, 4)
                inner.stats(dve, 4)
                dve.wait_ge(inner.rstd_done, 1)
                for t in range(B + 1):
                    if t == 4:
                        dve.wait_ge(inner.rstd_done, 2)
                    if t < B:
                        if t >= 2:
                            dve.wait_ge(x_full, t - 1)
                        inner.normalise(dve, xn[:, t % 2, :], t).then_inc(xn_ready, 1)
                    if t > 0:
                        u = t - 1
                        bank = 2 * (u % 2)
                        dve.wait_ge(y_full, 2 * u + 1)
                        dve.tensor_scalar(tokens[:, Q, u, :], psY[:, bank, 0:D], float(dh) ** -0.5, None, ALU.mult)
                        dve.tensor_copy(tokens[:, K, u, :], psY[:, bank, D:2 * D]).then_inc(y_read, 1)
                        dve.wait_ge(y_full, 2 * u + 2)
                        dve.tensor_copy(tokens[:, V, u, :], psY[:, bank + 1, 0:D])
                        dve.tensor_copy(rates[:, :, u, :], psY[:, bank + 1, D:D + 2 * H].rearrange("p (j h) -> p j h", j=2)).then_inc(y_read, 1)

            @block.scalar
            def _(act):
                act.wait_ge(loaded, 16 * 7)
                for t in range(B):
                    act.wait_ge(x_full, t + 1)
                    if t >= 2:
                        act.wait_ge(y_full, 2 * (t - 1))
                    for c in range(DC):
                        a = act.activation(xT[:, t % 2, c, :], psX[:, t % 2, c * P:(c + 1) * P], ACT.Identity,
                                           bias=bet[:, c:c + 1], scale=gam[:, c:c + 1])
                    a.then_inc(x_read, 1)

            @block.tensor
            def _(pe):
                def rows(t):
                    pe.wait_ge(xn_ready, t + 1)
                    if t >= 2:
                        pe.wait_ge(x_read, t - 1)
                    for c in range(DC):
                        mm = pe.transpose(psX[:, t % 2, c * P:(c + 1) * P], xn[:, t % 2, c * P:(c + 1) * P], core.ident[:, :])
                    mm.then_inc(x_full, 1)

                rows(0)
                pe.wait_ge(loaded, 16 * 7)
                for t in range(B):
                    if t + 1 < B:
                        rows(t + 1)
                    pe.wait_ge(x_read, t + 1)
                    for bank, a, b in ((0, 0, 2 * D), (1, 2 * D, W)):
                        if t >= 2:
                            pe.wait_ge(y_read, 2 * (t - 2) + bank + 1)
                        for c in range(DC):
                            mm = pe.matmul(psY[:, 2 * (t % 2) + bank, 0:b - a], xT[:, t % 2, c, :], w[:, c, a:b],
                                           start=c == 0, stop=c == DC - 1)
                        mm.then_inc(y_full, 1)

        ctx2, sb2, ps2, sem2 = stage(nc, "dn2")
        with ctx2:
            sq = sb2("sq", [P, B, D])
            nrm = sb2("nrm", [P, B * H])
            psT = ps2("t", [P, 4, 512])
            chained, squared, rooted, gated, vals_ready, keys_ready, t_full, t_read = (
                sem2(n) for n in ("chained", "squared", "rooted", "gated", "vals_ready", "keys_ready", "t_full", "t_read"))
            block = ctx2.enter_context(nc.Block())
            keys = tokens[:, K]
            vals = tokens[:, V]
            heads = lambda a: a.rearrange("p b (h d) -> p (b h) d", d=dh)
            beta, gate = (rates[:, j].rearrange("p b h -> p (b h)") for j in range(2))
            views = []
            for off, side, dst in ((Q, 1, pairs_kq), (V, None, pairs_bv), (K, 0, pairs_kq)):
                for s in range(S2):
                    to = dst[:, s] if side is None else dst[:, s, side]
                    for d0 in range(0, dh, 4):
                        srcs = [heads(tokens[:, off])[:, s * P:(s + 1) * P, d0 + i] for i in range(4)]
                        views.append((srcs, to[:, d0:d0 + 4, :]))
            first_v, first_k = len(views) // 3, 2 * len(views) // 3
            for s in range(S2):
                views.append(([r[:, s * P:(s + 1) * P] for r in (beta, gate)], pairs_g[:, s]))

            @block.vector
            def _(dve):
                chain = Chain(dve, chained)
                dve.tensor_tensor(sq[:, :, :], keys, keys, ALU.mult).then_inc(squared, 1)
                dve.wait_ge(squared, 1)
                dve.tensor_reduce(nrm[:, :], heads(sq[:, :, :]), AX.X, ALU.add).then_inc(squared, 1)
                dve.wait_ge(rooted, 1)
                chain.step(dve.tensor_scalar(nrm[:, :], nrm[:, :], 1e-6, None, ALU.add))
                chain.step(dve.reciprocal(nrm[:, :], nrm[:, :]))
                wide = [P, B * H, dh]
                dve.tensor_tensor(heads(keys), heads(keys), nrm[:, :].unsqueeze(2).to_broadcast(wide), ALU.mult).then_inc(keys_ready, 1)

            @block.gpsimd
            def _(pool):
                pool.wait_ge(gated, 1)
                pool.tensor_tensor(heads(vals), heads(vals), beta.unsqueeze(2).to_broadcast([P, B * H, dh]), ALU.mult).then_inc(vals_ready, 1)
                pool.wait_ge(vals_ready, 1)
                pool.tensor_tensor(beta, beta, gate, ALU.mult).then_inc(vals_ready, 1)

            @block.scalar
            def _(act):
                act.activation(rates[:, :, :, :], rates[:, :, :, :], ACT.Sigmoid).then_inc(gated, 1)
                for n, (srcs, dst) in enumerate(views):
                    if n == first_v:
                        act.wait_ge(squared, 2)
                        act.activation(nrm[:, :], nrm[:, :], ACT.Sqrt).then_inc(rooted, 1)
                    act.wait_ge(t_full, n + 1)
                    act.copy(dst, psT[:, n % 4, 0:len(srcs) * P].rearrange("p (a t) -> p a t", t=P)).then_inc(t_read, 1)

            @block.tensor
            def _(pe):
                for n, (srcs, dst) in enumerate(views):
                    if n == first_v:
                        pe.wait_ge(vals_ready, 2)
                    if n == first_k:
                        pe.wait_ge(keys_ready, 1)
                    if n >= 4:
                        pe.wait_ge(t_read, n - 3)
                    for i, src in enumerate(srcs):
                        mm = pe.transpose(psT[:, n % 4, i * P:(i + 1) * P], src, core.ident[:, :])
                    mm.then_inc(t_full, 1)

        ctx3, sb3, ps3, sem3 = stage(nc, "dn3")
        with ctx3:
            TURN = 8
            state = sb3("state", [P, 2, S2, dh, dh])
            prod = sb3("prod", [P, S2, dh, dh])
            a_k = sb3("a_k", [P, S2, dh])
            minus_u = sb3("minus_u", [P, S2, dh])
            outp = sb3("outp", [P, S2, dh, dh])
            prod_q = sb3("prod_q", [P, S2, dh, dh])
            out_chained, state_ready, state_read, begun = (sem3(n) for n in ("out_chained", "state_ready", "state_read", "begun"))
            links = [sem3("links0"), sem3("links1")]
            kq = pairs_kq
            wide = [P, S2, dh, dh]
            block = ctx3.enter_context(nc.Block())

            @block.vector
            def _(dve):
                dve.sem_inc(state_read, 2)
                dve.memset(state[:, :, :, :, :], 0.0).then_inc(begun, 1)
                dve.wait_ge(begun, 1)
                dve.sem_inc(state_ready, S2)

                def step(t, u):
                    old, new = state[:, u % 2], state[:, (u + 1) % 2]
                    flat3 = [P, dh, dh]
                    k = [kq[:, s, 0, :, t].unsqueeze(1).to_broadcast(flat3) for s in range(S2)]
                    for s in range(S2):
                        dve.wait_ge(state_ready, S2 * t + (s + 1))
                        dve.tensor_tensor(prod[:, s], old[:, s], k[s], ALU.mult).then_inc(links[s], 1)
                    for s in range(S2):
                        dve.wait_ge(links[s], 4 * t + 1)
                        dve.tensor_reduce(a_k[:, s], prod[:, s], AX.X, ALU.add).then_inc(links[s], 1)
                    for s in range(S2):
                        dve.wait_ge(links[s], 4 * t + 2)
                        dve.scalar_tensor_tensor(out=minus_u[:, s], in0=a_k[:, s], scalar=pairs_g[:, s, 0, t].unsqueeze(1),
                                                 in1=pairs_bv[:, s, :, t], op0=ALU.mult, op1=ALU.subtract).then_inc(links[s], 1)
                    for s in range(S2):
                        dve.wait_ge(links[s], 4 * t + 3)
                        dve.tensor_tensor(outp[:, s], minus_u[:, s].unsqueeze(2).to_broadcast(flat3), k[s], ALU.mult).then_inc(links[s], 1)
                    dve.wait_ge(state_read, t + 1)
                    for s in range(S2):
                        dve.wait_ge(links[s], 4 * t + 4)
                        dve.scalar_tensor_tensor(out=new[:, s], in0=old[:, s], scalar=pairs_g[:, s, 1, t].unsqueeze(1),
                                                 in1=outp[:, s], op0=ALU.mult, op1=ALU.subtract).then_inc(state_ready, 1)

                with dve.Fori(0, P // TURN) as i:
                    for u in range(TURN):
                        step(i * TURN + u, u)

            @block.gpsimd
            def _(pool):
                def own(count):
                    pool.wait_ge(out_chained, count)
                    pool.wait_ge(begun, 1)

                per = 5
                with pool.Fori(0, P // TURN) as i:
                    for u in range(TURN):
                        t = i * TURN + u
                        pool.wait_ge(state_ready, S2 * t + 2 * S2)
                        pool.wait_ge(begun, 1)
                        pool.tensor_tensor(prod_q[:, :, :, :], state[:, (u + 1) % 2], kq[:, :, 1, :, t].unsqueeze(2).to_broadcast(wide),
                                           ALU.mult).then_inc(out_chained, 1)
                        own(per * t + 1)
                        pool.sem_inc(state_read, 1)
                        for m, n in enumerate((8, 4, 2, 1)):
                            dst = prod_q[:, :, :, 0:n] if n > 1 else pairs_bv[:, :, :, t].unsqueeze(3)
                            pool.tensor_tensor(dst, prod_q[:, :, :, 0:n], prod_q[:, :, :, n:2 * n], ALU.add).then_inc(out_chained, 1)
                            own(per * t + (m + 2))

        ctx4, sb4, ps4, sem4 = stage(nc, "dn4")
        with ctx4:
            att = sb4("att", [P, B, D])
            aT = sb4("aT", [P, 2, DC, P])
            wo, bo = sb4("wo", [P, DC, D]), sb4("bo", [1, D])
            psT, psA, psO = ps4("t", [P, 4, 512]), ps4("a", [P, 2, 512]), ps4("o", [P, 2, 512])
            loaded, t_full, t_read0, t_read1 = sem4("loaded"), sem4("t_full"), sem4("t_read0"), sem4("t_read1")
            a_full, a_read, o_full, o_added, x_added = sem4("a_full"), sem4("a_read"), sem4("o_full"), sem4("o_added"), sem4("x_added")
            t_read = [t_read0, t_read1]
            block = ctx4.enter_context(nc.Block())
            views = [(s, v0) for s in range(S2) for v0 in range(0, dh, 4)]

            def spread(n):
                s, v0 = views[n]
                src = psT[:, n % 4, :].rearrange("p (v b h) -> p b h v", v=4, b=BL)
                dst = heads4(att[:, s * BL:(s + 1) * BL, :])[:, :, :, v0:v0 + 4]
                return dst, src

            heads4 = lambda a: a.rearrange("p b (h d) -> p b h d", d=dh)

            @block.sync
            def _(sp):
                sp.dma_start(wo[:, :, :], ins[pre + "Wo"].rearrange("(c p) n -> p c n", p=P)).then_inc(loaded, 16)
                sp.dma_start(bo[:, :], ins[pre + "bo"].unsqueeze(0)).then_inc(loaded, 16)

            def spread_all(eng, par):
                for n in range(par, len(views), 2):
                    eng.wait_ge(t_full, n + 1)
                    dst, src = spread(n)
                    for v in range(4):
                        if par:
                            i_ = eng.tensor_copy(dst[:, :, :, v], src[:, :, :, v])
                        else:
                            i_ = eng.copy(dst[:, :, :, v], src[:, :, :, v])
                    i_.then_inc(t_read[par], 1)

            @block.scalar
            def _(act):
                spread_all(act, 0)
                for t in range(B):
                    act.wait_ge(a_full, t + 1)
                    if t >= 2:
                        act.wait_ge(o_full, t - 1)
                    act.copy(aT[:, t % 2, :, :], psA[:, t % 2, 0:D].rearrange("p (c t) -> p c t", c=DC)).then_inc(a_read, 1)

            @block.vector
            def _(dve):
                spread_all(dve, 1)
                for t in range(B):
                    dve.wait_ge(o_full, t + 1)
                    dve.tensor_tensor(x0[:, t, :], x0[:, t, :], psO[:, t % 2, 0:D], ALU.add).then_inc(o_added, 1)

            @block.gpsimd
            def _(pool):
                for t in range(B):
                    pool.wait_ge(o_added, t + 1)
                    pool.tensor_tensor(h[:, t, :], h[:, t, :], x0[:, t, :], ALU.add).then_inc(x_added, 1)

            @block.tensor
            def _(pe):
                for n, (s, v0) in enumerate(views):
                    if n >= 4:
                        pe.wait_ge(t_read[n % 2], (n - 4) // 2 + 1)
                    for i in range(4):
                        mm = pe.transpose(psT[:, n % 4, i * P:(i + 1) * P], pairs_bv[:, s, v0 + i, :], core.ident[:, :])
                    mm.then_inc(t_full, 1)

                def rows(t):
                    if t >= 2:
                        pe.wait_ge(a_read, t - 1)
                    for c in range(DC):
                        mm = pe.transpose(psA[:, t % 2, c * P:(c + 1) * P], att[:, t, c * P:(c + 1) * P], core.ident[:, :])
                    mm.then_inc(a_full, 1)

                pe.wait_ge(t_read[0], len(views) // 2)
                pe.wait_ge(t_read[1], len(views) // 2)
                pe.wait_ge(loaded, 32)
                rows(0)
                for t in range(B):
                    if t + 1 < B:
                        rows(t + 1)
                    pe.wait_ge(a_read, t + 1)
                    if t >= 2:
                        pe.wait_ge(o_added, t - 1)
                    pe.matmul(psO[:, t % 2, 0:D], core.ones[0:1, :], bo[:, :], start=True, stop=False)
                    for c in range(DC):
                        mm = pe.matmul(psO[:, t % 2, 0:D], aT[:, t % 2, c, :], wo[:, c, :], start=False, stop=c == DC - 1)
                    mm.then_inc(o_full, 1)


def fp4_ffn(core, weights):
    nc, ins, h = core.nc, core.ins, core.h
    I, IC, IP = weights.I, weights.IC, weights.IP
    HALF = I // 2
    ctx, sb, ps, sem = stage(nc, "f4")
    with ctx:
        wT = sb("wT", [P, DC, 2 * IP])
        dT = sb("dT", [P, IC, D])
        ctx1, sb1, ps1, sem1 = stage(nc, "f4w")
        with ctx1:
            raw, raw_d = weights.raw, weights.raw_d
            psT = ps1("t", [P, 8, 512])
            t_full = sem1("t_full")
            t_read = [sem1("t_read0"), sem1("t_read1")]
            views = []
            for side in range(2):
                for c in range(DC):
                    for a in range(0, IC, 3):
                        views.append(([raw[:, side * IC + a + i, c * P:(c + 1) * P] for i in range(3)],
                                      wT[:, c, side * IP + a * P:side * IP + (a + 3) * P]))
            for j in range(0, IC, 2):
                views.append(([raw_d[:, c, (j + i) * P:(j + i + 1) * P] for i in range(2) for c in range(DC)],
                              dT[:, j:j + 2, :].rearrange("p a b -> p (a b)")))
            block = ctx1.enter_context(nc.Block())

            @block.scalar
            def _(act):
                for n in range(0, len(views), 2):
                    srcs, dst = views[n]
                    act.wait_ge(t_full, n + 1)
                    act.copy(dst, psT[:, n % 8, 0:len(srcs) * P]).then_inc(t_read[0], 1)

            @block.vector
            def _(dve):
                for n in range(1, len(views), 2):
                    srcs, dst = views[n]
                    dve.wait_ge(t_full, n + 1)
                    dve.tensor_copy(dst, psT[:, n % 8, 0:len(srcs) * P]).then_inc(t_read[1], 1)

            @block.tensor
            def _(pe):
                for n, (srcs, _) in enumerate(views):
                    if n >= 8:
                        pe.wait_ge(t_read[n % 2], (n - 8) // 2 + 1)
                    for i, src in enumerate(srcs):
                        mm = pe.transpose(psT[:, n % 8, i * P:(i + 1) * P], src, core.ident[:, :])
                    mm.then_inc(t_full, 1)

        ctx2, sb2, ps2, sem2 = stage(nc, "f4t")
        with ctx2:
            norm = TokenNorm(core, sb2, sem2, h)
            xn, xq, xT = sb2("xn", [P, D]), sb2("xq", [P, D]), sb2("xT", [P, DC, P])
            gate, hid, hq, hT = sb2("gate", [P, I]), sb2("hid", [P, I]), sb2("hq", [P, IP]), sb2("hT", [P, IC, P])
            fx, fh = Fp4(sb2, "x", D), Fp4(sb2, "h", I)
            psX, psU, psH, psO = ps2("x", [P, 512]), ps2("u", [P, 4, 512]), ps2("h", [P, 2, 512]), ps2("o", [P, 512])
            names = ("xn_ready", "x_mag", "xq_ready", "x_full", "x_read", "gate_full", "up_full", "gate_read", "hid_ready",
                     "h_mag", "hq_ready", "h_full", "h_read", "o_full", "o_added", "padded", "chained")
            (xn_ready, x_mag, xq_ready, x_full, x_read, gate_full, up_full, gate_read, hid_ready,
             h_mag, hq_ready, h_full, h_read, o_full, o_added, padded, chained) = (sem2(n) for n in names)
            banks = lambda a: a.rearrange("p (j n) -> p j n", j=2)
            block = ctx2.enter_context(nc.Block())

            @block.gpsimd
            def _(pool):
                pool.memset(hq[:, I:IP], 0.0).then_inc(padded, 1)
                norm.rsqrt(pool, 0, 4)
                norm.rsqrt(pool, 4)

            @block.vector
            def _(dve):
                chain = Chain(dve, chained)
                norm.stats(dve, 0, 4)
                norm.stats(dve, 4)
                dve.wait_ge(norm.rstd_done, 1)
                STEPS = Fp4.STEPS

                def normal(t):
                    norm.normalise(dve, xn[:, :], t).then_inc(xn_ready, 1)

                def quant_x(t, links):
                    dve.wait_ge(x_mag, t + 1)
                    chain.begin(links)
                    fx.steps(dve, chain, xn[:, :], xq[:, :]).then_inc(xq_ready, 1)

                def quant_both(t, links):
                    for n in range(STEPS):
                        if n == 0:
                            dve.wait_ge(x_mag, t + 3)
                        else:
                            dve.wait_ge(chained, links + (2 * n - 1))
                        ix = fx.step(dve, n, xn[:, :], xq[:, :])
                        ix.then_inc(chained if n < STEPS - 1 else xq_ready, 1)
                        if n == 0:
                            dve.wait_ge(h_mag, t + 1)
                        else:
                            dve.wait_ge(chained, links + 2 * n)
                        ih = fh.step(dve, n, hid[:, :], hq[:, 0:I])
                        ih.then_inc(chained if n < STEPS - 1 else hq_ready, 1)

                def add(t):
                    dve.wait_ge(o_full, t + 1)
                    dve.tensor_tensor(h[:, t, :], h[:, t, :], psO[:, 0:D], ALU.add).then_inc(o_added, 1)

                first = 2 * (STEPS - 1)
                per = 2 * (STEPS - 1)

                def turn(t, ahead):
                    dve.wait_ge(gate_read, t + 1)
                    dve.wait_ge(up_full, t + 1)
                    dve.tensor_tensor(banks(hid[:, :]), banks(gate[:, :]), psU[:, 2:4, 0:HALF], ALU.mult).then_inc(hid_ready, 1)
                    if ahead >= 2:
                        quant_both(t, t * per + first)
                    else:
                        dve.wait_ge(h_mag, t + 1)
                        chain.begin(first + (B - 2) * per + (1 - ahead) * (STEPS - 1))
                        fh.steps(dve, chain, hid[:, :], hq[:, 0:I]).then_inc(hq_ready, 1)
                    if ahead >= 3:
                        normal(t + 3)
                    if not isinstance(t, int) or t > 0:
                        add(t - 1)

                normal(0)
                quant_x(0, 0)
                normal(1)
                quant_x(1, STEPS - 1)
                normal(2)
                dve.wait_ge(norm.rstd_done, 2)
                turn(0, 3)
                with dve.Fori(1, B - 3) as t:
                    turn(t, 3)
                turn(B - 3, 2)
                turn(B - 2, 1)
                turn(B - 1, 0)
                add(B - 1)

            @block.scalar
            def _(act):
                def x_magnitude(t):
                    act.wait_ge(xn_ready, t + 1)
                    fx.magnitude(act, xn[:, :]).then_inc(x_mag, 1)

                def copy_x(t):
                    act.wait_ge(x_full, t + 1)
                    act.copy(xT[:, :, :], psX[:, 0:D].rearrange("p (c t) -> p c t", c=DC)).then_inc(x_read, 1)

                def silu(t):
                    act.wait_ge(gate_full, t + 1)
                    act.activation(banks(gate[:, :]), psU[:, 0:2, 0:HALF], ACT.Silu).then_inc(gate_read, 1)

                def turn(t, ahead):
                    act.wait_ge(hid_ready, t + 1)
                    fh.magnitude(act, hid[:, :]).then_inc(h_mag, 1)
                    if ahead >= 1:
                        silu(t + 1)
                    if ahead >= 3:
                        x_magnitude(t + 3)
                    if ahead >= 2:
                        copy_x(t + 2)
                    act.wait_ge(h_full, t + 1)
                    for j in range(2):
                        a = act.copy(hT[:, 3 * j:3 * j + 3, :], psH[:, j, 0:3 * P].rearrange("p (c t) -> p c t", c=3))
                    a.then_inc(h_read, 1)

                x_magnitude(0)
                copy_x(0)
                silu(0)
                x_magnitude(1)
                copy_x(1)
                x_magnitude(2)
                with act.Fori(0, B - 3) as t:
                    turn(t, 3)
                turn(B - 3, 2)
                turn(B - 2, 1)
                turn(B - 1, 0)

            @block.tensor
            def _(pe):
                def rows(t):
                    pe.wait_ge(xq_ready, t + 1)
                    for c in range(DC):
                        mm = pe.transpose(psX[:, c * P:(c + 1) * P], xq[:, c * P:(c + 1) * P], core.ident[:, :])
                    mm.then_inc(x_full, 1)

                def up(t):
                    pe.wait_ge(x_read, t + 1)
                    if not isinstance(t, int) or t > 0:
                        pe.wait_ge(hid_ready, t)
                    for side, full in ((0, gate_full), (1, up_full)):
                        for j in range(2):
                            for c in range(DC):
                                mm = pe.matmul(psU[:, 2 * side + j, 0:HALF], xT[:, c, :],
                                               wT[:, c, side * IP + j * HALF:side * IP + (j + 1) * HALF], start=c == 0, stop=c == DC - 1)
                        mm.then_inc(full, 1)

                def back(t):
                    pe.wait_ge(hq_ready, t + 1)
                    for j in range(IC):
                        mm = pe.transpose(psH[:, j // 3, (j % 3) * P:(j % 3 + 1) * P], hq[:, j * P:(j + 1) * P], core.ident[:, :])
                    mm.then_inc(h_full, 1)
                    pe.wait_ge(h_read, t + 1)
                    if not isinstance(t, int) or t > 0:
                        pe.wait_ge(o_added, t + 1)
                    for j in range(IC):
                        mm = pe.matmul(psO[:, 0:D], hT[:, j, :], dT[:, j, :], start=j == 0, stop=j == IC - 1)
                    mm.then_inc(o_full, 1)

                pe.wait_ge(padded, 1)
                pe.sem_inc(o_added, 1)
                rows(0)
                up(0)
                rows(1)
                with pe.Fori(0, B - 2) as t:
                    up(t + 1)
                    rows(t + 2)
                    back(t)
                up(B - 1)
                back(B - 2)
                back(B - 1)


def layer2(core):
    with ExitStack() as ctx:
        weights = Fp4Weights(core, ctx)
        with core.nc.sbuf_tensor("x0", [P, B, D], F32) as x0:
            delta_net(core, x0)
            mlp(core, x0, weights)
        fp4_ffn(core, weights)


def lm_tower(nc, ins, out):
    core = Core(nc, ins, out)
    ctx = ExitStack()
    with ctx:
        core.h = ctx.enter_context(nc.sbuf_tensor("h", [P, B, D], F32))
        core.ident = ctx.enter_context(nc.sbuf_tensor("ident", [P, P], F32))
        core.ident_bf = ctx.enter_context(nc.sbuf_tensor("ident_bf", [P, P], BF16))
        core.causal = ctx.enter_context(nc.sbuf_tensor("causal", [P, 4 * P], BF16))
        core.ones = ctx.enter_context(nc.sbuf_tensor("ones", [P, P], F32))
        core.minus_half = ctx.enter_context(nc.sbuf_tensor("minus_half", [P, 2 * B], F32))
        core.ones_bf = ctx.enter_context(nc.sbuf_tensor("ones_bf", [P, P], BF16))
        core.zeros = ctx.enter_context(nc.sbuf_tensor("zeros", [P, D], F32))
        core.rows_cleared = ctx.enter_context(nc.semaphore("rows_cleared"))
        slots = P * moe_tiles(4, 16)
        core.slot_rows = nc.dram_tensor("slot_rows", (slots, D), F32)
        core.slot_outputs = nc.dram_tensor("slot_outputs", (slots, D), F32)
        core.bias_parts = nc.dram_tensor("bias_parts", (3, 8 * (1024 + D)), BF16)
        embed(core)
        attention(core, "headnorm")
        moe(core, "swiglu")
        attention(core, "nd")
        moe(core, "gelu")
        layer2(core)
        attention(core, "rel")
        moe(core, "silu")
        done = ctx.enter_context(nc.semaphore("out_done"))
        block = ctx.enter_context(nc.Block())

        @block.sync
        def _(sp):
            sp.dma_start(out.rearrange("b t d -> t b d"), core.h[:, :, :]).then_inc(done, 16)
            sp.wait_ge(done, 16)


def layouts(inputs):
    a = {k: np.ascontiguousarray(v) for k, v in inputs.items()}
    a["token_ids"] = np.ascontiguousarray(a.pop("x").T)
    a["ident"] = np.eye(P, dtype=np.float32)
    tri = np.where(np.arange(P)[:, None] >= np.arange(P)[None, :], 0.0, -1e30).astype(np.float32)
    a["causal"] = np.tile(tri, (1, 4))
    a["masked"] = np.full((16, P), -1e9, np.float32)

    def strips(w, width, strip):
        w = w.reshape(w.shape[0], -1, width)
        o = np.zeros((*w.shape[:2], strip), w.dtype)
        o[:, :, :width] = w
        return o.reshape(w.shape[0], -1)

    def by_partition(v, n):
        return np.ascontiguousarray(v.reshape(n, P).T)

    for s in ("q", "k"):
        a[f"L3_attn_W{s}_strips"] = strips(a.pop(f"L3_attn_W{s}"), 16, 32)
        a[f"L3_attn_b{s}_strips"] = by_partition(strips(a.pop(f"L3_attn_b{s}")[None], 16, 32), 4)
    a["L1_attn_Wq_strips"] = a.pop("L1_attn_Wq")
    a["L1_attn_Wk_strips"] = a.pop("L1_attn_Wk")
    a["L1_attn_bq_strips"] = by_partition(a.pop("L1_attn_bq"), 8)
    order = [8 * (s // 2) + 2 * c + s % 2 for c in range(4) for s in range(4)]
    for n in ("Wr", "br"):
        w = a.pop(f"L1_attn_{n}").reshape(-1, 16, 10)[:, order].reshape(-1, 160)
        a[f"L1_attn_{n}_strips"] = strips(w, 10, 32)
    a["L1_attn_br_strips"] = by_partition(a["L1_attn_br_strips"], 4)
    d = np.zeros((P, P), np.float32)
    rel = np.zeros((P, 2 * P), np.float32)
    b_nd, emb = a.pop("L1_attn_b_nd"), a.pop("L3_attn_rel_emb")
    mid = emb.shape[0] // 2
    for s in range(4):
        d[32 * s:32 * s + 10] = b_nd[:, 0:P][:, ::-1]
        rel[32 * s:32 * s + 16, 0:2 * P - 1] = emb[mid - P + 1:mid + P][::-1].T
    a["L1_attn_dist"], a["L3_attn_dist"] = d, rel

    def chunked_bias(v, n):
        return np.ascontiguousarray(v.reshape(v.shape[0], n, P).transpose(0, 2, 1))

    a["f0_w1"], a["f0_w2"] = a.pop("L0_ffn_gate_up_proj"), a.pop("L0_ffn_down_proj")
    a["f0_biases"] = np.concatenate([a.pop("L0_ffn_gate_up_bias"), a.pop("L0_ffn_down_bias")], axis=1).reshape(-1)
    a["f0_wr"], a["f0_rb"] = np.ascontiguousarray(a.pop("L0_ffn_router_weight").T), a.pop("L0_ffn_router_bias")
    a["f1_w1"], a["f1_w2"] = a.pop("L1_ffn_W1"), a.pop("L1_ffn_W2")
    a["f1_biases"] = np.concatenate([a.pop("L1_ffn_b1"), a.pop("L1_ffn_b2")], axis=1).reshape(-1)
    a["f1_wr"], a["f1_rb"] = a.pop("L1_ffn_Wr"), a.pop("L1_ffn_br")
    a["f2_w1"] = np.ascontiguousarray(a.pop("L2_attn_w1").reshape(D, 2, 512).transpose(1, 0, 2))
    a["f2_w2"], a["f2_b1"] = a.pop("L2_attn_w2").reshape(2, 512, D), chunked_bias(a.pop("L2_attn_b1").reshape(2, 512), 4)
    a["f2_ln1_g"], a["f2_ln1_b"] = by_partition(a.pop("L2_attn_ln1_g"), 2), by_partition(a.pop("L2_attn_ln1_b"), 2)
    pad = 6 * P - 704
    for n in ("gate", "up"):
        a[f"f4_{n}"] = np.pad(a.pop(f"L2_ffn_w_{n}"), ((0, pad), (0, 0)))
    a["f4_down"] = np.pad(a.pop("L2_ffn_w_down"), ((0, 0), (0, pad)))
    a["f2_b2"] = a.pop("L2_attn_b2")[None]
    a["f2_g"], a["f2_b"] = by_partition(a.pop("L2_attn_ln2_g"), 2), by_partition(a.pop("L2_attn_ln2_b"), 2)
    I3 = 352
    side = {}
    for n in ("gate", "up"):
        side[n] = np.concatenate([a.pop(f"L3_ffn_{n}_proj"), a.pop(f"L3_ffn_shared_{n}_w").reshape(2, I3, D)])
    a["f3_w1"] = np.concatenate([side["gate"].transpose(0, 2, 1), side["up"].transpose(0, 2, 1)], axis=2)
    down = np.concatenate([a.pop("L3_ffn_down_proj").transpose(0, 2, 1), a.pop("L3_ffn_shared_down_w").T.reshape(2, I3, D)])
    a["f3_w2"] = np.concatenate([down, np.zeros((18, 3 * P - I3, D), down.dtype)], axis=1)
    a["f3_wr"], a["f3_rb"] = np.ascontiguousarray(a.pop("L3_ffn_gate_w").T), a.pop("L3_ffn_gate_bias")
    a["before"] = (np.arange(P)[:, None] < np.arange(P)[None, :]).astype(np.float32)
    for n in (8, 16):
        a[f"earlier{n}"] = (np.arange(n)[:, None] > np.arange(n)[None, :]).astype(np.float32).reshape(-1)
    a["tile_starts"] = np.array([-1.0] + [P * j for j in range(1, B)], np.float32)
    a["tile_ids"] = np.arange(moe_tiles(4, 16), dtype=np.float32)[None]
    for n in (4, 8, 16):
        a[f"rank{n}"] = np.arange(n, 0, -1, dtype=np.float32)
    return a


def kernel(**inputs):
    from concourse import bacc
    from concourse.bass_utils import run_bass_kernel_spmd

    nc = bacc.Bacc("TRN2", target_bir_lowering=False, num_devices=1)
    arrays, ins = {}, {}
    for name, v in layouts(inputs).items():
        arrays["in_" + name] = v
        ins[name] = nc.dram_tensor("in_" + name, v.shape, mybir.dt.from_np(v.dtype), kind="ExternalInput").ap()
    out = nc.dram_tensor("out_0_dram", (B, P, D), F32, kind="ExternalOutput").ap()
    lm_tower(nc, ins, out)
    r = run_bass_kernel_spmd(nc, [arrays], core_ids=[0])
    return r.results[0]["out_0_dram"]
```
